# Optimizing a Trainium2 kernel written in Bass

```python
import numpy as np
import jax
import jax.numpy as jnp

def _softmax(x, axis=-1):
    return jax.nn.softmax(x, axis=axis)

def _gelu(x):
    return jax.nn.gelu(x, approximate=True)

def _silu(x):
    return jax.nn.silu(x)

def _sigmoid(x):
    return jax.nn.sigmoid(x)

def _layernorm(x, axis=-1, eps=1e-05):
    m = jnp.mean(x, axis=axis, keepdims=True)
    v = jnp.var(x, axis=axis, keepdims=True)
    return (x - m) / jnp.sqrt(v + eps)

def _scatter_add(tgt, idx, src, axis=0):
    return tgt.at[idx].add(src)

def _segment_sum(src, seg, n):
    return jax.ops.segment_sum(src, seg, n)
kernel_name = 'mk_hybrid_d1_jaxref_r8_8fa387'

def setup_inputs(seed: int=0):
    np.random.seed(seed)
    _w = jnp.asarray

    def _L0_attn_a_setup():
        import jax, jax.numpy as jnp
        import numpy as np
        B, T, D, C = (8, 256, 128, 128)
        key = jax.random.key(seed)
        ks = jax.random.split(key, 16)
        s = 1.0 / np.sqrt(D)
        so = 1.0 / np.sqrt(C)
        return {'x': jax.random.normal(ks[0], (B, T, D), jnp.float32), 'Wq': jax.random.normal(ks[1], (D, C), jnp.float32) * s, 'bq': jax.random.normal(ks[2], (C,), jnp.float32) * 0.01, 'Wk': jax.random.normal(ks[3], (D, C), jnp.float32) * s, 'bk': jax.random.normal(ks[4], (C,), jnp.float32) * 0.01, 'Wv': jax.random.normal(ks[5], (D, C), jnp.float32) * s, 'bv': jax.random.normal(ks[6], (C,), jnp.float32) * 0.01, 'Wa': jax.random.normal(ks[7], (D, 1), jnp.float32) * s, 'ba': jax.random.normal(ks[8], (1,), jnp.float32) * 0.01, 'Wb': jax.random.normal(ks[9], (D, 1), jnp.float32) * s, 'bb': jax.random.normal(ks[10], (1,), jnp.float32) * 0.01, 'Wg': jax.random.normal(ks[11], (D, C), jnp.float32) * s, 'bg': jax.random.normal(ks[12], (C,), jnp.float32) * 0.01, 'Wo': jax.random.normal(ks[13], (C, D), jnp.float32) * so, 'bo': jax.random.normal(ks[14], (D,), jnp.float32) * 0.01}
    _L0_attn_a_in = _L0_attn_a_setup()

    def _L0_attn_b_setup():
        import jax, jax.numpy as jnp
        import numpy as np
        D_MODEL = 128
        D_STATE = 128
        D_CONV = 4
        HEADDIM = 64
        EXPAND = 2
        NGROUPS = 1
        CHUNK = 32
        D_INNER = EXPAND * D_MODEL
        NHEADS = D_INNER // HEADDIM
        CONV_DIM = D_INNER + 2 * NGROUPS * D_STATE
        D_IN_PROJ = 2 * D_INNER + 2 * NGROUPS * D_STATE + NHEADS
        EPS = 1e-05

        def _causal_dwconv(x, w, b):
            xp = jnp.pad(x, ((0, 0), (D_CONV - 1, 0), (0, 0))).transpose(0, 2, 1)
            y = jax.lax.conv_general_dilated(xp, w[:, None, :], window_strides=(1,), padding='VALID', dimension_numbers=('NCH', 'OIH', 'NCH'), feature_group_count=w.shape[0])
            return y.transpose(0, 2, 1) + b

        def _ssd(x, dt, A, Bm, Cm):
            b, l, h, p = x.shape
            g, n = (Bm.shape[2], Bm.shape[3])
            nc = l // CHUNK
            xc = x.reshape(b, nc, CHUNK, h, p)
            dtc = dt.reshape(b, nc, CHUNK, h)
            Bc = jnp.repeat(Bm.reshape(b, nc, CHUNK, g, n), h // g, axis=3)
            Cc = jnp.repeat(Cm.reshape(b, nc, CHUNK, g, n), h // g, axis=3)
            dA = dtc * A
            dA_cs = jnp.cumsum(dA, axis=2)
            xt = xc * dtc[..., None]
            diff = dA_cs[:, :, :, None, :] - dA_cs[:, :, None, :, :]
            causal = jnp.tril(jnp.ones((CHUNK, CHUNK), bool))[None, None, :, :, None]
            Lmat = jnp.where(causal, jnp.exp(diff), 0.0)
            scores = jnp.einsum('bcihn,bcjhn->bcijh', Cc, Bc) * Lmat
            y_diag = jnp.einsum('bcijh,bcjhp->bcihp', scores, xt)
            decay_states = jnp.exp(dA_cs[:, :, -1:, :] - dA_cs)
            states = jnp.einsum('bcjhn,bcjh,bcjhp->bchpn', Bc, decay_states, xt)
            chunk_decay = jnp.exp(dA_cs[:, :, -1, :])

            def step(s_prev, inp):
                cd, st = inp
                return (cd[:, :, None, None] * s_prev + st, s_prev)
            init = jnp.zeros((b, h, p, n), x.dtype)
            _, prev_states = jax.lax.scan(step, init, (jnp.moveaxis(chunk_decay, 1, 0), jnp.moveaxis(states, 1, 0)))
            prev_states = jnp.moveaxis(prev_states, 0, 1)
            y_off = jnp.einsum('bcihn,bcih,bchpn->bcihp', Cc, jnp.exp(dA_cs), prev_states)
            return (y_diag + y_off).reshape(b, l, h, p)
        key = jax.random.key(seed)
        ks = jax.random.split(key, 9)
        B, L = (1, 512)
        hidden_states = jax.random.normal(ks[0], (B, L, D_MODEL), jnp.float32)
        W_in = jax.random.normal(ks[1], (D_MODEL, D_IN_PROJ), jnp.float32) * D_MODEL ** (-0.5)
        conv_w = jax.random.normal(ks[2], (CONV_DIM, D_CONV), jnp.float32) * D_CONV ** (-0.5)
        conv_b = jnp.zeros((CONV_DIM,), jnp.float32)
        dt = jnp.exp(jax.random.uniform(ks[3], (NHEADS,), jnp.float32) * (np.log(0.1) - np.log(0.001)) + np.log(0.001))
        dt_bias = dt + jnp.log(-jnp.expm1(-dt))
        A_log = jnp.log(jax.random.uniform(ks[4], (NHEADS,), jnp.float32) * 15.0 + 1.0)
        D = jax.random.normal(ks[5], (NHEADS,), jnp.float32)
        norm_w = jnp.ones((D_INNER,), jnp.float32)
        W_out = jax.random.normal(ks[6], (D_INNER, D_MODEL), jnp.float32) * D_INNER ** (-0.5)
        return {'hidden_states': hidden_states, 'W_in': W_in, 'conv_w': conv_w, 'conv_b': conv_b, 'dt_bias': dt_bias, 'A_log': A_log, 'D': D, 'norm_w': norm_w, 'W_out': W_out}
    _L0_attn_b_in = _L0_attn_b_setup()

    def _L0_ffn_setup():
        import jax, jax.numpy as jnp
        import numpy as np
        DIM = 128
        HIDDEN = 384
        SCALE = 1.0 / 127.0

        def _dequant(w_int, dtype):
            return w_int.astype(dtype) * jnp.asarray(SCALE, dtype)
        key = jax.random.key(seed)
        k_x, k_g, k_u, k_d = jax.random.split(key, 4)
        x = jax.random.normal(k_x, (4, 256, DIM), dtype=jnp.float32)
        w_gate = jax.random.randint(k_g, (HIDDEN, DIM), -127, 128, dtype=jnp.int32)
        w_up = jax.random.randint(k_u, (HIDDEN, DIM), -127, 128, dtype=jnp.int32)
        w_down = jax.random.randint(k_d, (DIM, HIDDEN), -127, 128, dtype=jnp.int32)
        return {'x': x, 'w_gate': w_gate, 'w_up': w_up, 'w_down': w_down}
    _L0_ffn_in = _L0_ffn_setup()
    _d = {'L0_attn_a_x': _L0_attn_a_in['x'], 'L0_attn_a_Wq': _L0_attn_a_in['Wq'], 'L0_attn_a_bq': _L0_attn_a_in['bq'], 'L0_attn_a_Wk': _L0_attn_a_in['Wk'], 'L0_attn_a_bk': _L0_attn_a_in['bk'], 'L0_attn_a_Wv': _L0_attn_a_in['Wv'], 'L0_attn_a_bv': _L0_attn_a_in['bv'], 'L0_attn_a_Wa': _L0_attn_a_in['Wa'], 'L0_attn_a_ba': _L0_attn_a_in['ba'], 'L0_attn_a_Wb': _L0_attn_a_in['Wb'], 'L0_attn_a_bb': _L0_attn_a_in['bb'], 'L0_attn_a_Wg': _L0_attn_a_in['Wg'], 'L0_attn_a_bg': _L0_attn_a_in['bg'], 'L0_attn_a_Wo': _L0_attn_a_in['Wo'], 'L0_attn_a_bo': _L0_attn_a_in['bo'], 'L0_attn_b_W_in': _L0_attn_b_in['W_in'], 'L0_attn_b_conv_w': _L0_attn_b_in['conv_w'], 'L0_attn_b_conv_b': _L0_attn_b_in['conv_b'], 'L0_attn_b_dt_bias': _L0_attn_b_in['dt_bias'], 'L0_attn_b_A_log': _L0_attn_b_in['A_log'], 'L0_attn_b_D': _L0_attn_b_in['D'], 'L0_attn_b_norm_w': _L0_attn_b_in['norm_w'], 'L0_attn_b_W_out': _L0_attn_b_in['W_out'], 'L0_ffn_w_gate': _L0_ffn_in['w_gate'], 'L0_ffn_w_up': _L0_ffn_in['w_up'], 'L0_ffn_w_down': _L0_ffn_in['w_down']}
    _x0 = _d['L0_attn_a_x']
    _d['L0_attn_a_x'] = jax.random.normal(jax.random.fold_in(jax.random.key(seed), 1), (32, 256, 128), dtype=_x0.dtype)
    del _x0
    return _d

def reference(L0_attn_a_x, L0_attn_a_Wq, L0_attn_a_bq, L0_attn_a_Wk, L0_attn_a_bk, L0_attn_a_Wv, L0_attn_a_bv, L0_attn_a_Wa, L0_attn_a_ba, L0_attn_a_Wb, L0_attn_a_bb, L0_attn_a_Wg, L0_attn_a_bg, L0_attn_a_Wo, L0_attn_a_bo, L0_attn_b_W_in, L0_attn_b_conv_w, L0_attn_b_conv_b, L0_attn_b_dt_bias, L0_attn_b_A_log, L0_attn_b_D, L0_attn_b_norm_w, L0_attn_b_W_out, L0_ffn_w_gate, L0_ffn_w_up, L0_ffn_w_down):

    def _L0_attn_a_ref(x, Wq, bq, Wk, bk, Wv, bv, Wa, ba, Wb, bb, Wg, bg, Wo, bo):
        import jax, jax.numpy as jnp
        import numpy as np
        B, T, D, C = (8, 256, 128, 128)
        Bn = x.shape[0]
        Cn = Wq.shape[1]
        q = x @ Wq + bq
        k = x @ Wk + bk
        v = x @ Wv + bv
        k = k / jnp.maximum(jnp.linalg.norm(k, axis=-1, keepdims=True), 1e-12)
        alpha = jax.nn.sigmoid(x @ Wa + ba)
        beta = jax.nn.sigmoid(x @ Wb + bb)
        gate = jax.nn.sigmoid(x @ Wg + bg)
        I = jnp.eye(Cn, dtype=x.dtype)

        def step(S, ins):
            q_t, k_t, v_t, a_t, b_t, g_t = ins
            kkT = k_t[:, :, None] * k_t[:, None, :]
            trans = a_t[:, :, None] * (I - b_t[:, :, None] * kkT)
            vkT = v_t[:, :, None] * k_t[:, None, :]
            S = jnp.einsum('bij,bjk->bik', S, trans) + b_t[:, :, None] * vkT
            o = jnp.einsum('bc,bcd->bd', q_t, S) * g_t
            return (S, o)
        tfirst = lambda a: jnp.swapaxes(a, 0, 1)
        S0 = jnp.zeros((Bn, Cn, Cn), x.dtype)
        _, o = jax.lax.scan(step, S0, (tfirst(q), tfirst(k), tfirst(v), tfirst(alpha), tfirst(beta), tfirst(gate)))
        y = jnp.swapaxes(o, 0, 1) @ Wo + bo
        return y

    def _L0_attn_b_ref(hidden_states, W_in, conv_w, conv_b, dt_bias, A_log, D, norm_w, W_out):
        import jax, jax.numpy as jnp
        import numpy as np
        D_MODEL = 128
        D_STATE = 128
        D_CONV = 4
        HEADDIM = 64
        EXPAND = 2
        NGROUPS = 1
        CHUNK = 32
        D_INNER = EXPAND * D_MODEL
        NHEADS = D_INNER // HEADDIM
        CONV_DIM = D_INNER + 2 * NGROUPS * D_STATE
        D_IN_PROJ = 2 * D_INNER + 2 * NGROUPS * D_STATE + NHEADS
        EPS = 1e-05

        def _causal_dwconv(x, w, b):
            xp = jnp.pad(x, ((0, 0), (D_CONV - 1, 0), (0, 0))).transpose(0, 2, 1)
            y = jax.lax.conv_general_dilated(xp, w[:, None, :], window_strides=(1,), padding='VALID', dimension_numbers=('NCH', 'OIH', 'NCH'), feature_group_count=w.shape[0])
            return y.transpose(0, 2, 1) + b

        def _ssd(x, dt, A, Bm, Cm):
            b, l, h, p = x.shape
            g, n = (Bm.shape[2], Bm.shape[3])
            nc = l // CHUNK
            xc = x.reshape(b, nc, CHUNK, h, p)
            dtc = dt.reshape(b, nc, CHUNK, h)
            Bc = jnp.repeat(Bm.reshape(b, nc, CHUNK, g, n), h // g, axis=3)
            Cc = jnp.repeat(Cm.reshape(b, nc, CHUNK, g, n), h // g, axis=3)
            dA = dtc * A
            dA_cs = jnp.cumsum(dA, axis=2)
            xt = xc * dtc[..., None]
            diff = dA_cs[:, :, :, None, :] - dA_cs[:, :, None, :, :]
            causal = jnp.tril(jnp.ones((CHUNK, CHUNK), bool))[None, None, :, :, None]
            Lmat = jnp.where(causal, jnp.exp(diff), 0.0)
            scores = jnp.einsum('bcihn,bcjhn->bcijh', Cc, Bc) * Lmat
            y_diag = jnp.einsum('bcijh,bcjhp->bcihp', scores, xt)
            decay_states = jnp.exp(dA_cs[:, :, -1:, :] - dA_cs)
            states = jnp.einsum('bcjhn,bcjh,bcjhp->bchpn', Bc, decay_states, xt)
            chunk_decay = jnp.exp(dA_cs[:, :, -1, :])

            def step(s_prev, inp):
                cd, st = inp
                return (cd[:, :, None, None] * s_prev + st, s_prev)
            init = jnp.zeros((b, h, p, n), x.dtype)
            _, prev_states = jax.lax.scan(step, init, (jnp.moveaxis(chunk_decay, 1, 0), jnp.moveaxis(states, 1, 0)))
            prev_states = jnp.moveaxis(prev_states, 0, 1)
            y_off = jnp.einsum('bcihn,bcih,bchpn->bcihp', Cc, jnp.exp(dA_cs), prev_states)
            return (y_diag + y_off).reshape(b, l, h, p)
        b, l, _ = hidden_states.shape
        zxbcdt = hidden_states @ W_in
        z = zxbcdt[..., :D_INNER]
        xBC = zxbcdt[..., D_INNER:D_INNER + CONV_DIM]
        dt = zxbcdt[..., D_INNER + CONV_DIM:]
        xBC = jax.nn.silu(_causal_dwconv(xBC, conv_w, conv_b))
        x = xBC[..., :D_INNER].reshape(b, l, NHEADS, HEADDIM)
        Bm = xBC[..., D_INNER:D_INNER + NGROUPS * D_STATE].reshape(b, l, NGROUPS, D_STATE)
        Cm = xBC[..., D_INNER + NGROUPS * D_STATE:].reshape(b, l, NGROUPS, D_STATE)
        dt = jax.nn.softplus(dt + dt_bias)
        A = -jnp.exp(A_log)
        y = _ssd(x, dt, A, Bm, Cm) + x * D[None, None, :, None]
        y = y.reshape(b, l, D_INNER)
        y = y * jax.nn.silu(z)
        y = y * jax.lax.rsqrt(jnp.mean(y * y, axis=-1, keepdims=True) + EPS) * norm_w
        return y @ W_out

    def _L0_ffn_ref(x, w_gate, w_up, w_down):
        import jax, jax.numpy as jnp
        import numpy as np
        DIM = 128
        HIDDEN = 384
        SCALE = 1.0 / 127.0

        def _dequant(w_int, dtype):
            return w_int.astype(dtype) * jnp.asarray(SCALE, dtype)
        wg = _dequant(w_gate, x.dtype)
        wu = _dequant(w_up, x.dtype)
        wd = _dequant(w_down, x.dtype)
        gate = jnp.einsum('bsd,hd->bsh', x, wg)
        up = jnp.einsum('bsd,hd->bsh', x, wu)
        h = jax.nn.silu(gate) * up
        return jnp.einsum('bsh,dh->bsd', h, wd)
    x = L0_attn_a_x
    x = x + _L0_attn_a_ref(_layernorm(x, axis=-1), L0_attn_a_Wq, L0_attn_a_bq, L0_attn_a_Wk, L0_attn_a_bk, L0_attn_a_Wv, L0_attn_a_bv, L0_attn_a_Wa, L0_attn_a_ba, L0_attn_a_Wb, L0_attn_a_bb, L0_attn_a_Wg, L0_attn_a_bg, L0_attn_a_Wo, L0_attn_a_bo)
    x = x + _L0_ffn_ref(_layernorm(x, axis=-1), L0_ffn_w_gate, L0_ffn_w_up, L0_ffn_w_down)
    x = x + _L0_attn_b_ref(_layernorm(x, axis=-1), L0_attn_b_W_in, L0_attn_b_conv_w, L0_attn_b_conv_b, L0_attn_b_dt_bias, L0_attn_b_A_log, L0_attn_b_D, L0_attn_b_norm_w, L0_attn_b_W_out)
    x = x + _L0_ffn_ref(_layernorm(x, axis=-1), L0_ffn_w_gate, L0_ffn_w_up, L0_ffn_w_down)
    return x

_drawn_inputs = setup_inputs


def setup_inputs(seed=0):
    import zlib

    import numpy as np

    out = dict(_drawn_inputs(seed))
    spreads = {'L0_attn_b_conv_b': (0.0, 2.0), 'L0_attn_b_norm_w': (1.0, 0.6)}
    factors = {'L0_attn_a_bq': 8.0,
     'L0_attn_a_bk': 8.0,
     'L0_attn_a_bv': 8.0,
     'L0_attn_a_bg': 28.298,
     'L0_attn_a_bo': 3.485,
     'L0_attn_b_W_in': 8.0,
     'L0_attn_b_conv_w': 8.0,
     'L0_attn_b_dt_bias': 8.0,
     'L0_attn_b_A_log': 24.981,
     'L0_attn_b_D': 64.0,
     'L0_attn_b_W_out': 8.0}
    for name, (base, spread) in spreads.items():
        noise = np.random.default_rng([zlib.crc32(name.encode()), seed]).standard_normal(out[name].shape)
        drawn = base * np.exp(spread * noise) if base else spread * noise
        out[name] = jnp.asarray(drawn.astype(out[name].dtype))
    for name, factor in factors.items():
        out[name] = (out[name] * factor).astype(out[name].dtype)
    return out
```

```python
import concourse.bass as bass
from concourse import mybir
from contextlib import ExitStack

BATCH, SEQ, DIM = 32, 256, 128
HIDDEN = 384
HEADS, HEAD_DIM, STATE = 4, 64, 128
INNER = HEADS * HEAD_DIM
TAPS = 4
CHUNK = 32
PROJ = 2 * INNER + 2 * STATE + HEADS
P = 128
TILES = BATCH * SEQ // P
GROUP_TILES = 4
GROUP = GROUP_TILES * P
STREAMS = 2
PAIRS = TILES // (GROUP_TILES * STREAMS)
PAIR_COLS = STREAMS * GROUP
BATCHES = GROUP // SEQ
TRI = SEQ + P
LEVELS = 7
FF_BLOCKS = HIDDEN // P
CONV_BLOCKS = (INNER + 2 * STATE) // P
INNER_BLOCKS = INNER // P
LN_EPS = 1e-5
RMS_EPS = 1e-5
DEQUANT = 1.0 / 127.0


def constants():
    import numpy as np

    r, c = np.arange(P)[:, None], np.arange(P)[None, :]
    eye = (r == c).astype(np.float32)
    parts = [eye, np.zeros((P, P), np.float32)]
    for level in range(LEVELS):
        n = 2 ** level
        below = (r // (2 * n) == c // (2 * n)) & (r % (2 * n) >= n) & (c % (2 * n) < n)
        parts.append(eye - below.astype(np.float32))
    parts.append(np.broadcast_to((c % CHUNK != 0).astype(np.float32), (P, P)))
    return np.ascontiguousarray(np.concatenate(parts, axis=1))


def build(nc, x_in, Wq, bq, Wk, bk, Wv, bv, Wa, ba, Wb, bb, Wg, bg, Wo, bo,
          W_in, conv_w, conv_b, dt_bias, A_log, D_skip, norm_w, W_out,
          w_gate, w_up, w_down, tables, out, stop_after=4):
    f32, i32 = mybir.dt.float32, mybir.dt.int32
    ALU, ACT, AX = mybir.AluOpType, mybir.ActivationFunctionType, mybir.AxisListType
    ds = bass.ds

    ctx = ExitStack()
    with ctx:
        def sb(name, shape, dt=f32):
            return ctx.enter_context(nc.sbuf_tensor(name, shape, dt))

        def sem(name):
            return ctx.enter_context(nc.semaphore(name))

        def upto(n, u):
            return STREAMS * n + u + 1

        paced = []

        def pace(name):
            paced.append(sem(name))
            return paced[-1]

        x_all = sb("x_all", [P, TILES * DIM])
        tab = sb("tab", [P, (3 + LEVELS) * P])
        ident, eye_zero = tab[:, 0:P], tab[:, 0:2 * P]
        keep = tab[:, (2 + LEVELS) * P:(3 + LEVELS) * P]
        masks = [tab[:, (2 + k) * P:(3 + k) * P] for k in range(LEVELS)]
        half_neg = sb("half_neg", [P, GROUP_TILES])
        eps_cols = sb("eps_cols", [P, GROUP_TILES])
        ones_col = sb("ones_col", [P, 1])

        wq_sb, wg_sb, wo_sb = sb("wq_sb", [P, P]), sb("wg_sb", [P, P]), sb("wo_sb", [P, P])
        wk_sb, wv_sb = sb("wk_sb", [P, P]), sb("wv_sb", [P, P])
        wab_sb = sb("wab_sb", [P, 2])
        bq_col, bg_col = sb("bq_col", [P, 1]), sb("bg_col", [P, 1])
        bk_row, bv_row, bo_row = sb("bk_row", [P, P]), sb("bv_row", [P, P]), sb("bo_row", [P, P])
        bab_row = sb("bab_row", [P, 2])
        win_sb = sb("win_sb", [P, PROJ])
        wout_sb = sb("wout_sb", [P, INNER_BLOCKS, DIM])
        wout_raw = sb("wout_raw", [P, INNER_BLOCKS, DIM])
        convw_sb = sb("convw_sb", [P, CONV_BLOCKS, TAPS])
        convb_sb = sb("convb_sb", [P, CONV_BLOCKS])
        normw_col = sb("normw_col", [P, INNER_BLOCKS])
        skip_col = sb("skip_col", [P, INNER_BLOCKS])
        dtb_row = sb("dtb_row", [P, HEADS])
        alog_row = sb("alog_row", [P, HEADS])
        aexp_row = sb("aexp_row", [P, HEADS])
        aneg_row = sb("aneg_row", [P, HEADS])
        ff_int = sb("ff_int", [P, 3, HIDDEN], i32)
        ff_raw = sb("ff_raw", [P, 3, HIDDEN])
        gateT, upT = sb("gateT", [P, HIDDEN]), sb("upT", [P, HIDDEN])
        downT = sb("downT", [P, FF_BLOCKS, DIM])

        U = range(STREAMS)
        stats = [sb(f"stats{u}", [P, GROUP_TILES, 6]) for u in U]
        mv = [sb(f"mv{u}", [P, GROUP_TILES, 2]) for u in U]
        carrier = [sb(f"carrier{u}", [P, 1]) for u in U]
        var_eps = [sb(f"var_eps{u}", [P, GROUP_TILES]) for u in U]
        rstd = [sb(f"rstd{u}", [P, GROUP_TILES]) for u in U]
        xn = [sb(f"xn{u}", [P, GROUP]) for u in U]
        xnT = [sb(f"xnT{u}", [P, GROUP]) for u in U]
        silu_g = [sb(f"silu_g{u}", [P, FF_BLOCKS, GROUP]) for u in U]
        hidT = [sb(f"hidT{u}", [P, FF_BLOCKS, GROUP]) for u in U]
        ARENA = 20 * GROUP + 64
        arena = [sb(f"arena{u}", [P, ARENA]) for u in U]

        def carver():
            at = [0]

            def carve(cols):
                a, at[0] = at[0], at[0] + cols
                assert at[0] <= ARENA, at[0]
                return [arena[u][:, a:a + cols] for u in U]
            return carve

        carve = carver()
        kb, ksq, kn, kT = carve(GROUP), carve(GROUP), carve(GROUP), carve(GROUP)
        vtok, qT, gT, xb = carve(GROUP), carve(GROUP), carve(GROUP), carve(GROUP)
        gam, LT, PT = carve(BATCHES * TRI), carve(BATCHES * TRI), carve(BATCHES * TRI)
        Tm, Rm, Wm, WT, og = carve(GROUP), carve(GROUP), carve(GROUP), carve(GROUP), carve(GROUP)
        w0tok = carve(BATCHES * P)
        ablog, ab = carve(2 * GROUP_TILES), carve(2 * GROUP_TILES)
        kss, kinv = carve(GROUP_TILES), carve(GROUP_TILES)
        carve = carver()
        xbc = [carve(GROUP) for _ in range(CONV_BLOCKS)]
        siluz = [carve(GROUP) for _ in range(INNER_BLOCKS)]
        xtok = carve(GROUP_TILES * INNER)
        cb = carve(BATCHES * TRI)
        hgam = [carve(BATCHES * TRI) for _ in range(2)]
        score = [carve(BATCHES * TRI) for _ in range(2)]
        yT = [carve(GROUP) for _ in range(INNER_BLOCKS)]
        ysq = [carve(GROUP) for _ in range(INNER_BLOCKS)]
        ms, rms = carve(GROUP_TILES), carve(GROUP_TILES)
        DT = GROUP_TILES * HEADS
        ROWS = STREAMS * DT
        csum, dstep = sb("csum", [ROWS, P]), sb("dstep", [P, P])
        small = [sb(f"dt_{n}", [P, STREAMS * DT]) for n in
                 ("z", "nabs", "e", "den", "rec", "w", "w2", "acc", "relu", "dt", "dA", "decay")]
        z_dt, nabs_dt, e_dt, den_dt, rec_dt, w_dt, w2_dt, acc_dt, relu_dt, dt_dt, dA_dt, decay = small

        bank = [[ctx.enter_context(nc.psum_tensor(f"bank{u}_{k}", [P, GROUP], f32)) for k in range(4)]
                for u in U]

        first_x_in, rest_x_in, weights_in, x_out = sem("first_x_in"), sem("rest_x_in"), sem("weights_in"), sem("x_out")
        consts_set, ff_float, ffT_mm, ffT_done, aexp_done, prep_done = (
            sem("consts_set"), sem("ff_float"), sem("ffT_mm"), sem("ffT_done"), sem("aexp_done"), sem("prep_done"))
        stats_done, mv_done, var_done, rstd_done, xn_done, tr_done, xnT_done, x_done = (
            pace(n) for n in ("stats_done", "mv_done", "var_done", "rstd_done", "xn_done", "tr_done", "xnT_done", "x_done"))
        gate_mm, up_mm, down_mm, silu_done, hid_done = (
            pace(n) for n in ("gate_mm", "up_mm", "down_mm", "silu_done", "hid_done"))
        k_mm, v_mm, ab_mm, q_mm, g_mm, kT_mm, abc_mm, G_mm, Z_mm, T_mm, R_mm, w0_mm, corr_mm, WT_mm, PT_mm, OT_mm, y_mm = (
            pace(n) for n in ("k_mm", "v_mm", "ab_mm", "q_mm", "g_mm", "kT_mm", "abc_mm", "G_mm", "Z_mm", "T_mm",
                              "R_mm", "w0_mm", "corr_mm", "WT_mm", "PT_mm", "OT_mm", "y_mm"))
        kb_done, v_done, ablog_done, ab_done, q_done, g_done, ksq_done, kss_done, kmax_done, kinv_done, kn_done, kT_done = (
            pace(n) for n in ("kb_done", "v_done", "ablog_done", "ab_done", "q_done", "g_done", "ksq_done", "kss_done",
                              "kmax_done", "kinv_done", "kn_done", "kT_done"))
        gam_done, LTraw_done, LT_done, W_done, T_done, R_done, w0_done, v1_done, WT_done, PT_done, og_done, xb_done = (
            pace(n) for n in ("gam_done", "LTraw_done", "LT_done", "W_done", "T_done", "R_done", "w0_done", "v1_done",
                              "WT_done", "PT_done", "og_done", "xb_done"))
        dt_mm, conv_mm, z_mm, xtok_mm, cb_mm, habc_mm, hy_mm, out_mm = (
            pace(n) for n in ("dt_mm", "conv_mm", "z_mm", "xtok_mm", "cb_mm", "habc_mm", "hy_mm", "out_mm"))
        conv_init, tap_done, xbc_done, sz_done, xtok_done, cb_done, hgam_done, score_done, ydt_done, yT_done, ysq_done, ms_done, rms_done = (
            pace(n) for n in ("conv_init", "tap_done", "xbc_done", "sz_done", "xtok_done", "cb_done", "hgam_done",
                              "score_done", "ydt_done", "yT_done", "ysq_done", "ms_done", "rms_done"))
        zdt_done = pace("zdt_done")
        dt_step, e_done, decay_done, dAT_mm, back_mm = (sem(n) for n in ("dt_step", "e_done", "decay_done", "dAT_mm", "back_mm"))
        N_WEIGHT_DMAS = 23 + CONV_BLOCKS + INNER_BLOCKS + HEADS

        def tile4(ap):
            return ap.rearrange("p (t c) -> p t c", t=GROUP_TILES)

        def cols(k):
            return slice(k * P, (k + 1) * P)

        def strip(b, c):
            a = b * TRI + c * SEQ
            return slice(a, a + SEQ - c * P)

        def diag(t):
            a = (t // 2) * TRI + (t % 2) * SEQ
            return slice(a, a + P)

        def group_cols(pair, u):
            return ds(pair * PAIR_COLS + u * GROUP, GROUP)

        SERIES = [1.0 / n for n in range(13, 2, -2)]
        DT_STEPS = 1 + 6 + len(SERIES) + 3
        CS_STEPS = 3

        block = ctx.enter_context(nc.Block())

        @block.sync
        def _(sp):
            x_tok = x_in.rearrange("b (c p) d -> p (b c) d", p=P)
            x_sb = x_all[:, :].rearrange("p (n d) -> p n d", d=DIM)
            step = GROUP_TILES * STREAMS
            sp.dma_start(x_sb[:, 0:step, :], x_tok[:, 0:step, :]).then_inc(first_x_in, 16)

            def load(dst, src):
                sp.dma_start(dst, src).then_inc(weights_in, 16)

            def column(v):
                return v.rearrange("(p a) -> p a", a=1)

            def row(v):
                return v.rearrange("(a n) -> a n", a=1).partition_broadcast(P)

            load(tab[:, :], tables)
            for dst, src in ((wk_sb, Wk), (wv_sb, Wv), (wq_sb, Wq), (wg_sb, Wg), (wo_sb, Wo)):
                load(dst[:, :], src)
            load(wab_sb[:, 0:1], Wa)
            load(wab_sb[:, 1:2], Wb)
            load(bq_col[:, :], column(bq))
            load(bg_col[:, :], column(bg))
            for dst, src in ((bk_row[:, :], bk), (bv_row[:, :], bv), (bo_row[:, :], bo),
                             (bab_row[:, 0:1], ba), (bab_row[:, 1:2], bb)):
                load(dst, row(src)[:, 0, :])
            load(ff_int[:, 0, :].rearrange("p (k d) -> p k d", d=DIM), w_gate.rearrange("(k p) d -> p k d", p=P))
            load(ff_int[:, 1, :].rearrange("p (k d) -> p k d", d=DIM), w_up.rearrange("(k p) d -> p k d", p=P))
            load(ff_int[:, 2, :], w_down)
            load(win_sb[:, :], W_in)
            load(wout_raw[:, :, :], W_out.rearrange("(k p) d -> p k d", p=P))
            load(convw_sb[:, :, :], conv_w.rearrange("(k p) t -> p k t", p=P))
            for k in range(CONV_BLOCKS):
                load(convb_sb[:, k:k + 1], column(conv_b[k * P:(k + 1) * P]))
            for k in range(INNER_BLOCKS):
                load(normw_col[:, k:k + 1], column(norm_w[k * P:(k + 1) * P]))
            load(dtb_row[:, :], row(dt_bias)[:, 0, :])
            load(alog_row[:, :], row(A_log)[:, 0, :])
            for h in range(HEADS):
                half = (h % 2) * HEAD_DIM
                load(skip_col[half:half + HEAD_DIM, h // 2:h // 2 + 1],
                     D_skip[h:h + 1].rearrange("(a n) -> a n", a=1).partition_broadcast(HEAD_DIM)[:, 0, :])
            for k in range(1, PAIRS):
                sp.dma_start(x_sb[:, k * step:(k + 1) * step, :],
                             x_tok[:, k * step:(k + 1) * step, :]).then_inc(rest_x_in, 16)
            out_tok = out.rearrange("b (c p) d -> p (b c) d", p=P)
            for k in range(PAIRS):
                for u in U:
                    sp.wait_ge(x_done, upto(PAIRS * (stop_after - 1) + k + 1, u))
                sp.dma_start(out_tok[:, k * step:(k + 1) * step, :],
                             x_sb[:, k * step:(k + 1) * step, :]).then_inc(x_out, 16)
            sp.wait_ge(x_out, 16 * PAIRS)

        @block.gpsimd
        def _(pool):
            nc.gpsimd.memset(half_neg[:, :], -0.5).then_inc(consts_set, 1)
            nc.gpsimd.memset(ones_col[:, :], 1.0).then_inc(consts_set, 1)
            nc.gpsimd.memset(eps_cols[:, :], LN_EPS).then_inc(consts_set, 1)
            nc.gpsimd.memset(dstep[:, :], 0.0).then_inc(consts_set, 1)
            pool.wait_ge(consts_set, 4)
            pool.wait_ge(weights_in, 16 * N_WEIGHT_DMAS)

            def ln_rstd(k):
                for u in U:
                    pool.wait_ge(mv_done, upto(k + 1, u))
                    nc.gpsimd.tensor_tensor(var_eps[u][:, :], mv[u][:, :, 1], eps_cols[:, :], ALU.add).then_inc(var_done, 1)
                for u in U:
                    pool.wait_ge(var_done, upto(k + 1, u))
                    nc.gpsimd.tensor_tensor(rstd[u][:, :], var_eps[u][:, :], half_neg[:, :], ALU.pow).then_inc(rstd_done, 1)

            ln_rstd(0)
            with pool.Fori(0, PAIRS) as i:
                for u in U:
                    pool.wait_ge(xb_done, upto(i, u))
                    pool.wait_ge(x_done, upto(i, u))
                    nc.gpsimd.tensor_tensor(tile4(xb[u]), tile4(x_all[:, group_cols(i, u)]),
                                            bo_row[:, :].unsqueeze(1).broadcast_to([P, GROUP_TILES, P]),
                                            ALU.add).then_inc(xb_done, 1)
                for u in U:
                    pool.wait_ge(kmax_done, upto(i + 1, u))
                    nc.gpsimd.tensor_tensor(kinv[u], kss[u], half_neg[:, :], ALU.pow).then_inc(kinv_done, 1)
                for u in U:
                    pool.wait_ge(consts_set, 4)
                    pool.wait_ge(LTraw_done, upto(i + 1, u))
                    for b in range(BATCHES):
                        square = LT[u][:, b * TRI:(b + 1) * TRI].rearrange("p (s c) -> p s c", c=P)[:, 0:3:2, :]
                        last = nc.gpsimd.affine_select(out=square, in_=square, compare_op=ALU.not_equal, fill=1.0, base=0,
                                                       pattern=[[0, 2], [-1, P]], channel_multiplier=1)
                    last.then_inc(LT_done, 1)
                ln_rstd(i + 1)
            if stop_after > 1:
                with pool.Fori(0, PAIRS) as i:
                    ln_rstd(PAIRS + i + 1)
            if stop_after > 2:
                with pool.Fori(0, PAIRS) as i:
                    ln_rstd(2 * PAIRS + i + 1)
                    for r in range(INNER_BLOCKS):
                        for u in U:
                            pool.wait_ge(ydt_done, upto(INNER_BLOCKS * i + r + 1, u))
                            pool.wait_ge(sz_done, upto(INNER_BLOCKS * i + r + 1, u))
                            nc.gpsimd.tensor_tensor(yT[r][u], yT[r][u], siluz[r][u], ALU.mult).then_inc(yT_done, 1)
                    for u in U:
                        pool.wait_ge(ms_done, upto(i + 1, u))
                        nc.gpsimd.tensor_tensor(rms[u], ms[u], half_neg[:, :], ALU.pow).then_inc(rms_done, 1)
            if stop_after > 3:
                with pool.Fori(0, PAIRS) as i:
                    ln_rstd(3 * PAIRS + i + 1)

        @block.scalar
        def _(act):
            act.wait_ge(weights_in, 16 * N_WEIGHT_DMAS)
            nc.scalar.activation(aexp_row[:, :], alog_row[:, :], ACT.Exp).then_inc(aexp_done, 1)

            def feature_major(k, src):
                for u in U:
                    act.wait_ge(tr_done, upto(k + 1, u))
                    nc.scalar.activation(xnT[u][:, :], bank[u][src][:, :], ACT.Copy).then_inc(xnT_done, 1)

            feature_major(0, 3)

            with act.Fori(0, PAIRS) as i:
                for u in U:
                    act.wait_ge(kb_done, upto(i + 1, u))
                    nc.scalar.activation(ksq[u], kb[u], ACT.Square).then_inc(ksq_done, 1)
                for u in U:
                    act.wait_ge(ablog_done, upto(i + 1, u))
                    act.wait_ge(PT_done, upto(i, u))
                    nc.scalar.activation(ab[u], ablog[u], ACT.Sigmoid).then_inc(ab_done, 1)
                for u in U:
                    act.wait_ge(q_mm, upto(i + 1, u))
                    act.wait_ge(PT_mm, upto(i, u))
                    nc.scalar.activation(qT[u], bank[u][3][:, :], ACT.Identity, bias=bq_col[:, :]).then_inc(q_done, 1)
                for u in U:
                    act.wait_ge(g_mm, upto(i + 1, u))
                    act.wait_ge(og_done, upto(i, u))
                    nc.scalar.activation(gT[u], bank[u][2][:, :], ACT.Sigmoid, bias=bg_col[:, :]).then_inc(g_done, 1)
                for u in U:
                    act.wait_ge(kT_mm, upto(i + 1, u))
                    nc.scalar.activation(kT[u], bank[u][1][:, :], ACT.Copy).then_inc(kT_done, 1)
                for level in range(LEVELS):
                    for u in U:
                        if 0 < level < LEVELS - 1:
                            act.wait_ge(T_mm, upto((LEVELS - 2) * i + level, u))
                            nc.scalar.activation(Tm[u], bank[u][2][:, :], ACT.Copy).then_inc(T_done, 1)
                        act.wait_ge(R_mm, upto(LEVELS * i + level + 1, u))
                        nc.scalar.activation(Rm[u], bank[u][0][:, :], ACT.Copy).then_inc(R_done, 1)
                for u in U:
                    act.wait_ge(w0_mm, upto(i + 1, u))
                    nc.scalar.activation(w0tok[u], bank[u][3][:, 0:BATCHES * P], ACT.Copy).then_inc(w0_done, 1)
                for u in U:
                    act.wait_ge(WT_mm, upto(i + 1, u))
                    nc.scalar.activation(WT[u], bank[u][1][:, :], ACT.Copy).then_inc(WT_done, 1)
                feature_major(i + 1, 3)

            def ffn(run):
                with act.Fori(0, PAIRS) as i:
                    n = FF_BLOCKS * (i + PAIRS * run)
                    for j in range(FF_BLOCKS):
                        for u in U:
                            act.wait_ge(gate_mm, upto(n + j + 1, u))
                            act.wait_ge(hid_done, upto(n, u))
                            nc.scalar.activation(silu_g[u][:, j, :], bank[u][(1, 3, 1)[j]][:, :], ACT.Silu,
                                                 scale=DEQUANT).then_inc(silu_done, 1)
                    for u in U:
                        act.wait_ge(up_mm, upto(n + FF_BLOCKS, u))
                    feature_major((2 * run + 1) * PAIRS + i + 1, 0)

            if stop_after > 1:
                ffn(0)

            if stop_after > 2:
                with act.Fori(0, PAIRS) as i:
                    act.wait_ge(dt_step, (DT_STEPS + CS_STEPS) * i + 1)
                    nc.scalar.activation(e_dt[:, :], nabs_dt[:, :], ACT.Exp).then_inc(e_done, 1)
                    for r in range(CONV_BLOCKS + 1):
                        for u in U:
                            if r < CONV_BLOCKS:
                                act.wait_ge(conv_mm, upto(CONV_BLOCKS * i + r + 1, u))
                                act.wait_ge(ydt_done, upto(INNER_BLOCKS * i, u))
                                nc.scalar.activation(xbc[r][u], bank[u][(0, 1, 2, 0)[r]][:, :], ACT.Identity,
                                                     scale=convw_sb[:, r, TAPS - 1:TAPS],
                                                     bias=convb_sb[:, r:r + 1]).then_inc(conv_init, 1)
                        for u in U:
                            if r > 0:
                                act.wait_ge(tap_done, upto((TAPS - 1) * (CONV_BLOCKS * i + r), u))
                                nc.scalar.activation(xbc[r - 1][u], xbc[r - 1][u], ACT.Silu).then_inc(xbc_done, 1)
                    for r in range(INNER_BLOCKS):
                        for u in U:
                            act.wait_ge(z_mm, upto(INNER_BLOCKS * i + r + 1, u))
                            act.wait_ge(yT_done, upto(INNER_BLOCKS * i, u))
                            nc.scalar.activation(siluz[r][u], bank[u][1 + r][:, :], ACT.Silu).then_inc(sz_done, 1)
                    act.wait_ge(back_mm, i + 2)
                    for u in U:
                        act.wait_ge(habc_mm, upto(HEADS * i, u))
                    nc.scalar.activation(decay[:, :], bank[1][3][:, 0:ROWS], ACT.Exp).then_inc(decay_done, 1)
                    for r in range(INNER_BLOCKS):
                        for u in U:
                            act.wait_ge(xtok_mm, upto(INNER_BLOCKS * i + r + 1, u))
                            act.wait_ge(hy_mm, upto(HEADS * i, u))
                            nc.scalar.activation(
                                xtok[u].rearrange("p (t c) -> p t c", t=GROUP_TILES)[:, :, cols(r)],
                                tile4(bank[u][(3, 0)[r]][:, :]), ACT.Copy).then_inc(xtok_done, 1)
                    for b in range(BATCHES):
                        for u in U:
                            act.wait_ge(cb_mm, upto(BATCHES * i + b + 1, u))
                            act.wait_ge(score_done, upto(HEADS * i, u))
                            nc.scalar.activation(cb[u][:, b * TRI:(b + 1) * TRI], bank[u][1 + b][:, 0:TRI],
                                                 ACT.Copy).then_inc(cb_done, 1)
                    for r in range(INNER_BLOCKS):
                        for u in U:
                            act.wait_ge(yT_done, upto(INNER_BLOCKS * i + r + 1, u))
                            act.wait_ge(out_mm, upto(i, u))
                            nc.scalar.activation(ysq[r][u], yT[r][u], ACT.Square).then_inc(ysq_done, 1)
                    feature_major(2 * PAIRS + i + 1, 1)
            if stop_after > 3:
                ffn(1)

        @block.vector
        def _(dve):
            def stats_of(k, pair):
                for u in U:
                    if not isinstance(k, int):
                        dve.wait_ge(x_done, upto(k - 1, u))
                    for t in range(GROUP_TILES):
                        last = nc.vector.bn_stats(stats[u][:, t, :], x_all[:, ds(pair * PAIR_COLS + u * GROUP + t * P, P)])
                    last.then_inc(stats_done, 1)
                for u in U:
                    dve.wait_ge(stats_done, upto(k + 1, u))
                    nc.vector.memset(carrier[u][:, :], 0.0)
                    for t in range(GROUP_TILES):
                        last = nc.vector.bn_aggr(mv[u][:, t, :], stats[u][:, t, :])
                    last.then_inc(mv_done, 1)

            def normalise(k, pair):
                for u in U:
                    dve.wait_ge(rstd_done, upto(k + 1, u))
                    dve.wait_ge(tr_done, upto(k, u))
                    for t in range(GROUP_TILES):
                        last = nc.vector.tensor_scalar(xn[u][:, cols(t)],
                                                       x_all[:, ds(pair * PAIR_COLS + u * GROUP + t * P, P)],
                                                       mv[u][:, t, 0:1], rstd[u][:, t:t + 1], ALU.subtract, ALU.mult)
                    last.then_inc(xn_done, 1)

            dve.wait_ge(first_x_in, 16)
            stats_of(0, 0)
            normalise(0, 0)
            dve.wait_ge(weights_in, 16 * N_WEIGHT_DMAS)
            nc.vector.tensor_copy(ff_raw[:, :, :], ff_int[:, :, :]).then_inc(ff_float, 1)
            for k in range(INNER_BLOCKS):
                nc.vector.tensor_scalar(wout_sb[:, k, :], wout_raw[:, k, :], normw_col[:, k:k + 1], None,
                                        ALU.mult).then_inc(prep_done, 1)
            dve.wait_ge(aexp_done, 1)
            nc.vector.tensor_scalar(aneg_row[:, :], aexp_row[:, :], -1.0, None, ALU.mult).then_inc(prep_done, 1)
            for n, dst in enumerate((gateT[:, :], upT[:, :], downT[:, :, :].rearrange("p k d -> p (k d)"))):
                dve.wait_ge(ffT_mm, n + 1)
                nc.vector.tensor_copy(dst, bank[0][n][:, 0:HIDDEN]).then_inc(ffT_done, 1)
            dve.wait_ge(consts_set, 4)
            dve.wait_ge(rest_x_in, 16 * (PAIRS - 1))

            def per_tile(ap):
                return ap.unsqueeze(1).broadcast_to([P, GROUP_TILES, ap.shape[-1]])

            with dve.Fori(0, PAIRS) as i:
                nxt = (i + 1) % PAIRS
                for u in U:
                    dve.wait_ge(k_mm, upto(i + 1, u))
                    nc.vector.tensor_tensor(tile4(kb[u]), tile4(bank[u][0][:, :]), per_tile(bk_row[:, :]),
                                            ALU.add).then_inc(kb_done, 1)
                for u in U:
                    dve.wait_ge(v_mm, upto(i + 1, u))
                    dve.wait_ge(WT_mm, upto(i, u))
                    nc.vector.tensor_tensor(tile4(vtok[u]), tile4(bank[u][1][:, :]), per_tile(bv_row[:, :]),
                                            ALU.add).then_inc(v_done, 1)
                for u in U:
                    dve.wait_ge(ab_mm, upto(i + 1, u))
                    nc.vector.tensor_tensor(tile4(ablog[u]), tile4(bank[u][2][:, 0:2 * GROUP_TILES]),
                                            per_tile(bab_row[:, :]), ALU.add).then_inc(ablog_done, 1)
                for u in U:
                    dve.wait_ge(ksq_done, upto(i + 1, u))
                    nc.vector.tensor_reduce(kss[u], tile4(ksq[u]), AX.X, ALU.add).then_inc(kss_done, 1)
                for u in U:
                    dve.wait_ge(kss_done, upto(i + 1, u))
                    nc.vector.tensor_scalar(kss[u], kss[u], 1e-24, None, ALU.max).then_inc(kmax_done, 1)
                for u in U:
                    dve.wait_ge(kinv_done, upto(i + 1, u))
                    dve.wait_ge(OT_mm, upto(i, u))
                    nc.vector.tensor_tensor(tile4(kn[u]), tile4(kb[u]),
                                            kinv[u].unsqueeze(2).broadcast_to([P, GROUP_TILES, P]),
                                            ALU.mult).then_inc(kn_done, 1)
                for u in U:
                    dve.wait_ge(abc_mm, upto(i + 1, u))
                    for b in range(BATCHES):
                        for c in range(2):
                            n = SEQ - c * P
                            last = nc.vector.tensor_tensor_scan(
                                gam[u][:, strip(b, c)], bank[u][0][:, b * SEQ + c * P:(b + 1) * SEQ],
                                eye_zero[:, 0:n], 0.0, ALU.mult, ALU.add)
                    last.then_inc(gam_done, 1)
                stats_of(i + 1, nxt)
                for u in U:
                    dve.wait_ge(gam_done, upto(i + 1, u))
                    dve.wait_ge(G_mm, upto(i + 1, u))
                    dve.wait_ge(corr_mm, upto(i, u))
                    for b in range(BATCHES):
                        for c in range(2):
                            n = SEQ - c * P
                            last = nc.vector.scalar_tensor_tensor(
                                LT[u][:, strip(b, c)], bank[u][2 + b][:, c * SEQ:c * SEQ + n],
                                tile4(ab[u])[:, 2 * b + c, 1:2], gam[u][:, strip(b, c)], ALU.mult, ALU.mult)
                    last.then_inc(LTraw_done, 1)
                for level in range(LEVELS):
                    for u in U:
                        dve.wait_ge(Z_mm, upto(LEVELS * i + level + 1, u))
                        dst = Tm if level == 0 else Wm
                        if level == 0:
                            dve.wait_ge(R_mm, upto(LEVELS * i, u))
                        else:
                            dve.wait_ge(R_mm, upto(LEVELS * i + level, u))
                            if level > 1:
                                dve.wait_ge(T_mm, upto((LEVELS - 2) * i + level - 1, u))
                        nc.vector.tensor_tensor(tile4(dst[u]), tile4(bank[u][1][:, :]), per_tile(masks[level]),
                                                ALU.mult).then_inc(W_done, 1)
                    if level == 2:
                        normalise(i + 1, nxt)
                for u in U:
                    dve.wait_ge(corr_mm, upto(i + 1, u))
                    second = tile4(vtok[u])[:, 1:GROUP_TILES:2, :]
                    nc.vector.tensor_tensor(second, second,
                                            bank[u][2][:, 0:BATCHES * P].rearrange("p (b c) -> p b c", c=P),
                                            ALU.subtract).then_inc(v1_done, 1)
                for u in U:
                    dve.wait_ge(PT_mm, upto(i + 1, u))
                    dve.wait_ge(OT_mm, upto(i, u))
                    for b in range(BATCHES):
                        for c in range(2):
                            n = SEQ - c * P
                            last = nc.vector.scalar_tensor_tensor(
                                PT[u][:, strip(b, c)], bank[u][(0, 3)[b]][:, c * SEQ:c * SEQ + n],
                                tile4(ab[u])[:, 2 * b + c, 1:2], gam[u][:, strip(b, c)], ALU.mult, ALU.mult)
                    last.then_inc(PT_done, 1)
                for u in U:
                    dve.wait_ge(OT_mm, upto(i + 1, u))
                    dve.wait_ge(y_mm, upto(i, u))
                    nc.vector.tensor_tensor(og[u], bank[u][2][:, :], gT[u], ALU.mult).then_inc(og_done, 1)
                for u in U:
                    dve.wait_ge(y_mm, upto(i + 1, u))
                    dve.wait_ge(xb_done, upto(i + 1, u))
                    nc.vector.tensor_tensor(x_all[:, group_cols(i, u)], bank[u][1][:, :], xb[u],
                                            ALU.add).then_inc(x_done, 1)

            def ffn(run):
                phase = 2 * run + 1
                with dve.Fori(0, PAIRS) as i:
                    nxt = (i + 1) % PAIRS
                    it = phase * PAIRS + i
                    n = FF_BLOCKS * (i + PAIRS * run)
                    for j in range(FF_BLOCKS):
                        for u in U:
                            dve.wait_ge(silu_done, upto(n + j + 1, u))
                            dve.wait_ge(up_mm, upto(n + j + 1, u))
                            dve.wait_ge(down_mm, upto(i + PAIRS * run, u))
                            nc.vector.scalar_tensor_tensor(hidT[u][:, j, :], bank[u][(2, 0, 2)[j]][:, :], DEQUANT,
                                                           silu_g[u][:, j, :], ALU.mult, ALU.mult).then_inc(hid_done, 1)
                        if j == 0:
                            stats_of(it + 1, nxt)
                        if j == 1:
                            normalise(it + 1, nxt)
                    for u in U:
                        dve.wait_ge(down_mm, upto(i + PAIRS * run + 1, u))
                        nc.vector.scalar_tensor_tensor(x_all[:, group_cols(i, u)], bank[u][3][:, :], DEQUANT,
                                                       x_all[:, group_cols(i, u)], ALU.mult, ALU.add).then_inc(x_done, 1)

            if stop_after > 1:
                ffn(0)

            if stop_after > 2:
                with dve.Fori(0, PAIRS) as i:
                    nxt = (i + 1) % PAIRS
                    it = 2 * PAIRS + i
                    taken = [0]

                    def step(ins):
                        taken[0] += 1
                        ins.then_inc(dt_step, 1)

                    def prior():
                        dve.wait_ge(dt_step, (DT_STEPS + CS_STEPS) * i + taken[0])

                    for u in U:
                        dve.wait_ge(dt_mm, upto(i + 1, u))
                        nc.vector.tensor_tensor(tile4(z_dt[:, u * DT:(u + 1) * DT]), tile4(bank[u][3][:, 0:DT]),
                                                per_tile(dtb_row[:, :]), ALU.add).then_inc(zdt_done, 1)
                    for u in U:
                        dve.wait_ge(zdt_done, upto(i + 1, u))
                    dve.wait_ge(e_done, i + 1)
                    step(nc.vector.scalar_tensor_tensor(nabs_dt[:, :], z_dt[:, :], -1.0, z_dt[:, :], ALU.mult, ALU.min))
                    dve.wait_ge(e_done, i + 2)
                    step(nc.vector.tensor_scalar(den_dt[:, :], e_dt[:, :], 2.0, None, ALU.add))
                    prior()
                    step(nc.vector.reciprocal(rec_dt[:, :], den_dt[:, :]))
                    prior()
                    step(nc.vector.tensor_tensor(w_dt[:, :], e_dt[:, :], rec_dt[:, :], ALU.mult))
                    prior()
                    step(nc.vector.tensor_tensor(w2_dt[:, :], w_dt[:, :], w_dt[:, :], ALU.mult))
                    prior()
                    step(nc.vector.tensor_scalar(acc_dt[:, :], w2_dt[:, :], 1.0 / 15, None, ALU.mult))
                    for c in SERIES:
                        prior()
                        step(nc.vector.scalar_tensor_tensor(acc_dt[:, :], acc_dt[:, :], c, w2_dt[:, :], ALU.add, ALU.mult))
                    prior()
                    step(nc.vector.scalar_tensor_tensor(acc_dt[:, :], acc_dt[:, :], 1.0, w_dt[:, :], ALU.add, ALU.mult))
                    step(nc.vector.tensor_scalar(relu_dt[:, :], z_dt[:, :], 0.0, None, ALU.max))
                    prior()
                    step(nc.vector.scalar_tensor_tensor(dt_dt[:, :], acc_dt[:, :], 2.0, relu_dt[:, :], ALU.mult, ALU.add))
                    prior()
                    step(nc.vector.tensor_tensor(
                        dA_dt[:, :].rearrange("p (t h) -> p t h", h=HEADS), dt_dt[:, :].rearrange("p (t h) -> p t h", h=HEADS),
                        aneg_row[:, :].unsqueeze(1).broadcast_to([P, STREAMS * GROUP_TILES, HEADS]), ALU.mult))
                    assert taken[0] == DT_STEPS, taken[0]

                    for r in range(CONV_BLOCKS):
                        for s in range(1, TAPS):
                            for u in U:
                                if s == 1:
                                    dve.wait_ge(conv_init, upto(CONV_BLOCKS * i + r + 1, u))
                                else:
                                    dve.wait_ge(tap_done, upto((TAPS - 1) * (CONV_BLOCKS * i + r) + s - 1, u))
                                src = bank[u][(0, 1, 2, 0)[r]][:, :].rearrange("p (b t) -> p b t", t=SEQ)[:, :, 0:SEQ - s]
                                acc = xbc[r][u].rearrange("p (b t) -> p b t", t=SEQ)[:, :, s:SEQ]
                                nc.vector.scalar_tensor_tensor(acc, src, convw_sb[:, r, TAPS - 1 - s:TAPS - s], acc,
                                                               ALU.mult, ALU.add).then_inc(tap_done, 1)
                        if r == 2:
                            dve.wait_ge(dAT_mm, i + 1)
                            step(nc.vector.tensor_tensor_scan(csum[:, :], keep[0:ROWS, :], bank[0][3][0:ROWS, 0:P], 0.0,
                                                              ALU.mult, ALU.add))
                            prior()
                            dve.wait_ge(back_mm, i + 1)
                            of_chunk = csum[:, :].rearrange("r (c t) -> r c t", t=CHUNK)
                            step_of_chunk = dstep[0:ROWS, :].rearrange("r (c t) -> r c t", t=CHUNK)
                            step(nc.vector.tensor_tensor(step_of_chunk[:, :, 1:CHUNK], of_chunk[:, :, 1:CHUNK],
                                                         of_chunk[:, :, 0:CHUNK - 1], ALU.subtract))
                            step(nc.vector.tensor_copy(step_of_chunk[:, :, 0:1], of_chunk[:, :, 0:1]))
                            assert taken[0] == DT_STEPS + CS_STEPS, taken[0]
                    stats_of(it + 1, nxt)
                    for h in range(HEADS):
                        for u in U:
                            dve.wait_ge(habc_mm, upto(HEADS * i + h + 1, u))
                            for b in range(BATCHES):
                                for c in range(2):
                                    n = SEQ - c * P
                                    last = nc.vector.tensor_tensor_scan(
                                        hgam[h % 2][u][:, strip(b, c)], bank[u][(3, 0)[h % 2]][:, b * SEQ + c * P:(b + 1) * SEQ],
                                        eye_zero[:, 0:n], 0.0, ALU.mult, ALU.add)
                            last.then_inc(hgam_done, 1)
                        for u in U:
                            dve.wait_ge(hgam_done, upto(HEADS * i + h + 1, u))
                            dve.wait_ge(cb_done, upto(BATCHES * (i + 1), u))
                            if h >= 2:
                                dve.wait_ge(hy_mm, upto(HEADS * i + h - 1, u))
                            else:
                                dve.wait_ge(hy_mm, upto(HEADS * i, u))
                            for b in range(BATCHES):
                                for c in range(2):
                                    at = u * DT + (2 * b + c) * HEADS + h
                                    last = nc.vector.scalar_tensor_tensor(
                                        score[h % 2][u][:, strip(b, c)], cb[u][:, strip(b, c)], dt_dt[:, at:at + 1],
                                        hgam[h % 2][u][:, strip(b, c)], ALU.mult, ALU.mult)
                            last.then_inc(score_done, 1)
                        if h == 1:
                            normalise(it + 1, nxt)
                    for r in range(INNER_BLOCKS):
                        for u in U:
                            dve.wait_ge(hy_mm, upto(HEADS * i + 2 * r + 2, u))
                            dve.wait_ge(out_mm, upto(i, u))
                            dve.wait_ge(ysq_done, upto(INNER_BLOCKS * i, u))
                            dve.wait_ge(xbc_done, upto(CONV_BLOCKS * (i + 1), u))
                            nc.vector.scalar_tensor_tensor(yT[r][u], xbc[r][u], skip_col[:, r:r + 1], bank[u][1 + r][:, :],
                                                           ALU.mult, ALU.add).then_inc(ydt_done, 1)
                    for u in U:
                        dve.wait_ge(out_mm, upto(i + 1, u))
                        dve.wait_ge(rms_done, upto(i, u))
                        nc.vector.tensor_scalar(ms[u], bank[u][3][:, 0:GROUP_TILES], 1.0 / INNER, RMS_EPS,
                                                ALU.mult, ALU.add).then_inc(ms_done, 1)
                    for u in U:
                        dve.wait_ge(rms_done, upto(i + 1, u))
                        for t in range(GROUP_TILES):
                            xs = x_all[:, ds(i * PAIR_COLS + u * GROUP + t * P, P)]
                            last = nc.vector.scalar_tensor_tensor(xs, bank[u][0][:, cols(t)], rms[u][:, t:t + 1], xs,
                                                                  ALU.mult, ALU.add)
                        last.then_inc(x_done, 1)
            if stop_after > 3:
                ffn(1)

        @block.tensor
        def _(pe):
            mm = nc.tensor.matmul

            def transposes(k, dst):
                for u in U:
                    pe.wait_ge(xn_done, upto(k + 1, u))
                    for t in range(GROUP_TILES):
                        last = nc.tensor.transpose(bank[u][dst][:, cols(t)], xn[u][:, cols(t)], ident)
                    last.then_inc(tr_done, 1)

            for s in paced:
                pe.sem_inc(s, STREAMS)
            for s in (e_done, decay_done, back_mm):
                pe.sem_inc(s, 1)
            pe.wait_ge(weights_in, 16 * N_WEIGHT_DMAS)
            pe.wait_ge(consts_set, 4)
            transposes(0, 3)
            pe.wait_ge(ff_float, 1)
            for n in range(3):
                for k in range(FF_BLOCKS):
                    last = nc.tensor.transpose(bank[0][n][:, cols(k)], ff_raw[:, n, cols(k)], ident)
                last.then_inc(ffT_mm, 1)
            pe.wait_ge(ffT_done, 3)

            with pe.Fori(0, PAIRS) as i:
                for u in U:
                    pe.wait_ge(xnT_done, upto(i + 1, u))
                    pe.wait_ge(PT_done, upto(i, u))
                    for t in range(GROUP_TILES):
                        last = mm(bank[u][0][:, cols(t)], xnT[u][:, cols(t)], wk_sb[:, :], start=True, stop=True)
                    last.then_inc(k_mm, 1)
                for u in U:
                    pe.wait_ge(x_done, upto(i, u))
                    for t in range(GROUP_TILES):
                        last = mm(bank[u][1][:, cols(t)], xnT[u][:, cols(t)], wv_sb[:, :], start=True, stop=True)
                    last.then_inc(v_mm, 1)
                for u in U:
                    pe.wait_ge(og_done, upto(i, u))
                    for t in range(GROUP_TILES):
                        last = mm(bank[u][2][:, 2 * t:2 * t + 2], xnT[u][:, cols(t)], wab_sb[:, :], start=True, stop=True)
                    last.then_inc(ab_mm, 1)
                for u in U:
                    mm(bank[u][3][:, :], wq_sb[:, :], xnT[u][:, :], start=True, stop=True).then_inc(q_mm, 1)
                for u in U:
                    pe.wait_ge(ablog_done, upto(i + 1, u))
                    mm(bank[u][2][:, :], wg_sb[:, :], xnT[u][:, :], start=True, stop=True).then_inc(g_mm, 1)
                for u in U:
                    pe.wait_ge(ab_done, upto(i + 1, u))
                    pe.wait_ge(kb_done, upto(i + 1, u))
                    for t in range(GROUP_TILES):
                        last = nc.tensor.transpose(bank[u][0][:, cols(t)],
                                                   ab[u][:, 2 * t:2 * t + 1].broadcast_to([P, P]), ident)
                    last.then_inc(abc_mm, 1)
                for u in U:
                    pe.wait_ge(kn_done, upto(i + 1, u))
                    pe.wait_ge(v_done, upto(i + 1, u))
                    for t in range(GROUP_TILES):
                        last = nc.tensor.transpose(bank[u][1][:, cols(t)], kn[u][:, cols(t)], ident)
                    last.then_inc(kT_mm, 1)
                for u in U:
                    pe.wait_ge(kT_done, upto(i + 1, u))
                    pe.wait_ge(q_done, upto(i + 1, u))
                    pe.wait_ge(g_done, upto(i + 1, u))
                    for b in range(BATCHES):
                        for c in range(2):
                            last = mm(bank[u][2 + b][:, c * SEQ:c * SEQ + SEQ - c * P], kT[u][:, cols(2 * b + c)],
                                      kT[u][:, b * SEQ + c * P:(b + 1) * SEQ], start=True, stop=True)
                    last.then_inc(G_mm, 1)
                for level in range(LEVELS):
                    for u in U:
                        if level == 0:
                            pe.wait_ge(LT_done, upto(i + 1, u))
                        elif level == 1:
                            pe.wait_ge(W_done, upto(LEVELS * i + 1, u))
                        else:
                            pe.wait_ge(T_done, upto((LEVELS - 2) * i + level - 1, u))
                        for t in range(GROUP_TILES):
                            if level == 0:
                                last = nc.tensor.transpose(bank[u][1][:, cols(t)], LT[u][:, diag(t)], ident)
                            else:
                                last = mm(bank[u][1][:, cols(t)], LT[u][:, diag(t)], Tm[u][:, cols(t)], start=True, stop=True)
                        last.then_inc(Z_mm, 1)
                    for u in U:
                        pe.wait_ge(W_done, upto(LEVELS * i + level + 1, u))
                        if level == 0:
                            pe.wait_ge(gam_done, upto(i + 1, u))
                        else:
                            pe.wait_ge(R_done, upto(LEVELS * i + level, u))
                        if 0 < level < LEVELS - 1:
                            for t in range(GROUP_TILES):
                                last = mm(bank[u][2][:, cols(t)], Rm[u][:, cols(t)], Wm[u][:, cols(t)], start=True, stop=True)
                            last.then_inc(T_mm, 1)
                        for t in range(GROUP_TILES):
                            if level == 0:
                                last = nc.tensor.transpose(bank[u][0][:, cols(t)], Tm[u][:, cols(t)], ident)
                            else:
                                last = mm(bank[u][0][:, cols(t)], Wm[u][:, cols(t)], Rm[u][:, cols(t)], start=True, stop=True)
                        last.then_inc(R_mm, 1)
                for u in U:
                    pe.wait_ge(R_done, upto(LEVELS * (i + 1), u))
                    for b in range(BATCHES):
                        last = mm(bank[u][3][:, cols(b)], Rm[u][:, cols(2 * b)], vtok[u][:, cols(2 * b)], start=True, stop=True)
                    last.then_inc(w0_mm, 1)
                for u in U:
                    pe.wait_ge(w0_done, upto(i + 1, u))
                    for b in range(BATCHES):
                        last = mm(bank[u][2][:, cols(b)], LT[u][:, b * TRI + P:b * TRI + 2 * P], w0tok[u][:, cols(b)],
                                  start=True, stop=True)
                    last.then_inc(corr_mm, 1)
                for u in U:
                    pe.wait_ge(v1_done, upto(i + 1, u))
                    for t in range(GROUP_TILES):
                        last = mm(bank[u][1][:, cols(t)], vtok[u][:, cols(t)], Rm[u][:, cols(t)], start=True, stop=True)
                    last.then_inc(WT_mm, 1)
                for u in U:
                    pe.wait_ge(WT_done, upto(i + 1, u))
                    for b in range(BATCHES):
                        for c in range(2):
                            last = mm(bank[u][(0, 3)[b]][:, c * SEQ:c * SEQ + SEQ - c * P], WT[u][:, cols(2 * b + c)],
                                      qT[u][:, b * SEQ + c * P:(b + 1) * SEQ], start=True, stop=True)
                    last.then_inc(PT_mm, 1)
                for u in U:
                    pe.wait_ge(PT_done, upto(i + 1, u))
                    for b in range(BATCHES):
                        mm(bank[u][2][:, b * SEQ:(b + 1) * SEQ], kn[u][:, cols(2 * b)], PT[u][:, strip(b, 0)],
                           start=True, stop=False)
                        last = mm(bank[u][2][:, b * SEQ + P:(b + 1) * SEQ], kn[u][:, cols(2 * b + 1)], PT[u][:, strip(b, 1)],
                                  start=False, stop=True)
                    last.then_inc(OT_mm, 1)
                transposes(i + 1, 3)
                for u in U:
                    pe.wait_ge(og_done, upto(i + 1, u))
                    for t in range(GROUP_TILES):
                        last = mm(bank[u][1][:, cols(t)], og[u][:, cols(t)], wo_sb[:, :], start=True, stop=True)
                    last.then_inc(y_mm, 1)

            def ffn(run):
                phase = 2 * run + 1
                for u in U:
                    pe.wait_ge(x_done, upto(phase * PAIRS, u))
                with pe.Fori(0, PAIRS) as i:
                    it = phase * PAIRS + i
                    n = FF_BLOCKS * (i + PAIRS * run)
                    for j in range(FF_BLOCKS):
                        for u in U:
                            if j == 0:
                                pe.wait_ge(xnT_done, upto(it + 1, u))
                                pe.wait_ge(silu_done, upto(n, u))
                            elif j == 1:
                                pe.wait_ge(x_done, upto(it, u))
                            else:
                                pe.wait_ge(silu_done, upto(n + 1, u))
                            mm(bank[u][(1, 3, 1)[j]][:, :], gateT[:, cols(j)], xnT[u][:, :],
                               start=True, stop=True).then_inc(gate_mm, 1)
                            if j == 0:
                                pe.wait_ge(hid_done, upto(n, u))
                            elif j == 2:
                                pe.wait_ge(hid_done, upto(n + 1, u))
                            mm(bank[u][(2, 0, 2)[j]][:, :], upT[:, cols(j)], xnT[u][:, :],
                               start=True, stop=True).then_inc(up_mm, 1)
                    for u in U:
                        pe.wait_ge(hid_done, upto(n + 2, u))
                    transposes(it + 1, 0)
                    for u in U:
                        pe.wait_ge(hid_done, upto(n + FF_BLOCKS, u))
                        for t in range(GROUP_TILES):
                            for j in range(FF_BLOCKS):
                                last = mm(bank[u][3][:, cols(t)], hidT[u][:, j, cols(t)], downT[:, j, :],
                                          start=(j == 0), stop=(j == FF_BLOCKS - 1))
                        last.then_inc(down_mm, 1)

            if stop_after > 1:
                ffn(0)

            if stop_after > 2:
                for u in U:
                    pe.wait_ge(x_done, upto(2 * PAIRS, u))
                pe.wait_ge(prep_done, INNER_BLOCKS + 1)
                with pe.Fori(0, PAIRS) as i:
                    it = 2 * PAIRS + i
                    for u in U:
                        pe.wait_ge(xnT_done, upto(it + 1, u))
                        pe.wait_ge(ms_done, upto(i, u))
                        for t in range(GROUP_TILES):
                            last = mm(bank[u][3][:, t * HEADS:(t + 1) * HEADS], xnT[u][:, cols(t)],
                                      win_sb[:, PROJ - HEADS:PROJ], start=True, stop=True)
                        last.then_inc(dt_mm, 1)
                    for r in range(CONV_BLOCKS):
                        for u in U:
                            if r == 0:
                                pe.wait_ge(x_done, upto(it, u))
                            elif r == 3:
                                pe.wait_ge(tap_done, upto((TAPS - 1) * (CONV_BLOCKS * i + 1), u))
                            mm(bank[u][(0, 1, 2, 0)[r]][:, :], win_sb[:, INNER + r * P:INNER + (r + 1) * P], xnT[u][:, :],
                               start=True, stop=True).then_inc(conv_mm, 1)
                    pe.wait_ge(dt_step, (DT_STEPS + CS_STEPS) * i + DT_STEPS)
                    nc.tensor.transpose(bank[0][3][0:ROWS, 0:P], dA_dt[:, :], ident).then_inc(dAT_mm, 1)
                    for r in range(INNER_BLOCKS):
                        for u in U:
                            pe.wait_ge(tap_done, upto((TAPS - 1) * (CONV_BLOCKS * i + 2 + r), u))
                            mm(bank[u][1 + r][:, :], win_sb[:, cols(r)], xnT[u][:, :], start=True, stop=True).then_inc(z_mm, 1)
                    pe.wait_ge(dt_step, (DT_STEPS + CS_STEPS) * (i + 1))
                    nc.tensor.transpose(bank[1][3][:, 0:P], dstep[:, :], ident).then_inc(back_mm, 1)
                    for r in range(INNER_BLOCKS):
                        for u in U:
                            pe.wait_ge(xbc_done, upto(CONV_BLOCKS * i + r + 1, u))
                            if r == 0:
                                pe.wait_ge(decay_done, i + 2)
                            else:
                                pe.wait_ge(tap_done, upto((TAPS - 1) * CONV_BLOCKS * (i + 1), u))
                            for t in range(GROUP_TILES):
                                last = nc.tensor.transpose(bank[u][(3, 0)[r]][:, cols(t)], xbc[r][u][:, cols(t)], ident)
                            last.then_inc(xtok_mm, 1)
                    for b in range(BATCHES):
                        for u in U:
                            pe.wait_ge(xbc_done, upto(CONV_BLOCKS * (i + 1), u))
                            pe.wait_ge(sz_done, upto(INNER_BLOCKS * i + b + 1, u))
                            for c in range(2):
                                last = mm(bank[u][1 + b][:, c * SEQ:c * SEQ + SEQ - c * P], xbc[2][u][:, cols(2 * b + c)],
                                          xbc[3][u][:, b * SEQ + c * P:(b + 1) * SEQ], start=True, stop=True)
                            last.then_inc(cb_mm, 1)

                    def spread_decay(h):
                        for u in U:
                            pe.wait_ge(decay_done, i + 2)
                            if h < 2:
                                pe.wait_ge(xtok_done, upto(INNER_BLOCKS * i + h + 1, u))
                            else:
                                pe.wait_ge(hgam_done, upto(HEADS * i + h - 1, u))
                            for t in range(GROUP_TILES):
                                at = u * DT + t * HEADS + h
                                last = nc.tensor.transpose(bank[u][(3, 0)[h % 2]][:, cols(t)],
                                                           decay[:, at:at + 1].broadcast_to([P, P]), ident)
                            last.then_inc(habc_mm, 1)

                    spread_decay(0)
                    spread_decay(1)
                    for h in range(HEADS):
                        for u in U:
                            pe.wait_ge(score_done, upto(HEADS * i + h + 1, u))
                            pe.wait_ge(xtok_done, upto(INNER_BLOCKS * (i + 1), u))
                            pe.wait_ge(cb_done, upto(BATCHES * (i + 1), u))
                            half = (h % 2) * HEAD_DIM
                            xh = xtok[u].rearrange("p (t c) -> p t c", t=GROUP_TILES)[:, :, h * HEAD_DIM:(h + 1) * HEAD_DIM]
                            for b in range(BATCHES):
                                yh = bank[u][1 + h // 2][half:half + HEAD_DIM, :]
                                mm(yh[:, b * SEQ:(b + 1) * SEQ], xh[:, 2 * b, :], score[h % 2][u][:, strip(b, 0)],
                                   start=True, stop=False)
                                last = mm(yh[:, b * SEQ + P:(b + 1) * SEQ], xh[:, 2 * b + 1, :],
                                          score[h % 2][u][:, strip(b, 1)], start=False, stop=True)
                            last.then_inc(hy_mm, 1)
                        if h < 2:
                            spread_decay(h + 2)
                    for u in U:
                        pe.wait_ge(ydt_done, upto(INNER_BLOCKS * i + 1, u))
                    transposes(it + 1, 1)
                    for u in U:
                        pe.wait_ge(ysq_done, upto(INNER_BLOCKS * (i + 1), u))
                        pe.wait_ge(hgam_done, upto(HEADS * (i + 1), u))
                        for t in range(GROUP_TILES):
                            for r in range(INNER_BLOCKS):
                                mm(bank[u][3][:, t:t + 1], ysq[r][u][:, cols(t)], ones_col[:, :],
                                   start=(r == 0), stop=(r == INNER_BLOCKS - 1))
                        for t in range(GROUP_TILES):
                            for r in range(INNER_BLOCKS):
                                last = mm(bank[u][0][:, cols(t)], yT[r][u][:, cols(t)], wout_sb[:, r, :],
                                          start=(r == 0), stop=(r == INNER_BLOCKS - 1))
                        last.then_inc(out_mm, 1)
            if stop_after > 3:
                ffn(1)


_INS = ['L0_attn_a_x', 'L0_attn_a_Wq', 'L0_attn_a_bq', 'L0_attn_a_Wk', 'L0_attn_a_bk', 'L0_attn_a_Wv', 'L0_attn_a_bv',
        'L0_attn_a_Wa', 'L0_attn_a_ba', 'L0_attn_a_Wb', 'L0_attn_a_bb', 'L0_attn_a_Wg', 'L0_attn_a_bg', 'L0_attn_a_Wo',
        'L0_attn_a_bo', 'L0_attn_b_W_in', 'L0_attn_b_conv_w', 'L0_attn_b_conv_b', 'L0_attn_b_dt_bias', 'L0_attn_b_A_log',
        'L0_attn_b_D', 'L0_attn_b_norm_w', 'L0_attn_b_W_out', 'L0_ffn_w_gate', 'L0_ffn_w_up', 'L0_ffn_w_down']


def kernel(**inputs):
    import numpy as _np
    import concourse.bacc as _bacc
    from concourse import mybir as _mybir
    from concourse.bass_utils import run_bass_kernel_spmd as _run

    nc = _bacc.Bacc("TRN2", target_bir_lowering=False, num_devices=1)
    arrays, args = {}, []
    for name in _INS:
        a = _np.ascontiguousarray(inputs[name])
        arrays[f"in_{name}"] = a
        args.append(nc.dram_tensor(f"in_{name}", a.shape, _mybir.dt.from_np(a.dtype), kind="ExternalInput").ap())
    table = constants()
    arrays["in_tables"] = table
    args.append(nc.dram_tensor("in_tables", table.shape, _mybir.dt.float32, kind="ExternalInput").ap())
    out = nc.dram_tensor("out", (BATCH, SEQ, DIM), _mybir.dt.float32, kind="ExternalOutput").ap()
    build(nc, *args, out)
    r = _run(nc, [arrays], core_ids=[0])
    return r.results[0]["out"]
```

```python
import concourse.bass as bass
from concourse import mybir
from contextlib import ExitStack

BATCH, SEQ, DIM = 32, 256, 128
HIDDEN = 384
HEADS, HEAD_DIM, STATE = 4, 64, 128
INNER = HEADS * HEAD_DIM
TAPS = 4
CHUNK = 32
PROJ = 2 * INNER + 2 * STATE + HEADS
P = 128
TILES = BATCH * SEQ // P
GROUP_TILES = 4
GROUP = GROUP_TILES * P
STREAMS = 2
PAIRS = TILES // (GROUP_TILES * STREAMS)
PAIR_COLS = STREAMS * GROUP
BATCHES = GROUP // SEQ
TRI = SEQ + P
LEVELS = 7
FF_BLOCKS = HIDDEN // P
CONV_BLOCKS = (INNER + 2 * STATE) // P
INNER_BLOCKS = INNER // P
PHASES = 4
LN_EPS = 1e-5
RMS_EPS = 1e-5
DEQUANT = 1.0 / 127.0


def constants():
    import numpy as np

    r, c = np.arange(P)[:, None], np.arange(P)[None, :]
    eye = (r == c).astype(np.float32)
    parts = [eye, np.zeros((P, P), np.float32)]
    for level in range(LEVELS):
        n = 2 ** level
        below = (r // (2 * n) == c // (2 * n)) & (r % (2 * n) >= n) & (c % (2 * n) < n)
        parts.append(eye - below.astype(np.float32))
    parts.append(np.broadcast_to((c % CHUNK != 0).astype(np.float32), (P, P)))
    return np.ascontiguousarray(np.concatenate(parts, axis=1))


def build(nc, x_in, Wq, bq, Wk, bk, Wv, bv, Wa, ba, Wb, bb, Wg, bg, Wo, bo,
          W_in, conv_w, conv_b, dt_bias, A_log, D_skip, norm_w, W_out,
          w_gate, w_up, w_down, tables, out):
    f32, i32 = mybir.dt.float32, mybir.dt.int32
    ALU, ACT, AX = mybir.AluOpType, mybir.ActivationFunctionType, mybir.AxisListType
    ds = bass.ds

    ctx = ExitStack()
    with ctx:
        def sb(name, shape, dt=f32):
            return ctx.enter_context(nc.sbuf_tensor(name, shape, dt))

        def sem(name):
            return ctx.enter_context(nc.semaphore(name))

        def upto(n, u):
            return STREAMS * n + u + 1

        paced = []

        def pace(name):
            paced.append(sem(name))
            return paced[-1]

        x_all = sb("x_all", [P, TILES * DIM])
        tab = sb("tab", [P, (3 + LEVELS) * P])
        ident, eye_zero = tab[:, 0:P], tab[:, 0:2 * P]
        keep = tab[:, (2 + LEVELS) * P:(3 + LEVELS) * P]
        masks = [tab[:, (2 + k) * P:(3 + k) * P] for k in range(LEVELS)]
        half_neg = sb("half_neg", [P, GROUP_TILES])
        eps_cols = sb("eps_cols", [P, GROUP_TILES])
        ones_col = sb("ones_col", [P, 1])

        wq_sb, wg_sb, wo_sb = sb("wq_sb", [P, P]), sb("wg_sb", [P, P]), sb("wo_sb", [P, P])
        wk_sb, wv_sb = sb("wk_sb", [P, P]), sb("wv_sb", [P, P])
        wab_sb = sb("wab_sb", [P, 2])
        bq_col, bg_col = sb("bq_col", [P, 1]), sb("bg_col", [P, 1])
        bk_row, bv_row, bo_row = sb("bk_row", [P, P]), sb("bv_row", [P, P]), sb("bo_row", [P, P])
        bab_row = sb("bab_row", [P, 2])
        win_sb = sb("win_sb", [P, PROJ])
        wout_sb = sb("wout_sb", [P, INNER_BLOCKS, DIM])
        wout_raw = sb("wout_raw", [P, INNER_BLOCKS, DIM])
        convw_sb = sb("convw_sb", [P, CONV_BLOCKS, TAPS])
        convb_sb = sb("convb_sb", [P, CONV_BLOCKS])
        normw_col = sb("normw_col", [P, INNER_BLOCKS])
        skip_col = sb("skip_col", [P, INNER_BLOCKS])
        dtb_row = sb("dtb_row", [P, HEADS])
        alog_row = sb("alog_row", [P, HEADS])
        aexp_row = sb("aexp_row", [P, HEADS])
        aneg_row = sb("aneg_row", [P, HEADS])
        ff_int = sb("ff_int", [P, 3, HIDDEN], i32)
        ff_raw = sb("ff_raw", [P, 3, HIDDEN])
        gateT, upT = sb("gateT", [P, HIDDEN]), sb("upT", [P, HIDDEN])
        downT = sb("downT", [P, FF_BLOCKS, DIM])

        U = range(STREAMS)
        stats = [sb(f"stats{u}", [P, GROUP_TILES, 6]) for u in U]
        mv = [sb(f"mv{u}", [P, GROUP_TILES, 2]) for u in U]
        carrier = [sb(f"carrier{u}", [P, 1]) for u in U]
        var_eps = [sb(f"var_eps{u}", [P, GROUP_TILES]) for u in U]
        rstd = [sb(f"rstd{u}", [P, GROUP_TILES]) for u in U]
        xn = [sb(f"xn{u}", [P, GROUP]) for u in U]
        xnT = [sb(f"xnT{u}", [P, GROUP]) for u in U]
        ff = [sb(f"ff{u}", [P, 2 * FF_BLOCKS, GROUP]) for u in U]
        silu_g = [ff[u][:, 0:FF_BLOCKS, :] for u in U]
        hidT = [ff[u][:, FF_BLOCKS:, :] for u in U]
        assert LEVELS - 1 == 2 * FF_BLOCKS
        Wlev = [None] + [[ff[u][:, k, :] for u in U] for k in range(LEVELS - 1)]
        ARENA = 20 * GROUP + 64
        arena = [sb(f"arena{u}", [P, ARENA]) for u in U]

        def carver():
            at = [0]

            def carve(cols):
                a, at[0] = at[0], at[0] + cols
                assert at[0] <= ARENA, at[0]
                return [arena[u][:, a:a + cols] for u in U]
            return carve

        carve = carver()
        kb, ksq, kn, kT = carve(GROUP), carve(GROUP), carve(GROUP), carve(GROUP)
        vtok, qT, gT, xb = carve(GROUP), carve(GROUP), carve(GROUP), carve(GROUP)
        gam, LT, PT = carve(BATCHES * TRI), carve(BATCHES * TRI), carve(BATCHES * TRI)
        Tm, Rm, WT, og = carve(GROUP), carve(GROUP), carve(GROUP), carve(GROUP)
        w0tok = carve(BATCHES * P)
        ablog, ab = carve(2 * GROUP_TILES), carve(2 * GROUP_TILES)
        kss, kinv = carve(GROUP_TILES), carve(GROUP_TILES)
        carve = carver()
        xbc = [carve(GROUP) for _ in range(CONV_BLOCKS)]
        siluz = [carve(GROUP) for _ in range(INNER_BLOCKS)]
        xt = carve(GROUP_TILES * INNER)
        cb = carve(BATCHES * TRI)
        hgam = [carve(BATCHES * TRI) for _ in range(2)]
        score = [carve(BATCHES * TRI) for _ in range(2)]
        yT = [carve(GROUP) for _ in range(INNER_BLOCKS)]
        ysq = [carve(GROUP) for _ in range(INNER_BLOCKS)]
        ms, rms = carve(GROUP_TILES), carve(GROUP_TILES)
        DT = GROUP_TILES * HEADS
        ROWS = STREAMS * DT
        csum, dstep = sb("csum", [ROWS, P]), sb("dstep", [P, P])
        small = [sb(f"dt_{n}", [P, STREAMS * DT]) for n in
                 ("z", "nabs", "e", "den", "rec", "w", "w2", "acc", "relu", "dt", "dA", "decay")]
        z_dt, nabs_dt, e_dt, den_dt, rec_dt, w_dt, w2_dt, acc_dt, relu_dt, dt_dt, dA_dt, decay = small
        decay1 = sb("decay1", [P, DT])

        bank = [[ctx.enter_context(nc.psum_tensor(f"bank{u}_{k}", [P, GROUP], f32)) for k in range(4)]
                for u in U]

        first_x_in, second_x_in, rest_x_in, x_out = (sem(n) for n in ("first_x_in", "second_x_in", "rest_x_in", "x_out"))
        tables_in, attn_in, later_in = sem("tables_in"), sem("attn_in"), sem("later_in")
        consts_set, ff_float, ffT_mm, ffT_done, aexp_done, prep_done = (
            sem("consts_set"), sem("ff_float"), sem("ffT_mm"), sem("ffT_done"), sem("aexp_done"), sem("prep_done"))
        stats_done, mv_done, var_done, rstd_done, xn_done, tr_done, xnT_done, x_done = (
            pace(n) for n in ("stats_done", "mv_done", "var_done", "rstd_done", "xn_done", "tr_done", "xnT_done", "x_done"))
        gate_mm, up_mm, down_mm, silu_done, hid_done = (
            pace(n) for n in ("gate_mm", "up_mm", "down_mm", "silu_done", "hid_done"))
        k_mm, v_mm, ab_mm, q_mm, g_mm, kT_mm, abc_mm, G_mm, w0_mm, corr_mm, WT_mm, PT_mm, OT_mm, y_mm = (
            pace(n) for n in ("k_mm", "v_mm", "ab_mm", "q_mm", "g_mm", "kT_mm", "abc_mm", "G_mm",
                              "w0_mm", "corr_mm", "WT_mm", "PT_mm", "OT_mm", "y_mm"))
        kb_done, v_done, ablog_done, ab_done, q_done, g_done, ksq_done, kss_done, kmax_done, kinv_done, kn_done, kT_done = (
            pace(n) for n in ("kb_done", "v_done", "ablog_done", "ab_done", "q_done", "g_done", "ksq_done", "kss_done",
                              "kmax_done", "kinv_done", "kn_done", "kT_done"))
        gam_done, LTraw_done, LT_done, w0_done, v1_done, WT_done, PT_done, og_done, xb_done = (
            pace(n) for n in ("gam_done", "LTraw_done", "LT_done", "w0_done", "v1_done",
                              "WT_done", "PT_done", "og_done", "xb_done"))
        ms_mm, out_mm, ms_done, rms_done = (pace(n) for n in ("ms_mm", "out_mm", "ms_done", "rms_done"))
        Z_mm, T_mm, R_mm, W_done, T_done, R_done = ([sem(f"{n}{u}") for u in U] for n in
                                                    ("Z_mm", "T_mm", "R_mm", "W_done", "T_done", "R_done"))
        conv_mm, z_mm, xtok_mm, cb_mm, habc_mm, hy_mm = ([sem(f"{n}{u}") for u in U] for n in (
            "conv_mm", "z_mm", "xtok_mm", "cb_mm", "habc_mm", "hy_mm"))
        conv_init, tap_done, xbc_done, sz_done, xt_done, cb_done = ([sem(f"{n}{u}") for u in U] for n in (
            "conv_init", "tap_done", "xbc_done", "sz_done", "xt_done", "cb_done"))
        hgam_done, score_done, ydt_done, yT_done, ysq_done = ([sem(f"{n}{u}") for u in U] for n in (
            "hgam_done", "score_done", "ydt_done", "yT_done", "ysq_done"))
        per_stream = (Z_mm, T_mm, R_mm, W_done, T_done, R_done, conv_mm, z_mm, xtok_mm, cb_mm, habc_mm, hy_mm, conv_init,
                      tap_done, xbc_done, sz_done, xt_done, cb_done, hgam_done, score_done, ydt_done, yT_done, ysq_done)
        W_set, dt_step = [sem(f"W_set{u}") for u in U], sem("dt_step")
        per_pair = dt_mm, e_done, decay_done, decay1_done, dAT_mm, back_mm = [
            sem(n) for n in ("dt_mm", "e_done", "decay_done", "decay1_done", "dAT_mm", "back_mm")]
        ATTN_DMAS = 14
        LATER_DMAS = 8 + CONV_BLOCKS + INNER_BLOCKS + HEADS

        def tile4(ap):
            return ap.rearrange("p (t c) -> p t c", t=GROUP_TILES)

        def cols(k):
            return slice(k * P, (k + 1) * P)

        def strip(b, c):
            a = b * TRI + c * SEQ
            return slice(a, a + SEQ - c * P)

        def diag(t):
            a = (t // 2) * TRI + (t % 2) * SEQ
            return slice(a, a + P)

        def halves(ap, level, which):
            return ap.rearrange("p (q s n) -> p q s n", s=2, n=2 ** level)[:, :, which, :]

        def packed(ap, level):
            return ap.rearrange("p (q n) -> p q n", n=2 ** level)

        def half_cols(t):
            return slice(t * P // 2, (t + 1) * P // 2)

        def nth(n):
            return n + 1

        def taps_upto(i, r, s):
            return TAPS_ALL * i + 2 * (TAPS - 1) * (r // 2) + 2 * (s - 1) + r % 2 + 1

        def group_cols(pair, u):
            return ds(pair * PAIR_COLS + u * GROUP, GROUP)

        SERIES = [1.0 / n for n in range(13, 2, -2)]
        TAPS_ALL = (TAPS - 1) * CONV_BLOCKS
        DT_STEPS = 2 + 6 + len(SERIES) + 3
        CS_STEPS = 3

        def dt_steps(i, n):
            return (DT_STEPS + CS_STEPS) * i + n

        block = ctx.enter_context(nc.Block())

        @block.sync
        def _(sp):
            x_tok = x_in.rearrange("b (c p) d -> p (b c) d", p=P)
            x_sb = x_all[:, :].rearrange("p (n d) -> p n d", d=DIM)
            step = GROUP_TILES * STREAMS
            for u in U:
                group = slice(u * GROUP_TILES, (u + 1) * GROUP_TILES)
                sp.dma_start(x_sb[:, group, :], x_tok[:, group, :]).then_inc(first_x_in, 16)
            sp.dma_start(tab[:, :], tables).then_inc(tables_in, 16)

            def load(dst, src, loaded):
                sp.dma_start(dst, src).then_inc(loaded, 16)

            def column(v):
                return v.rearrange("(p a) -> p a", a=1)

            def row(v):
                return v.rearrange("(a n) -> a n", a=1).partition_broadcast(P)[:, 0, :]

            load(wk_sb[:, :], Wk, attn_in)
            load(wab_sb[:, 0:1], Wa, attn_in)
            load(wab_sb[:, 1:2], Wb, attn_in)
            for dst, src in ((bab_row[:, 0:1], ba), (bab_row[:, 1:2], bb), (bk_row[:, :], bk), (bv_row[:, :], bv)):
                load(dst, row(src), attn_in)
            load(wv_sb[:, :], Wv, attn_in)
            load(wq_sb[:, :], Wq, attn_in)
            load(bq_col[:, :], column(bq), attn_in)
            load(wg_sb[:, :], Wg, attn_in)
            load(bg_col[:, :], column(bg), attn_in)
            load(wo_sb[:, :], Wo, attn_in)
            load(bo_row[:, :], row(bo), attn_in)
            for k in range(1, PAIRS):
                sp.dma_start(x_sb[:, k * step:(k + 1) * step, :],
                             x_tok[:, k * step:(k + 1) * step, :]).then_inc(second_x_in if k == 1 else rest_x_in, 16)
            load(ff_int[:, 0, :].rearrange("p (k d) -> p k d", d=DIM), w_gate.rearrange("(k p) d -> p k d", p=P), later_in)
            load(ff_int[:, 1, :].rearrange("p (k d) -> p k d", d=DIM), w_up.rearrange("(k p) d -> p k d", p=P), later_in)
            load(ff_int[:, 2, :], w_down, later_in)
            load(win_sb[:, :], W_in, later_in)
            load(wout_raw[:, :, :], W_out.rearrange("(k p) d -> p k d", p=P), later_in)
            load(convw_sb[:, :, :], conv_w.rearrange("(k p) t -> p k t", p=P), later_in)
            for k in range(CONV_BLOCKS):
                load(convb_sb[:, k:k + 1], column(conv_b[k * P:(k + 1) * P]), later_in)
            for k in range(INNER_BLOCKS):
                load(normw_col[:, k:k + 1], column(norm_w[k * P:(k + 1) * P]), later_in)
            load(dtb_row[:, :], row(dt_bias), later_in)
            load(alog_row[:, :], row(A_log), later_in)
            for h in range(HEADS):
                half = (h % 2) * HEAD_DIM
                load(skip_col[half:half + HEAD_DIM, h // 2:h // 2 + 1],
                     D_skip[h:h + 1].rearrange("(a n) -> a n", a=1).partition_broadcast(HEAD_DIM)[:, 0, :], later_in)
            out_tok = out.rearrange("b (c p) d -> p (b c) d", p=P)
            for k in range(PAIRS):
                for u in U:
                    sp.wait_ge(x_done, upto((PHASES - 1) * PAIRS + k + 1, u))
                sp.dma_start(out_tok[:, k * step:(k + 1) * step, :],
                             x_sb[:, k * step:(k + 1) * step, :]).then_inc(x_out, 16)
            sp.wait_ge(x_out, 16 * PAIRS)

        @block.gpsimd
        def _(pool):
            nc.gpsimd.memset(half_neg[:, :], -0.5).then_inc(consts_set, 1)
            nc.gpsimd.memset(eps_cols[:, :], LN_EPS).then_inc(consts_set, 1)
            nc.gpsimd.memset(ones_col[:, :], 1.0).then_inc(consts_set, 1)
            nc.gpsimd.memset(dstep[:, :], 0.0).then_inc(consts_set, 1)
            pool.wait_ge(consts_set, 4)

            def ln_rstd(k, u):
                pool.wait_ge(mv_done, upto(k + 1, u))
                nc.gpsimd.tensor_tensor(var_eps[u][:, :], mv[u][:, :, 1], eps_cols[:, :], ALU.add).then_inc(var_done, 1)
                pool.wait_ge(var_done, upto(k + 1, u))
                nc.gpsimd.tensor_tensor(rstd[u][:, :], var_eps[u][:, :], half_neg[:, :], ALU.pow).then_inc(rstd_done, 1)

            def attention_half(u, iu, v, ib, jf):
                if ib is not None:
                    pool.wait_ge(rest_x_in, 16 * (PAIRS - 2))
                    pool.wait_ge(second_x_in, 16)
                    pool.wait_ge(first_x_in, 16 * STREAMS)
                    pool.wait_ge(xb_done, upto(ib, v))
                    pool.wait_ge(x_done, upto(ib, v))
                    nc.gpsimd.tensor_tensor(tile4(xb[v]), tile4(x_all[:, group_cols(ib, v)]),
                                            bo_row[:, :].unsqueeze(1).broadcast_to([P, GROUP_TILES, P]),
                                            ALU.add).then_inc(xb_done, 1)
                if iu is not None:
                    ln_rstd(iu + 1, u)
                if jf is not None:
                    pool.wait_ge(kmax_done, upto(jf + 1, v))
                    nc.gpsimd.tensor_tensor(kinv[v], kss[v], half_neg[:, :], ALU.pow).then_inc(kinv_done, 1)
                    pool.wait_ge(consts_set, 4)
                    pool.wait_ge(LTraw_done, upto(jf + 1, v))
                    for b in range(BATCHES):
                        square = LT[v][:, b * TRI:(b + 1) * TRI].rearrange("p (s c) -> p s c", c=P)[:, 0:3:2, :]
                        last = nc.gpsimd.affine_select(out=square, in_=square, compare_op=ALU.not_equal, fill=1.0, base=0,
                                                       pattern=[[0, 2], [-1, P]], channel_multiplier=1)
                    last.then_inc(LT_done, 1)

            for u in U:
                ln_rstd(0, u)
            pool.wait_ge(attn_in, 16 * ATTN_DMAS)
            attention_half(None, None, 0, None, 0)
            attention_half(0, 0, 1, None, 0)
            with pool.Fori(0, PAIRS - 1) as i:
                attention_half(1, i, 0, i, i + 1)
                attention_half(0, i + 1, 1, i, i + 1)
            attention_half(1, PAIRS - 1, 0, PAIRS - 1, None)
            attention_half(None, None, 1, PAIRS - 1, None)
            with pool.Fori(0, PAIRS) as i:
                for u in U:
                    ln_rstd(PAIRS + i + 1, u)
            def space_half(u, iu, v, jf):
                if u is not None:
                    for h in range(HEADS):
                        pool.wait_ge(hgam_done[u], nth(HEADS * iu + h + 1))
                        pool.wait_ge(cb_done[u], nth(BATCHES * (iu + 1)))
                        pool.wait_ge(hy_mm[u], nth(HEADS * iu + (h - 1 if h >= 2 else 0)))
                        nc.gpsimd.tensor_tensor(score[h % 2][u], cb[u], hgam[h % 2][u], ALU.mult).then_inc(score_done[u], 1)
                    for r in range(INNER_BLOCKS):
                        pool.wait_ge(ydt_done[u], nth(INNER_BLOCKS * iu + r + 1))
                        pool.wait_ge(sz_done[u], nth(INNER_BLOCKS * (iu + 1)))
                        nc.gpsimd.tensor_tensor(yT[r][u], yT[r][u], siluz[r][u], ALU.mult).then_inc(yT_done[u], 1)
                if v is not None:
                    ln_rstd(2 * PAIRS + jf + 1, v)
                if u is not None:
                    pool.wait_ge(ms_done, upto(iu + 1, u))
                    nc.gpsimd.tensor_tensor(rms[u], ms[u], half_neg[:, :], ALU.pow).then_inc(rms_done, 1)

            space_half(None, None, 0, 0)
            space_half(0, 0, 1, 0)
            with pool.Fori(0, PAIRS - 1) as i:
                space_half(1, i, 0, i + 1)
                space_half(0, i + 1, 1, i + 1)
            space_half(1, PAIRS - 1, None, None)
            with pool.Fori(0, PAIRS) as i:
                for u in U:
                    ln_rstd(3 * PAIRS + i + 1, u)

        @block.scalar
        def _(act):
            def feature_major(k, u, src):
                act.wait_ge(tr_done, upto(k + 1, u))
                nc.scalar.activation(xnT[u][:, :], bank[u][src][:, :], ACT.Copy).then_inc(xnT_done, 1)

            def inverse_level(u, i, level):
                if 0 < level < LEVELS - 1:
                    act.wait_ge(T_mm[u], nth((LEVELS - 2) * i + level))
                    nc.scalar.activation(halves(Tm[u], level, 0), packed(bank[u][2][:, 0:GROUP // 2], level),
                                         ACT.Copy).then_inc(T_done[u], 1)
                act.wait_ge(R_mm[u], nth(LEVELS * i + level + 1))
                if level == 0:
                    nc.scalar.activation(Rm[u], bank[u][0][:, :], ACT.Copy).then_inc(R_done[u], 1)
                else:
                    nc.scalar.activation(halves(Rm[u], level, 1), packed(bank[u][0][:, 0:GROUP // 2], level),
                                         ACT.Copy).then_inc(R_done[u], 1)

            def attention_half(u, iu, v, ib, jf):
                inverse, end, begin = iu is not None, ib is not None, jf is not None
                if end:
                    act.wait_ge(w0_mm, upto(ib + 1, v))
                    nc.scalar.activation(w0tok[v], bank[v][3][:, 0:BATCHES * P], ACT.Copy).then_inc(w0_done, 1)
                if inverse:
                    inverse_level(u, iu, 0)
                if end:
                    act.wait_ge(WT_mm, upto(ib + 1, v))
                    nc.scalar.activation(WT[v], bank[v][1][:, :], ACT.Copy).then_inc(WT_done, 1)
                if inverse:
                    inverse_level(u, iu, 1)
                if end:
                    feature_major(ib + 1, v, 2)
                if inverse:
                    inverse_level(u, iu, 2)
                if begin:
                    act.wait_ge(ablog_done, upto(jf + 1, v))
                    act.wait_ge(PT_done, upto(jf, v))
                    nc.scalar.activation(ab[v], ablog[v], ACT.Sigmoid).then_inc(ab_done, 1)
                    act.wait_ge(kb_done, upto(jf + 1, v))
                    nc.scalar.activation(ksq[v], kb[v], ACT.Square).then_inc(ksq_done, 1)
                if inverse:
                    inverse_level(u, iu, 3)
                if begin:
                    act.wait_ge(q_mm, upto(jf + 1, v))
                    act.wait_ge(PT_mm, upto(jf, v))
                    nc.scalar.activation(qT[v], bank[v][3][:, :], ACT.Identity, bias=bq_col[:, :]).then_inc(q_done, 1)
                    act.wait_ge(kT_mm, upto(jf + 1, v))
                    nc.scalar.activation(kT[v], bank[v][1][:, :], ACT.Copy).then_inc(kT_done, 1)
                if inverse:
                    inverse_level(u, iu, 4)
                if begin:
                    act.wait_ge(g_mm, upto(jf + 1, v))
                    act.wait_ge(og_done, upto(jf, v))
                    nc.scalar.activation(gT[v], bank[v][1][:, :], ACT.Sigmoid, bias=bg_col[:, :]).then_inc(g_done, 1)
                if inverse:
                    inverse_level(u, iu, 5)
                    inverse_level(u, iu, 6)

            act.wait_ge(tables_in, 16)
            nc.scalar.activation(ff[0][:, :, :].rearrange("p k (t c) -> p (k t) c", c=P),
                                 ident.unsqueeze(1).broadcast_to([P, 2 * FF_BLOCKS * GROUP_TILES, P]),
                                 ACT.Copy).then_inc(W_set[0], 1)
            for u in U:
                feature_major(0, u, 3)
            act.wait_ge(attn_in, 16 * ATTN_DMAS)
            attention_half(None, None, 0, None, 0)
            attention_half(0, 0, 1, None, 0)
            with act.Fori(0, PAIRS - 1) as i:
                attention_half(1, i, 0, i, i + 1)
                attention_half(0, i + 1, 1, i, i + 1)
            attention_half(1, PAIRS - 1, 0, PAIRS - 1, None)
            for n, dst in enumerate((gateT[:, :], upT[:, :], downT[:, :, :].rearrange("p k d -> p (k d)"))):
                act.wait_ge(ffT_mm, n + 1)
                nc.scalar.activation(dst, bank[0][1 + n][:, 0:HIDDEN], ACT.Copy).then_inc(ffT_done, 1)
            attention_half(None, None, 1, PAIRS - 1, None)

            def ffn(run):
                with act.Fori(0, PAIRS) as i:
                    n = FF_BLOCKS * (i + PAIRS * run)
                    for j in range(FF_BLOCKS):
                        for u in U:
                            act.wait_ge(gate_mm, upto(n + j + 1, u))
                            act.wait_ge(hid_done, upto(n, u))
                            nc.scalar.activation(silu_g[u][:, j, :], bank[u][(1, 3, 1)[j]][:, :], ACT.Silu,
                                                 scale=DEQUANT).then_inc(silu_done, 1)
                    for u in U:
                        act.wait_ge(up_mm, upto(n + FF_BLOCKS, u))
                    for u in U:
                        feature_major((2 * run + 1) * PAIRS + i + 1, u, 0)

            act.wait_ge(later_in, 16 * LATER_DMAS)
            nc.scalar.activation(aexp_row[:, :], alog_row[:, :], ACT.Exp).then_inc(aexp_done, 1)
            ffn(0)

            def space_half(u, iu, v, jf):
                end, begin = u is not None, v is not None

                def first_tap(r):
                    act.wait_ge(conv_mm[v], nth(CONV_BLOCKS * jf + r + 1))
                    act.wait_ge(ydt_done[v], nth(INNER_BLOCKS * jf))
                    nc.scalar.activation(xbc[r][v], bank[v][(0, 3, 1, 0)[r]][:, :], ACT.Identity,
                                         scale=convw_sb[:, r, TAPS - 1:TAPS],
                                         bias=convb_sb[:, r:r + 1]).then_inc(conv_init[v], 1)

                def silu_x(r):
                    act.wait_ge(tap_done[v], nth(taps_upto(jf, r, TAPS - 1)))
                    nc.scalar.activation(xbc[r][v], xbc[r][v], ACT.Silu).then_inc(xbc_done[v], 1)

                def silu_z(r):
                    act.wait_ge(z_mm[v], nth(INNER_BLOCKS * jf + r + 1))
                    act.wait_ge(yT_done[v], nth(INNER_BLOCKS * jf))
                    nc.scalar.activation(siluz[r][v], bank[v][(3, 1)[r]][:, :], ACT.Silu).then_inc(sz_done[v], 1)

                def square_y(r):
                    act.wait_ge(yT_done[u], nth(INNER_BLOCKS * iu + r + 1))
                    act.wait_ge(out_mm, upto(iu, u))
                    nc.scalar.activation(ysq[r][u], yT[r][u], ACT.Square).then_inc(ysq_done[u], 1)

                if begin and v == 0:
                    act.wait_ge(dt_step, dt_steps(jf, 2))
                    nc.scalar.activation(e_dt[:, :], nabs_dt[:, :], ACT.Exp).then_inc(e_done, 1)
                if begin:
                    first_tap(0)
                    first_tap(1)
                    first_tap(2)
                if begin and v == 0:
                    act.wait_ge(back_mm, nth(jf + 1))
                    act.wait_ge(habc_mm[0], nth(HEADS * jf))
                    act.wait_ge(decay1_done, nth(jf))
                    nc.scalar.activation(decay[:, :], bank[0][2][:, 0:ROWS], ACT.Exp).then_inc(decay_done, 1)
                elif begin:
                    act.wait_ge(decay_done, nth(jf + 1))
                    act.wait_ge(habc_mm[v], nth(HEADS * jf))
                    nc.scalar.activation(decay1[:, :], decay[:, DT:2 * DT], ACT.Copy).then_inc(decay1_done, 1)
                if begin:
                    silu_x(0)
                if end:
                    square_y(0)
                if begin:
                    silu_x(1)
                    first_tap(3)
                if end:
                    square_y(1)
                if begin:
                    silu_z(0)
                    silu_x(2)
                    silu_x(3)
                    silu_z(1)
                    feature_major(2 * PAIRS + jf + 1, v, 0)
                    for b in range(BATCHES):
                        act.wait_ge(cb_mm[v], nth(BATCHES * jf + b + 1))
                        act.wait_ge(score_done[v], nth(HEADS * jf))
                        nc.scalar.activation(cb[v][:, b * TRI:(b + 1) * TRI], bank[v][1 + b][:, 0:TRI],
                                             ACT.Copy).then_inc(cb_done[v], 1)

            space_half(None, None, 0, 0)
            space_half(0, 0, 1, 0)
            with act.Fori(0, PAIRS - 1) as i:
                space_half(1, i, 0, i + 1)
                space_half(0, i + 1, 1, i + 1)
            space_half(1, PAIRS - 1, None, None)
            ffn(1)

        @block.vector
        def _(dve):
            def stats_of(k, u, pair):
                if not isinstance(k, int) or k >= PAIRS:
                    dve.wait_ge(x_done, upto(k - 1, u))
                for t in range(GROUP_TILES):
                    last = nc.vector.bn_stats(stats[u][:, t, :], x_all[:, ds(pair * PAIR_COLS + u * GROUP + t * P, P)])
                last.then_inc(stats_done, 1)
                dve.wait_ge(stats_done, upto(k + 1, u))
                nc.vector.memset(carrier[u][:, :], 0.0)
                for t in range(GROUP_TILES):
                    last = nc.vector.bn_aggr(mv[u][:, t, :], stats[u][:, t, :])
                last.then_inc(mv_done, 1)

            def normalise(k, u, pair):
                dve.wait_ge(rstd_done, upto(k + 1, u))
                dve.wait_ge(tr_done, upto(k, u))
                for t in range(GROUP_TILES):
                    last = nc.vector.tensor_scalar(xn[u][:, cols(t)],
                                                   x_all[:, ds(pair * PAIR_COLS + u * GROUP + t * P, P)],
                                                   mv[u][:, t, 0:1], rstd[u][:, t:t + 1], ALU.subtract, ALU.mult)
                last.then_inc(xn_done, 1)

            dve.wait_ge(first_x_in, 16 * STREAMS)
            for u in U:
                stats_of(0, u, 0)
            for u in U:
                normalise(0, u, 0)
            dve.wait_ge(tables_in, 16)
            nc.vector.tensor_copy(ff[1][:, :, :].rearrange("p k (t c) -> p (k t) c", c=P),
                                  ident.unsqueeze(1).broadcast_to([P, 2 * FF_BLOCKS * GROUP_TILES, P])).then_inc(W_set[1], 1)
            dve.wait_ge(consts_set, 4)
            dve.wait_ge(attn_in, 16 * ATTN_DMAS)

            def per_tile(ap):
                return ap.unsqueeze(1).broadcast_to([P, GROUP_TILES, ap.shape[-1]])

            def masked(u, i, level):
                dve.wait_ge(Z_mm[u], nth(LEVELS * i + level + 1))
                dve.wait_ge(R_mm[u], nth(LEVELS * i))
                if level == 0:
                    nc.vector.tensor_tensor(tile4(Tm[u]), tile4(bank[u][1][:, :]), per_tile(masks[0]),
                                            ALU.mult).then_inc(W_done[u], 1)
                else:
                    n = 2 ** level
                    nc.vector.tensor_tensor(
                        halves(Wlev[level][u], level, 0).rearrange("p (t q) n -> p t q n", t=GROUP_TILES),
                        bank[u][1][:, 0:GROUP // 2].rearrange("p (t q n) -> p t q n", t=GROUP_TILES, n=n),
                        halves(masks[level], level, 0).unsqueeze(1).broadcast_to([P, GROUP_TILES, P // (2 * n), n]),
                        ALU.mult).then_inc(W_done[u], 1)

            def gated(dst, u, banks):
                for b in range(BATCHES):
                    for c in range(2):
                        last = nc.vector.scalar_tensor_tensor(
                            dst[u][:, strip(b, c)], bank[u][banks[b]][:, c * SEQ:c * SEQ + SEQ - c * P],
                            tile4(ab[u])[:, 2 * b + c, 1:2], gam[u][:, strip(b, c)], ALU.mult, ALU.mult)
                return last

            def attention_half(u, iu, v, ib, jf):
                inverse, end, begin = iu is not None, ib is not None, jf is not None
                if inverse:
                    masked(u, iu, 0)
                if end:
                    dve.wait_ge(corr_mm, upto(ib + 1, v))
                    second = tile4(vtok[v])[:, 1:GROUP_TILES:2, :]
                    nc.vector.tensor_tensor(second, second,
                                            bank[v][2][:, 0:BATCHES * P].rearrange("p (b c) -> p b c", c=P),
                                            ALU.subtract).then_inc(v1_done, 1)
                if inverse:
                    masked(u, iu, 1)
                    nxt = (iu + 1) % PAIRS
                    stats_of(iu + 1, u, nxt)
                    masked(u, iu, 2)
                if end:
                    dve.wait_ge(PT_mm, upto(ib + 1, v))
                    dve.wait_ge(OT_mm, upto(ib, v))
                    gated(PT, v, (0, 3)).then_inc(PT_done, 1)
                if begin:
                    dve.wait_ge(ab_mm, upto(jf + 1, v))
                    nc.vector.tensor_tensor(tile4(ablog[v]), tile4(bank[v][2][:, 0:2 * GROUP_TILES]),
                                            per_tile(bab_row[:, :]), ALU.add).then_inc(ablog_done, 1)
                    dve.wait_ge(k_mm, upto(jf + 1, v))
                    nc.vector.tensor_tensor(tile4(kb[v]), tile4(bank[v][0][:, :]), per_tile(bk_row[:, :]),
                                            ALU.add).then_inc(kb_done, 1)
                if inverse:
                    masked(u, iu, 3)
                if begin:
                    dve.wait_ge(v_mm, upto(jf + 1, v))
                    dve.wait_ge(WT_mm, upto(jf, v))
                    nc.vector.tensor_tensor(tile4(vtok[v]), tile4(bank[v][1][:, :]), per_tile(bv_row[:, :]),
                                            ALU.add).then_inc(v_done, 1)
                    dve.wait_ge(ksq_done, upto(jf + 1, v))
                    nc.vector.tensor_reduce(kss[v], tile4(ksq[v]), AX.X, ALU.add).then_inc(kss_done, 1)
                    dve.wait_ge(kss_done, upto(jf + 1, v))
                    nc.vector.tensor_scalar(kss[v], kss[v], 1e-24, None, ALU.max).then_inc(kmax_done, 1)
                if end:
                    dve.wait_ge(OT_mm, upto(ib + 1, v))
                    dve.wait_ge(y_mm, upto(ib, v))
                    nc.vector.tensor_tensor(og[v], bank[v][2][:, :], gT[v], ALU.mult).then_inc(og_done, 1)
                if begin:
                    dve.wait_ge(kinv_done, upto(jf + 1, v))
                    dve.wait_ge(OT_mm, upto(jf, v))
                    nc.vector.tensor_tensor(tile4(kn[v]), tile4(kb[v]),
                                            kinv[v].unsqueeze(2).broadcast_to([P, GROUP_TILES, P]),
                                            ALU.mult).then_inc(kn_done, 1)
                if inverse:
                    masked(u, iu, 4)
                if begin:
                    dve.wait_ge(abc_mm, upto(jf + 1, v))
                    for b in range(BATCHES):
                        for c in range(2):
                            last = nc.vector.tensor_tensor_scan(
                                gam[v][:, strip(b, c)], bank[v][0][:, b * SEQ + c * P:(b + 1) * SEQ],
                                eye_zero[:, 0:SEQ - c * P], 0.0, ALU.mult, ALU.add)
                    last.then_inc(gam_done, 1)
                if inverse:
                    normalise(iu + 1, u, nxt)
                    masked(u, iu, 5)
                if begin:
                    dve.wait_ge(gam_done, upto(jf + 1, v))
                    dve.wait_ge(G_mm, upto(jf + 1, v))
                    dve.wait_ge(corr_mm, upto(jf, v))
                    gated(LT, v, (2, 3)).then_inc(LTraw_done, 1)
                if inverse:
                    masked(u, iu, 6)
                if end:
                    dve.wait_ge(y_mm, upto(ib + 1, v))
                    dve.wait_ge(xb_done, upto(ib + 1, v))
                    nc.vector.tensor_tensor(x_all[:, group_cols(ib, v)], bank[v][0][:, :], xb[v],
                                            ALU.add).then_inc(x_done, 1)

            attention_half(None, None, 0, None, 0)
            dve.wait_ge(W_set[0], 1)
            dve.wait_ge(second_x_in, 16)
            attention_half(0, 0, 1, None, 0)
            dve.wait_ge(W_set[1], 1)
            dve.wait_ge(rest_x_in, 16 * (PAIRS - 2))
            with dve.Fori(0, PAIRS - 1) as i:
                attention_half(1, i, 0, i, i + 1)
                attention_half(0, i + 1, 1, i, i + 1)
            dve.wait_ge(later_in, 16 * LATER_DMAS)
            nc.vector.tensor_copy(ff_raw[:, :, :], ff_int[:, :, :]).then_inc(ff_float, 1)
            for k in range(INNER_BLOCKS):
                nc.vector.tensor_scalar(wout_sb[:, k, :], wout_raw[:, k, :], normw_col[:, k:k + 1], None,
                                        ALU.mult).then_inc(prep_done, 1)
            attention_half(1, PAIRS - 1, 0, PAIRS - 1, None)
            attention_half(None, None, 1, PAIRS - 1, None)

            def ffn(run):
                phase = 2 * run + 1
                with dve.Fori(0, PAIRS) as i:
                    nxt = (i + 1) % PAIRS
                    it = phase * PAIRS + i
                    n = FF_BLOCKS * (i + PAIRS * run)
                    for j in range(FF_BLOCKS):
                        for u in U:
                            dve.wait_ge(silu_done, upto(n + j + 1, u))
                            dve.wait_ge(up_mm, upto(n + j + 1, u))
                            dve.wait_ge(down_mm, upto(i + PAIRS * run, u))
                            nc.vector.scalar_tensor_tensor(hidT[u][:, j, :], bank[u][(2, 0, 2)[j]][:, :], DEQUANT,
                                                           silu_g[u][:, j, :], ALU.mult, ALU.mult).then_inc(hid_done, 1)
                        if j == 0:
                            for u in U:
                                stats_of(it + 1, u, nxt)
                        if j == 1:
                            for u in U:
                                normalise(it + 1, u, nxt)
                    for u in U:
                        dve.wait_ge(down_mm, upto(i + PAIRS * run + 1, u))
                        nc.vector.scalar_tensor_tensor(x_all[:, group_cols(i, u)], bank[u][3][:, :], DEQUANT,
                                                       x_all[:, group_cols(i, u)], ALU.mult, ALU.add).then_inc(x_done, 1)

            dve.wait_ge(aexp_done, 1)
            nc.vector.tensor_scalar(aneg_row[:, :], aexp_row[:, :], -1.0, None, ALU.mult).then_inc(prep_done, 1)
            ffn(0)

            def space_half(u, iu, v, jf):
                end, begin, pair_dt = u is not None, v is not None, v == 0
                taken = [0]

                def step(ins):
                    taken[0] += 1
                    ins.then_inc(dt_step, 1)

                def prior():
                    dve.wait_ge(dt_step, dt_steps(jf, taken[0]))

                def taps(s, *blocks):
                    for q in blocks:
                        if s == 1:
                            dve.wait_ge(conv_init[v], nth(CONV_BLOCKS * jf + q + 1))
                        else:
                            dve.wait_ge(tap_done[v], nth(taps_upto(jf, q, s - 1)))
                        src = bank[v][(0, 3, 1, 0)[q]][:, :].rearrange("p (b t) -> p b t", t=SEQ)[:, :, 0:SEQ - s]
                        acc = xbc[q][v].rearrange("p (b t) -> p b t", t=SEQ)[:, :, s:SEQ]
                        nc.vector.scalar_tensor_tensor(acc, src, convw_sb[:, q, TAPS - 1 - s:TAPS - s], acc,
                                                       ALU.mult, ALU.add).then_inc(tap_done[v], 1)

                def head_decay(h):
                    dve.wait_ge(habc_mm[u], nth(HEADS * iu + h + 1))
                    dve.wait_ge(score_done[u], nth(HEADS * iu + (h - 1 if h >= 2 else 0)))
                    for b in range(BATCHES):
                        for c in range(2):
                            last = nc.vector.tensor_tensor_scan(
                                hgam[h % 2][u][:, strip(b, c)], bank[u][(3, 0)[h % 2]][:, b * SEQ + c * P:(b + 1) * SEQ],
                                eye_zero[:, 0:SEQ - c * P], 0.0, ALU.mult, ALU.add)
                    last.then_inc(hgam_done[u], 1)

                def skip(r):
                    dve.wait_ge(hy_mm[u], nth(HEADS * iu + 2 * r + 2))
                    dve.wait_ge(out_mm, upto(iu, u))
                    dve.wait_ge(ysq_done[u], nth(INNER_BLOCKS * iu))
                    dve.wait_ge(xbc_done[u], nth(CONV_BLOCKS * (iu + 1)))
                    nc.vector.scalar_tensor_tensor(yT[r][u], xbc[r][u], skip_col[:, r:r + 1], bank[u][1 + r][:, :],
                                                   ALU.mult, ALU.add).then_inc(ydt_done[u], 1)

                def times_dt(r):
                    dve.wait_ge(xtok_mm[v], nth(INNER_BLOCKS * jf + r + 1))
                    dve.wait_ge(hy_mm[v], nth(HEADS * jf))
                    dve.wait_ge(dt_step, dt_steps(jf, DT_STEPS))
                    by_head = "p (t h c) -> p t h c"
                    dt = dt_dt[:, v * DT:(v + 1) * DT].rearrange("p (t h) -> p t h", h=HEADS)[:, :, 2 * r:2 * r + 2]
                    nc.vector.tensor_tensor(
                        xt[v].rearrange(by_head, t=GROUP_TILES, h=HEADS)[:, :, 2 * r:2 * r + 2, :],
                        bank[v][(2, 3)[r]][:, :].rearrange(by_head, t=GROUP_TILES, h=2),
                        dt.unsqueeze(3).broadcast_to([P, GROUP_TILES, 2, HEAD_DIM]), ALU.mult).then_inc(xt_done[v], 1)

                if end:
                    head_decay(0)
                if pair_dt:
                    dve.wait_ge(dt_mm, nth(jf + 1))
                    step(nc.vector.tensor_tensor(
                        z_dt[:, :].rearrange("p (t h) -> p t h", h=HEADS),
                        bank[0][2][:, 0:STREAMS * DT].rearrange("p (t h) -> p t h", h=HEADS),
                        dtb_row[:, :].unsqueeze(1).broadcast_to([P, STREAMS * GROUP_TILES, HEADS]), ALU.add))
                    prior()
                    dve.wait_ge(e_done, nth(jf))
                    step(nc.vector.scalar_tensor_tensor(nabs_dt[:, :], z_dt[:, :], -1.0, z_dt[:, :], ALU.mult, ALU.min))
                if end:
                    head_decay(1)
                if pair_dt:
                    dve.wait_ge(e_done, nth(jf + 1))
                    step(nc.vector.tensor_scalar(den_dt[:, :], e_dt[:, :], 2.0, None, ALU.add))
                    prior()
                    step(nc.vector.reciprocal(rec_dt[:, :], den_dt[:, :]))
                    prior()
                    step(nc.vector.tensor_tensor(w_dt[:, :], e_dt[:, :], rec_dt[:, :], ALU.mult))
                    prior()
                    step(nc.vector.tensor_tensor(w2_dt[:, :], w_dt[:, :], w_dt[:, :], ALU.mult))
                    prior()
                    step(nc.vector.tensor_scalar(acc_dt[:, :], w2_dt[:, :], 1.0 / 15, None, ALU.mult))
                if begin:
                    taps(1, 0)
                if end:
                    head_decay(2)
                if pair_dt:
                    for c in SERIES:
                        prior()
                        step(nc.vector.scalar_tensor_tensor(acc_dt[:, :], acc_dt[:, :], c, w2_dt[:, :], ALU.add, ALU.mult))
                    prior()
                    step(nc.vector.scalar_tensor_tensor(acc_dt[:, :], acc_dt[:, :], 1.0, w_dt[:, :], ALU.add, ALU.mult))
                    step(nc.vector.tensor_scalar(relu_dt[:, :], z_dt[:, :], 0.0, None, ALU.max))
                    prior()
                    step(nc.vector.scalar_tensor_tensor(dt_dt[:, :], acc_dt[:, :], 2.0, relu_dt[:, :], ALU.mult, ALU.add))
                    prior()
                    step(nc.vector.tensor_tensor(
                        dA_dt[:, :].rearrange("p (t h) -> p t h", h=HEADS), dt_dt[:, :].rearrange("p (t h) -> p t h", h=HEADS),
                        aneg_row[:, :].unsqueeze(1).broadcast_to([P, STREAMS * GROUP_TILES, HEADS]), ALU.mult))
                    assert taken[0] == DT_STEPS, taken[0]
                if begin:
                    taps(1, 1)
                if end:
                    head_decay(3)
                if pair_dt:
                    dve.wait_ge(dAT_mm, nth(jf + 1))
                    step(nc.vector.tensor_tensor_scan(csum[:, :], keep[0:ROWS, :], bank[0][2][0:ROWS, 0:P], 0.0,
                                                      ALU.mult, ALU.add))
                    prior()
                    dve.wait_ge(back_mm, nth(jf))
                    of_chunk = csum[:, :].rearrange("r (c t) -> r c t", t=CHUNK)
                    step_of_chunk = dstep[0:ROWS, :].rearrange("r (c t) -> r c t", t=CHUNK)
                    step(nc.vector.tensor_tensor(step_of_chunk[:, :, 1:CHUNK], of_chunk[:, :, 1:CHUNK],
                                                 of_chunk[:, :, 0:CHUNK - 1], ALU.subtract))
                    step(nc.vector.tensor_copy(step_of_chunk[:, :, 0:1], of_chunk[:, :, 0:1]))
                    assert taken[0] == DT_STEPS + CS_STEPS, taken[0]
                if begin:
                    taps(2, 0, 1)
                if end:
                    skip(0)
                if begin:
                    taps(3, 0, 1)
                if end:
                    skip(1)
                if begin:
                    nxt = (jf + 1) % PAIRS
                    stats_of(2 * PAIRS + jf + 1, v, nxt)
                    taps(1, 2, 3)
                    times_dt(0)
                    taps(2, 2, 3)
                    normalise(2 * PAIRS + jf + 1, v, nxt)
                    taps(3, 2)
                if end:
                    dve.wait_ge(ms_mm, upto(iu + 1, u))
                    dve.wait_ge(rms_done, upto(iu, u))
                    nc.vector.tensor_scalar(ms[u], bank[u][2][:, 0:GROUP_TILES], 1.0 / INNER, RMS_EPS,
                                            ALU.mult, ALU.add).then_inc(ms_done, 1)
                if begin:
                    taps(3, 3)
                if end:
                    dve.wait_ge(out_mm, upto(iu + 1, u))
                    dve.wait_ge(rms_done, upto(iu + 1, u))
                    for t in range(GROUP_TILES):
                        xs = x_all[:, ds(iu * PAIR_COLS + u * GROUP + t * P, P)]
                        last = nc.vector.scalar_tensor_tensor(xs, bank[u][1][:, cols(t)], rms[u][:, t:t + 1], xs,
                                                              ALU.mult, ALU.add)
                    last.then_inc(x_done, 1)
                if begin:
                    times_dt(1)

            space_half(None, None, 0, 0)
            space_half(0, 0, 1, 0)
            with dve.Fori(0, PAIRS - 1) as i:
                space_half(1, i, 0, i + 1)
                space_half(0, i + 1, 1, i + 1)
            space_half(1, PAIRS - 1, None, None)
            ffn(1)

        @block.tensor
        def _(pe):
            mm = nc.tensor.matmul

            def transposes(k, u, dst):
                pe.wait_ge(xn_done, upto(k + 1, u))
                for t in range(GROUP_TILES):
                    last = nc.tensor.transpose(bank[u][dst][:, cols(t)], xn[u][:, cols(t)], ident)
                last.then_inc(tr_done, 1)

            for s in paced:
                pe.sem_inc(s, STREAMS)
            for s in (*per_pair, *(s for pair in per_stream for s in pair)):
                pe.sem_inc(s, 1)
            pe.wait_ge(tables_in, 16)
            for u in U:
                transposes(0, u, 3)
            pe.wait_ge(attn_in, 16 * ATTN_DMAS)

            def Z_of(u, i, level):
                if level == 0:
                    pe.wait_ge(LT_done, upto(i + 1, u))
                    pe.wait_ge(g_done, upto(i + 1, u))
                elif level == 1:
                    pe.wait_ge(W_done[u], nth(LEVELS * i + 1))
                else:
                    pe.wait_ge(T_done[u], nth((LEVELS - 2) * i + level - 1))
                for t in range(GROUP_TILES):
                    if level == 0:
                        last = nc.tensor.transpose(bank[u][1][:, cols(t)], LT[u][:, diag(t)], ident)
                    else:
                        last = mm(packed(bank[u][1][:, half_cols(t)], level), LT[u][:, diag(t)],
                                  halves(Tm[u][:, cols(t)], level, 0), start=True, stop=True)
                last.then_inc(Z_mm[u], 1)

            def T_and_R_of(u, i, level):
                pe.wait_ge(W_done[u], nth(LEVELS * i + level + 1))
                if level == 0:
                    pe.wait_ge(x_done, upto(i, u))
                else:
                    pe.wait_ge(R_done[u], nth(LEVELS * i + level))
                if 0 < level < LEVELS - 1:
                    for t in range(GROUP_TILES):
                        last = mm(packed(bank[u][2][:, half_cols(t)], level), Rm[u][:, cols(t)],
                                  halves(Wlev[level][u][:, cols(t)], level, 0), start=True, stop=True)
                    last.then_inc(T_mm[u], 1)
                for t in range(GROUP_TILES):
                    if level == 0:
                        last = nc.tensor.transpose(bank[u][0][:, cols(t)], Tm[u][:, cols(t)], ident)
                    else:
                        last = mm(packed(bank[u][0][:, half_cols(t)], level), Wlev[level][u][:, cols(t)],
                                  halves(Rm[u][:, cols(t)], level, 1), start=True, stop=True)
                last.then_inc(R_mm[u], 1)

            def attention_half(u, iu, v, ib, jf):
                inverse, end, begin = iu is not None, ib is not None, jf is not None
                if inverse:
                    Z_of(u, iu, 0)
                if end:
                    pe.wait_ge(R_done[v], nth(LEVELS * (ib + 1)))
                    for b in range(BATCHES):
                        last = mm(bank[v][3][:, cols(b)], Rm[v][:, cols(2 * b)], vtok[v][:, cols(2 * b)], start=True, stop=True)
                    last.then_inc(w0_mm, 1)
                if inverse:
                    T_and_R_of(u, iu, 0)
                if end:
                    pe.wait_ge(w0_done, upto(ib + 1, v))
                    for b in range(BATCHES):
                        last = mm(bank[v][2][:, cols(b)], LT[v][:, b * TRI + P:b * TRI + 2 * P], w0tok[v][:, cols(b)],
                                  start=True, stop=True)
                    last.then_inc(corr_mm, 1)
                if inverse:
                    Z_of(u, iu, 1)
                if end:
                    pe.wait_ge(v1_done, upto(ib + 1, v))
                    for t in range(GROUP_TILES):
                        last = mm(bank[v][1][:, cols(t)], vtok[v][:, cols(t)], Rm[v][:, cols(t)], start=True, stop=True)
                    last.then_inc(WT_mm, 1)
                if inverse:
                    T_and_R_of(u, iu, 1)
                if end:
                    transposes(ib + 1, v, 2)
                if inverse:
                    Z_of(u, iu, 2)
                if end:
                    pe.wait_ge(WT_done, upto(ib + 1, v))
                    for b in range(BATCHES):
                        for c in range(2):
                            last = mm(bank[v][(0, 3)[b]][:, c * SEQ:c * SEQ + SEQ - c * P], WT[v][:, cols(2 * b + c)],
                                      qT[v][:, b * SEQ + c * P:(b + 1) * SEQ], start=True, stop=True)
                    last.then_inc(PT_mm, 1)
                if inverse:
                    T_and_R_of(u, iu, 2)
                if begin:
                    pe.wait_ge(xnT_done, upto(jf + 1, v))
                    for t in range(GROUP_TILES):
                        last = mm(bank[v][2][:, 2 * t:2 * t + 2], xnT[v][:, cols(t)], wab_sb[:, :], start=True, stop=True)
                    last.then_inc(ab_mm, 1)
                    pe.wait_ge(PT_done, upto(jf, v))
                    for t in range(GROUP_TILES):
                        last = mm(bank[v][0][:, cols(t)], xnT[v][:, cols(t)], wk_sb[:, :], start=True, stop=True)
                    last.then_inc(k_mm, 1)
                if inverse:
                    Z_of(u, iu, 3)
                if begin:
                    for t in range(GROUP_TILES):
                        last = mm(bank[v][1][:, cols(t)], xnT[v][:, cols(t)], wv_sb[:, :], start=True, stop=True)
                    last.then_inc(v_mm, 1)
                if end:
                    pe.wait_ge(PT_done, upto(ib + 1, v))
                    if begin:
                        pe.wait_ge(ablog_done, upto(jf + 1, v))
                    else:
                        pe.wait_ge(xnT_done, upto(ib + 2, v))
                    for b in range(BATCHES):
                        mm(bank[v][2][:, b * SEQ:(b + 1) * SEQ], kn[v][:, cols(2 * b)], PT[v][:, strip(b, 0)],
                           start=True, stop=False)
                        last = mm(bank[v][2][:, b * SEQ + P:(b + 1) * SEQ], kn[v][:, cols(2 * b + 1)], PT[v][:, strip(b, 1)],
                                  start=False, stop=True)
                    last.then_inc(OT_mm, 1)
                if inverse:
                    T_and_R_of(u, iu, 3)
                if begin:
                    mm(bank[v][3][:, :], wq_sb[:, :], xnT[v][:, :], start=True, stop=True).then_inc(q_mm, 1)
                    pe.wait_ge(ab_done, upto(jf + 1, v))
                    pe.wait_ge(kb_done, upto(jf + 1, v))
                    for t in range(GROUP_TILES):
                        last = nc.tensor.transpose(bank[v][0][:, cols(t)],
                                                   ab[v][:, 2 * t:2 * t + 1].broadcast_to([P, P]), ident)
                    last.then_inc(abc_mm, 1)
                if inverse:
                    Z_of(u, iu, 4)
                if begin:
                    pe.wait_ge(kn_done, upto(jf + 1, v))
                    pe.wait_ge(v_done, upto(jf + 1, v))
                    for t in range(GROUP_TILES):
                        last = nc.tensor.transpose(bank[v][1][:, cols(t)], kn[v][:, cols(t)], ident)
                    last.then_inc(kT_mm, 1)
                if inverse:
                    T_and_R_of(u, iu, 4)
                if begin:
                    pe.wait_ge(kT_done, upto(jf + 1, v))
                    pe.wait_ge(q_done, upto(jf + 1, v))
                    pe.wait_ge(og_done, upto(jf, v))
                    for b in range(BATCHES):
                        for c in range(2):
                            last = mm(bank[v][2 + b][:, c * SEQ:c * SEQ + SEQ - c * P], kT[v][:, cols(2 * b + c)],
                                      kT[v][:, b * SEQ + c * P:(b + 1) * SEQ], start=True, stop=True)
                    last.then_inc(G_mm, 1)
                if inverse:
                    Z_of(u, iu, 5)
                if begin:
                    mm(bank[v][1][:, :], wg_sb[:, :], xnT[v][:, :], start=True, stop=True).then_inc(g_mm, 1)
                if inverse:
                    T_and_R_of(u, iu, 5)
                if end:
                    pe.wait_ge(og_done, upto(ib + 1, v))
                    if begin:
                        pe.wait_ge(gam_done, upto(jf + 1, v))
                    for t in range(GROUP_TILES):
                        last = mm(bank[v][0][:, cols(t)], og[v][:, cols(t)], wo_sb[:, :], start=True, stop=True)
                    last.then_inc(y_mm, 1)
                if inverse:
                    Z_of(u, iu, 6)
                    T_and_R_of(u, iu, 6)

            attention_half(None, None, 0, None, 0)
            pe.wait_ge(W_set[0], 1)
            attention_half(0, 0, 1, None, 0)
            pe.wait_ge(W_set[1], 1)
            with pe.Fori(0, PAIRS - 1) as i:
                attention_half(1, i, 0, i, i + 1)
                attention_half(0, i + 1, 1, i, i + 1)
            attention_half(1, PAIRS - 1, 0, PAIRS - 1, None)
            pe.wait_ge(ff_float, 1)
            for n in range(3):
                for k in range(FF_BLOCKS):
                    last = nc.tensor.transpose(bank[0][1 + n][:, cols(k)], ff_raw[:, n, cols(k)], ident)
                last.then_inc(ffT_mm, 1)
            attention_half(None, None, 1, PAIRS - 1, None)

            def ffn(run):
                phase = 2 * run + 1
                for u in U:
                    pe.wait_ge(x_done, upto(phase * PAIRS, u))
                with pe.Fori(0, PAIRS) as i:
                    it = phase * PAIRS + i
                    n = FF_BLOCKS * (i + PAIRS * run)
                    for j in range(FF_BLOCKS):
                        for u in U:
                            if j == 0:
                                pe.wait_ge(xnT_done, upto(it + 1, u))
                                pe.wait_ge(silu_done, upto(n, u))
                            elif j == 1:
                                pe.wait_ge(x_done, upto(it, u))
                            else:
                                pe.wait_ge(silu_done, upto(n + 1, u))
                            mm(bank[u][(1, 3, 1)[j]][:, :], gateT[:, cols(j)], xnT[u][:, :],
                               start=True, stop=True).then_inc(gate_mm, 1)
                            if j == 0:
                                pe.wait_ge(hid_done, upto(n, u))
                            elif j == 2:
                                pe.wait_ge(hid_done, upto(n + 1, u))
                            mm(bank[u][(2, 0, 2)[j]][:, :], upT[:, cols(j)], xnT[u][:, :],
                               start=True, stop=True).then_inc(up_mm, 1)
                    for u in U:
                        pe.wait_ge(hid_done, upto(n + 2, u))
                    for u in U:
                        transposes(it + 1, u, 0)
                    for u in U:
                        pe.wait_ge(hid_done, upto(n + FF_BLOCKS, u))
                        for t in range(GROUP_TILES):
                            for j in range(FF_BLOCKS):
                                last = mm(bank[u][3][:, cols(t)], hidT[u][:, j, cols(t)], downT[:, j, :],
                                          start=(j == 0), stop=(j == FF_BLOCKS - 1))
                        last.then_inc(down_mm, 1)

            pe.wait_ge(ffT_done, 3)
            pe.wait_ge(consts_set, 4)
            pe.wait_ge(later_in, 16 * LATER_DMAS)
            ffn(0)

            for u in U:
                pe.wait_ge(x_done, upto(2 * PAIRS, u))
            pe.wait_ge(prep_done, INNER_BLOCKS + 1)

            def space_half(u, iu, v, jf):
                end, begin, pair_dt = u is not None, v is not None, v == 0

                def conv(r):
                    mm(bank[v][(0, 3, 1, 0)[r]][:, :], win_sb[:, INNER + r * P:INNER + (r + 1) * P], xnT[v][:, :],
                       start=True, stop=True).then_inc(conv_mm[v], 1)

                def gate(r):
                    pe.wait_ge(tap_done[v], nth(taps_upto(jf, 1 + r, TAPS - 1)))
                    mm(bank[v][(3, 1)[r]][:, :], win_sb[:, cols(r)], xnT[v][:, :], start=True, stop=True).then_inc(z_mm[v], 1)

                def token_major(r):
                    pe.wait_ge(xbc_done[v], nth(CONV_BLOCKS * jf + r + 1))
                    if r == 1:
                        pe.wait_ge(sz_done[v], nth(INNER_BLOCKS * jf + 1))
                    elif v == 0:
                        pe.wait_ge(decay_done, nth(jf + 1))
                    else:
                        pe.wait_ge(ms_done, upto(jf, v))
                    for t in range(GROUP_TILES):
                        last = nc.tensor.transpose(bank[v][(2, 3)[r]][:, cols(t)], xbc[r][v][:, cols(t)], ident)
                    last.then_inc(xtok_mm[v], 1)

                def spread_decay(h):
                    if u == 0:
                        pe.wait_ge(decay_done, nth(iu + 1))
                    else:
                        pe.wait_ge(decay1_done, nth(iu + 1))
                    if h == 0:
                        pe.wait_ge(xt_done[u], nth(INNER_BLOCKS * (iu + 1)))
                    elif h == 1:
                        pe.wait_ge(xnT_done, upto(2 * PAIRS + iu + 2, u))
                    else:
                        pe.wait_ge(hgam_done[u], nth(HEADS * iu + h - 1))
                    of_stream = (decay, decay1)[u]
                    for t in range(GROUP_TILES):
                        at = t * HEADS + h
                        last = nc.tensor.transpose(bank[u][(3, 0)[h % 2]][:, cols(t)],
                                                   of_stream[:, at:at + 1].broadcast_to([P, P]), ident)
                    last.then_inc(habc_mm[u], 1)

                def head_output(h):
                    pe.wait_ge(score_done[u], nth(HEADS * iu + h + 1))
                    pe.wait_ge(xt_done[u], nth(INNER_BLOCKS * (iu + 1)))
                    pe.wait_ge(cb_done[u], nth(BATCHES * (iu + 1)))
                    half = (h % 2) * HEAD_DIM
                    xh = xt[u].rearrange("p (t c) -> p t c", t=GROUP_TILES)[:, :, h * HEAD_DIM:(h + 1) * HEAD_DIM]
                    for b in range(BATCHES):
                        yh = bank[u][1 + h // 2][half:half + HEAD_DIM, :]
                        mm(yh[:, b * SEQ:(b + 1) * SEQ], xh[:, 2 * b, :], score[h % 2][u][:, strip(b, 0)],
                           start=True, stop=False)
                        last = mm(yh[:, b * SEQ + P:(b + 1) * SEQ], xh[:, 2 * b + 1, :],
                                  score[h % 2][u][:, strip(b, 1)], start=False, stop=True)
                    last.then_inc(hy_mm[u], 1)

                if end:
                    spread_decay(0)
                    spread_decay(1)
                if pair_dt:
                    pe.wait_ge(ms_done, upto(jf, 0))
                    for w in U:
                        pe.wait_ge(xnT_done, upto(2 * PAIRS + jf + 1, w))
                        for t in range(GROUP_TILES):
                            at = w * DT + t * HEADS
                            last = mm(bank[0][2][:, at:at + HEADS], xnT[w][:, cols(t)], win_sb[:, PROJ - HEADS:PROJ],
                                      start=True, stop=True)
                    last.then_inc(dt_mm, 1)
                if begin:
                    pe.wait_ge(xnT_done, upto(2 * PAIRS + jf + 1, v))
                    pe.wait_ge(hgam_done[v], nth(HEADS * jf))
                    conv(0)
                    conv(1)
                if end:
                    spread_decay(2)
                    head_output(0)
                if begin:
                    pe.wait_ge(x_done, upto(2 * PAIRS + jf, v))
                    conv(2)
                if end:
                    spread_decay(3)
                    head_output(1)
                    head_output(2)
                if pair_dt:
                    pe.wait_ge(dt_step, dt_steps(jf, DT_STEPS))
                    nc.tensor.transpose(bank[0][2][0:ROWS, 0:P], dA_dt[:, :], ident).then_inc(dAT_mm, 1)
                    pe.wait_ge(dt_step, dt_steps(jf, DT_STEPS + CS_STEPS))
                    nc.tensor.transpose(bank[0][2][:, 0:P], dstep[:, :], ident).then_inc(back_mm, 1)
                if end:
                    head_output(3)
                if begin:
                    pe.wait_ge(tap_done[v], nth(taps_upto(jf, 0, TAPS - 1)))
                    conv(3)
                    gate(0)
                    token_major(0)
                if end:
                    pe.wait_ge(ysq_done[u], nth(INNER_BLOCKS * (iu + 1)))
                    for t in range(GROUP_TILES):
                        for r in range(INNER_BLOCKS):
                            last = mm(bank[u][2][:, t:t + 1], ysq[r][u][:, cols(t)], ones_col[:, :],
                                      start=(r == 0), stop=(r == INNER_BLOCKS - 1))
                    last.then_inc(ms_mm, 1)
                    for t in range(GROUP_TILES):
                        for r in range(INNER_BLOCKS):
                            last = mm(bank[u][1][:, cols(t)], yT[r][u][:, cols(t)], wout_sb[:, r, :],
                                      start=(r == 0), stop=(r == INNER_BLOCKS - 1))
                    last.then_inc(out_mm, 1)
                if begin:
                    gate(1)
                    token_major(1)
                    pe.wait_ge(tap_done[v], nth(taps_upto(jf, 3, TAPS - 1)))
                    transposes(2 * PAIRS + jf + 1, v, 0)
                    for b in range(BATCHES):
                        pe.wait_ge(xbc_done[v], nth(CONV_BLOCKS * (jf + 1)))
                        if b == 0:
                            pe.wait_ge(sz_done[v], nth(INNER_BLOCKS * (jf + 1)))
                        else:
                            pe.wait_ge(xt_done[v], nth(INNER_BLOCKS * jf + 1))
                        for c in range(2):
                            last = mm(bank[v][1 + b][:, c * SEQ:c * SEQ + SEQ - c * P], xbc[2][v][:, cols(2 * b + c)],
                                      xbc[3][v][:, b * SEQ + c * P:(b + 1) * SEQ], start=True, stop=True)
                        last.then_inc(cb_mm[v], 1)

            space_half(None, None, 0, 0)
            space_half(0, 0, 1, 0)
            with pe.Fori(0, PAIRS - 1) as i:
                space_half(1, i, 0, i + 1)
                space_half(0, i + 1, 1, i + 1)
            space_half(1, PAIRS - 1, None, None)
            ffn(1)


_INS = ['L0_attn_a_x', 'L0_attn_a_Wq', 'L0_attn_a_bq', 'L0_attn_a_Wk', 'L0_attn_a_bk', 'L0_attn_a_Wv', 'L0_attn_a_bv',
        'L0_attn_a_Wa', 'L0_attn_a_ba', 'L0_attn_a_Wb', 'L0_attn_a_bb', 'L0_attn_a_Wg', 'L0_attn_a_bg', 'L0_attn_a_Wo',
        'L0_attn_a_bo', 'L0_attn_b_W_in', 'L0_attn_b_conv_w', 'L0_attn_b_conv_b', 'L0_attn_b_dt_bias', 'L0_attn_b_A_log',
        'L0_attn_b_D', 'L0_attn_b_norm_w', 'L0_attn_b_W_out', 'L0_ffn_w_gate', 'L0_ffn_w_up', 'L0_ffn_w_down']


def kernel(**inputs):
    import numpy as _np
    import concourse.bacc as _bacc
    from concourse import mybir as _mybir
    from concourse.bass_utils import run_bass_kernel_spmd as _run

    nc = _bacc.Bacc("TRN2", target_bir_lowering=False, num_devices=1)
    arrays, args = {}, []
    for name in _INS:
        a = _np.ascontiguousarray(inputs[name])
        arrays[f"in_{name}"] = a
        args.append(nc.dram_tensor(f"in_{name}", a.shape, _mybir.dt.from_np(a.dtype), kind="ExternalInput").ap())
    table = constants()
    arrays["in_tables"] = table
    args.append(nc.dram_tensor("in_tables", table.shape, _mybir.dt.float32, kind="ExternalInput").ap())
    out = nc.dram_tensor("out", (BATCH, SEQ, DIM), _mybir.dt.float32, kind="ExternalOutput").ap()
    build(nc, *args, out)
    r = _run(nc, [arrays], core_ids=[0])
    return r.results[0]["out"]
```

```python
import concourse.bass as bass
from concourse import mybir
from contextlib import ExitStack

BATCH, SEQ, DIM = 32, 256, 128
HIDDEN = 384
HEADS, HEAD_DIM, STATE = 4, 64, 128
INNER = HEADS * HEAD_DIM
TAPS = 4
CHUNK = 32
PROJ = 2 * INNER + 2 * STATE + HEADS
P = 128
TILES = BATCH * SEQ // P
GROUP_TILES = 4
GROUP = GROUP_TILES * P
STREAMS = 2
PAIRS = TILES // (GROUP_TILES * STREAMS)
PAIR_COLS = STREAMS * GROUP
BATCHES = GROUP // SEQ
TRI = SEQ + P
LEVELS = 7
FF_BLOCKS = HIDDEN // P
CONV_BLOCKS = (INNER + 2 * STATE) // P
INNER_BLOCKS = INNER // P
PHASES = 4
LN_EPS = 1e-5
RMS_EPS = 1e-5
DEQUANT = 1.0 / 127.0
NARROW = 128.0


def constants():
    import numpy as np

    r, c = np.arange(P)[:, None], np.arange(P)[None, :]
    eye = (r == c).astype(np.float32)
    parts = [eye, np.zeros((P, P), np.float32)]
    for level in range(LEVELS):
        n = 2 ** level
        below = (r // (2 * n) == c // (2 * n)) & (r % (2 * n) >= n) & (c % (2 * n) < n)
        parts.append(eye - below.astype(np.float32))
    parts.append(np.broadcast_to((c % CHUNK != 0).astype(np.float32), (P, P)))
    return np.ascontiguousarray(np.concatenate(parts, axis=1))


def build(nc, x_in, Wq, bq, Wk, bk, Wv, bv, Wa, ba, Wb, bb, Wg, bg, Wo, bo,
          W_in, conv_w, conv_b, dt_bias, A_log, D_skip, norm_w, W_out,
          w_gate, w_up, w_down, tables, out):
    f32, f16, i32 = mybir.dt.float32, mybir.dt.float16, mybir.dt.int32
    ALU, ACT, AX = mybir.AluOpType, mybir.ActivationFunctionType, mybir.AxisListType
    ds = bass.ds

    ctx = ExitStack()
    with ctx:
        def sb(name, shape, dt=f32):
            return ctx.enter_context(nc.sbuf_tensor(name, shape, dt))

        def sem(name):
            return ctx.enter_context(nc.semaphore(name))

        def upto(n, u):
            return STREAMS * n + u + 1

        paced = []

        def pace(name):
            paced.append(sem(name))
            return paced[-1]

        x_all = sb("x_all", [P, TILES * DIM])
        tab = sb("tab", [P, (3 + LEVELS) * P])
        ident, eye_zero = tab[:, 0:P], tab[:, 0:2 * P]
        keep = tab[:, (2 + LEVELS) * P:(3 + LEVELS) * P]
        masks = [tab[:, (2 + k) * P:(3 + k) * P] for k in range(LEVELS)]
        half_neg = sb("half_neg", [P, GROUP_TILES])
        eps_cols = sb("eps_cols", [P, GROUP_TILES])
        ones_col = sb("ones_col", [P, 1])

        wq_sb, wg_sb, wo_sb = sb("wq_sb", [P, P]), sb("wg_sb", [P, P]), sb("wo_sb", [P, P])
        wk_sb, wv_sb = sb("wk_sb", [P, P]), sb("wv_sb", [P, P])
        wab_sb = sb("wab_sb", [P, 2])
        bq_col, bg_col = sb("bq_col", [P, 1]), sb("bg_col", [P, 1])
        bk_row, bv_row, bo_row = sb("bk_row", [P, P]), sb("bv_row", [P, P]), sb("bo_row", [P, P])
        bab_row = sb("bab_row", [P, 2])
        win_sb = sb("win_sb", [P, PROJ])
        wout_sb = sb("wout_sb", [P, INNER_BLOCKS, DIM])
        wout_raw = sb("wout_raw", [P, INNER_BLOCKS, DIM])
        convw_sb = sb("convw_sb", [P, CONV_BLOCKS, TAPS])
        convb_sb = sb("convb_sb", [P, CONV_BLOCKS])
        normw_col = sb("normw_col", [P, INNER_BLOCKS])
        skip_col = sb("skip_col", [P, INNER_BLOCKS])
        dtb_row = sb("dtb_row", [P, HEADS])
        alog_row = sb("alog_row", [P, HEADS])
        aexp_row = sb("aexp_row", [P, HEADS])
        aneg_row = sb("aneg_row", [P, HEADS])
        ff_int = sb("ff_int", [P, 3, HIDDEN], i32)
        ff_raw = sb("ff_raw", [P, 3, HIDDEN])
        gateT, upT = sb("gateT", [P, HIDDEN]), sb("upT", [P, HIDDEN])
        downT = sb("downT", [P, FF_BLOCKS, DIM])
        gate16, up16 = sb("gate16", [P, HIDDEN], f16), sb("up16", [P, HIDDEN], f16)
        down16 = sb("down16", [P, FF_BLOCKS, DIM], f16)
        wmax, wmin, widest, widest_all = (sb(n, [P, 1]) for n in ("wmax", "wmin", "widest", "widest_all"))
        narrow = sb("narrow", [P, 1], i32)

        U = range(STREAMS)
        stats = [sb(f"stats{u}", [P, GROUP_TILES, 6]) for u in U]
        mv = [sb(f"mv{u}", [P, GROUP_TILES, 2]) for u in U]
        carrier = [sb(f"carrier{u}", [P, 1]) for u in U]
        var_eps = [sb(f"var_eps{u}", [P, GROUP_TILES]) for u in U]
        rstd = [sb(f"rstd{u}", [P, GROUP_TILES]) for u in U]
        xn = [sb(f"xn{u}", [P, GROUP]) for u in U]
        xnT = [sb(f"xnT{u}", [P, GROUP]) for u in U]
        ff = [sb(f"ff{u}", [P, 2 * FF_BLOCKS, GROUP]) for u in U]
        silu_g = [ff[u][:, 0:FF_BLOCKS, :] for u in U]
        xh, xl = ([sb(f"{n}{u}", [P, GROUP], f16) for u in U] for n in ("xh", "xl"))
        hh, hl = ([sb(f"{n}{u}", [P, FF_BLOCKS, GROUP], f16) for u in U] for n in ("hh", "hl"))
        hidT = [ff[u][:, FF_BLOCKS:, :] for u in U]
        assert LEVELS - 1 == 2 * FF_BLOCKS
        Wlev = [None] + [[ff[u][:, k, :] for u in U] for k in range(LEVELS - 1)]
        ARENA = 20 * GROUP + 64
        arena = [sb(f"arena{u}", [P, ARENA]) for u in U]

        def carver():
            at = [0]

            def carve(cols):
                a, at[0] = at[0], at[0] + cols
                assert at[0] <= ARENA, at[0]
                return [arena[u][:, a:a + cols] for u in U]
            return carve

        carve = carver()
        kb, ksq, kn, kT = carve(GROUP), carve(GROUP), carve(GROUP), carve(GROUP)
        vtok, qT, gT, xb = carve(GROUP), carve(GROUP), carve(GROUP), carve(GROUP)
        gam, LT, PT = carve(BATCHES * TRI), carve(BATCHES * TRI), carve(BATCHES * TRI)
        Tm, Rm, WT, og = carve(GROUP), carve(GROUP), carve(GROUP), carve(GROUP)
        w0tok = carve(BATCHES * P)
        ablog, ab = carve(2 * GROUP_TILES), carve(2 * GROUP_TILES)
        kss, kinv = carve(GROUP_TILES), carve(GROUP_TILES)
        carve = carver()
        xbc = [carve(GROUP) for _ in range(CONV_BLOCKS)]
        siluz = [carve(GROUP) for _ in range(INNER_BLOCKS)]
        xt = carve(GROUP_TILES * INNER)
        cb = carve(BATCHES * TRI)
        hgam = [carve(BATCHES * TRI) for _ in range(2)]
        score = [carve(BATCHES * TRI) for _ in range(2)]
        yT = [carve(GROUP) for _ in range(INNER_BLOCKS)]
        ysq = [carve(GROUP) for _ in range(INNER_BLOCKS)]
        ms, rms = carve(GROUP_TILES), carve(GROUP_TILES)
        DT = GROUP_TILES * HEADS
        ROWS = STREAMS * DT
        csum, dstep = sb("csum", [ROWS, P]), sb("dstep", [P, P])
        small = [sb(f"dt_{n}", [P, STREAMS * DT]) for n in
                 ("z", "nabs", "e", "den", "rec", "w", "w2", "acc", "relu", "dt", "dA", "decay")]
        z_dt, nabs_dt, e_dt, den_dt, rec_dt, w_dt, w2_dt, acc_dt, relu_dt, dt_dt, dA_dt, decay = small
        decay1 = sb("decay1", [P, DT])

        bank = [[ctx.enter_context(nc.psum_tensor(f"bank{u}_{k}", [P, GROUP], f32)) for k in range(4)]
                for u in U]

        first_x_in, second_x_in, rest_x_in, x_out = (sem(n) for n in ("first_x_in", "second_x_in", "rest_x_in", "x_out"))
        tables_in, attn_in, later_in = sem("tables_in"), sem("attn_in"), sem("later_in")
        widest_step, widest_mm, narrow_set = sem("widest_step"), sem("widest_mm"), sem("narrow_set")
        consts_set, ff_float, ffT_mm, ffT_done, aexp_done, prep_done = (
            sem("consts_set"), sem("ff_float"), sem("ffT_mm"), sem("ffT_done"), sem("aexp_done"), sem("prep_done"))
        stats_done, mv_done, var_done, rstd_done, xn_done, tr_done, xnT_done, x_done = (
            pace(n) for n in ("stats_done", "mv_done", "var_done", "rstd_done", "xn_done", "tr_done", "xnT_done", "x_done"))
        down_mm = pace("down_mm")
        k_mm, v_mm, ab_mm, q_mm, g_mm, kT_mm, abc_mm, G_mm, w0_mm, corr_mm, WT_mm, PT_mm, OT_mm, y_mm = (
            pace(n) for n in ("k_mm", "v_mm", "ab_mm", "q_mm", "g_mm", "kT_mm", "abc_mm", "G_mm",
                              "w0_mm", "corr_mm", "WT_mm", "PT_mm", "OT_mm", "y_mm"))
        kb_done, v_done, ablog_done, ab_done, q_done, g_done, ksq_done, kss_done, kmax_done, kinv_done, kn_done, kT_done = (
            pace(n) for n in ("kb_done", "v_done", "ablog_done", "ab_done", "q_done", "g_done", "ksq_done", "kss_done",
                              "kmax_done", "kinv_done", "kn_done", "kT_done"))
        gam_done, LTraw_done, LT_done, w0_done, v1_done, WT_done, PT_done, og_done, xb_done = (
            pace(n) for n in ("gam_done", "LTraw_done", "LT_done", "w0_done", "v1_done",
                              "WT_done", "PT_done", "og_done", "xb_done"))
        ms_mm, out_mm, ms_done, rms_done = (pace(n) for n in ("ms_mm", "out_mm", "ms_done", "rms_done"))
        Z_mm, T_mm, R_mm, W_done, T_done, R_done = ([sem(f"{n}{u}") for u in U] for n in
                                                    ("Z_mm", "T_mm", "R_mm", "W_done", "T_done", "R_done"))
        xh_done, xl_done, gate_mm, up_mm, silu_done, hid_done, hh_done, hl_done = ([sem(f"{n}{u}") for u in U] for n in (
            "xh_done", "xl_done", "gate_mm", "up_mm", "silu_done", "hid_done", "hh_done", "hl_done"))
        conv_mm, z_mm, xtok_mm, cb_mm, habc_mm, hy_mm = ([sem(f"{n}{u}") for u in U] for n in (
            "conv_mm", "z_mm", "xtok_mm", "cb_mm", "habc_mm", "hy_mm"))
        conv_init, tap_done, xbc_done, sz_done, xt_done, cb_done = ([sem(f"{n}{u}") for u in U] for n in (
            "conv_init", "tap_done", "xbc_done", "sz_done", "xt_done", "cb_done"))
        hgam_done, score_done, ydt_done, yT_done, ysq_done = ([sem(f"{n}{u}") for u in U] for n in (
            "hgam_done", "score_done", "ydt_done", "yT_done", "ysq_done"))
        per_stream = (xh_done, xl_done, gate_mm, up_mm, silu_done, hid_done, hh_done, hl_done, Z_mm, T_mm, R_mm, W_done, T_done, R_done, conv_mm, z_mm, xtok_mm, cb_mm, habc_mm, hy_mm, conv_init,
                      tap_done, xbc_done, sz_done, xt_done, cb_done, hgam_done, score_done, ydt_done, yT_done, ysq_done)
        W_set, dt_step = [sem(f"W_set{u}") for u in U], sem("dt_step")
        per_pair = dt_mm, e_done, decay_done, decay1_done, dAT_mm, back_mm = [
            sem(n) for n in ("dt_mm", "e_done", "decay_done", "decay1_done", "dAT_mm", "back_mm")]
        ATTN_DMAS = 14
        LATER_DMAS = 8 + CONV_BLOCKS + INNER_BLOCKS + HEADS

        def tile4(ap):
            return ap.rearrange("p (t c) -> p t c", t=GROUP_TILES)

        def cols(k):
            return slice(k * P, (k + 1) * P)

        def strip(b, c):
            a = b * TRI + c * SEQ
            return slice(a, a + SEQ - c * P)

        def diag(t):
            a = (t // 2) * TRI + (t % 2) * SEQ
            return slice(a, a + P)

        def halves(ap, level, which):
            return ap.rearrange("p (q s n) -> p q s n", s=2, n=2 ** level)[:, :, which, :]

        def packed(ap, level):
            return ap.rearrange("p (q n) -> p q n", n=2 ** level)

        def half_cols(t):
            return slice(t * P // 2, (t + 1) * P // 2)

        def nth(n):
            return n + 1

        def taps_upto(i, r, s):
            return TAPS_ALL * i + 2 * (TAPS - 1) * (r // 2) + 2 * (s - 1) + r % 2 + 1

        def x_parts(run, i, u):
            return nth(run * (PAIRS + 1 - u) + i + 1)

        def group_cols(pair, u):
            return ds(pair * PAIR_COLS + u * GROUP, GROUP)

        SERIES = [1.0 / n for n in range(13, 2, -2)]
        TAPS_ALL = (TAPS - 1) * CONV_BLOCKS
        DT_STEPS = 2 + 6 + len(SERIES) + 3
        CS_STEPS = 3

        def dt_steps(i, n):
            return (DT_STEPS + CS_STEPS) * i + n

        block = ctx.enter_context(nc.Block())

        @block.sync
        def _(sp):
            x_tok = x_in.rearrange("b (c p) d -> p (b c) d", p=P)
            x_sb = x_all[:, :].rearrange("p (n d) -> p n d", d=DIM)
            step = GROUP_TILES * STREAMS
            for u in U:
                group = slice(u * GROUP_TILES, (u + 1) * GROUP_TILES)
                sp.dma_start(x_sb[:, group, :], x_tok[:, group, :]).then_inc(first_x_in, 16)
            sp.dma_start(tab[:, :], tables).then_inc(tables_in, 16)

            def load(dst, src, loaded):
                sp.dma_start(dst, src).then_inc(loaded, 16)

            def column(v):
                return v.rearrange("(p a) -> p a", a=1)

            def row(v):
                return v.rearrange("(a n) -> a n", a=1).partition_broadcast(P)[:, 0, :]

            load(wk_sb[:, :], Wk, attn_in)
            load(wab_sb[:, 0:1], Wa, attn_in)
            load(wab_sb[:, 1:2], Wb, attn_in)
            for dst, src in ((bab_row[:, 0:1], ba), (bab_row[:, 1:2], bb), (bk_row[:, :], bk), (bv_row[:, :], bv)):
                load(dst, row(src), attn_in)
            load(wv_sb[:, :], Wv, attn_in)
            load(wq_sb[:, :], Wq, attn_in)
            load(bq_col[:, :], column(bq), attn_in)
            load(wg_sb[:, :], Wg, attn_in)
            load(bg_col[:, :], column(bg), attn_in)
            load(wo_sb[:, :], Wo, attn_in)
            load(bo_row[:, :], row(bo), attn_in)
            for k in range(1, PAIRS):
                sp.dma_start(x_sb[:, k * step:(k + 1) * step, :],
                             x_tok[:, k * step:(k + 1) * step, :]).then_inc(second_x_in if k == 1 else rest_x_in, 16)
            load(ff_int[:, 0, :].rearrange("p (k d) -> p k d", d=DIM), w_gate.rearrange("(k p) d -> p k d", p=P), later_in)
            load(ff_int[:, 1, :].rearrange("p (k d) -> p k d", d=DIM), w_up.rearrange("(k p) d -> p k d", p=P), later_in)
            load(ff_int[:, 2, :], w_down, later_in)
            load(win_sb[:, :], W_in, later_in)
            load(wout_raw[:, :, :], W_out.rearrange("(k p) d -> p k d", p=P), later_in)
            load(convw_sb[:, :, :], conv_w.rearrange("(k p) t -> p k t", p=P), later_in)
            for k in range(CONV_BLOCKS):
                load(convb_sb[:, k:k + 1], column(conv_b[k * P:(k + 1) * P]), later_in)
            for k in range(INNER_BLOCKS):
                load(normw_col[:, k:k + 1], column(norm_w[k * P:(k + 1) * P]), later_in)
            load(dtb_row[:, :], row(dt_bias), later_in)
            load(alog_row[:, :], row(A_log), later_in)
            for h in range(HEADS):
                half = (h % 2) * HEAD_DIM
                load(skip_col[half:half + HEAD_DIM, h // 2:h // 2 + 1],
                     D_skip[h:h + 1].rearrange("(a n) -> a n", a=1).partition_broadcast(HEAD_DIM)[:, 0, :], later_in)
            out_tok = out.rearrange("b (c p) d -> p (b c) d", p=P)
            for k in range(PAIRS):
                for u in U:
                    sp.wait_ge(x_done, upto((PHASES - 1) * PAIRS + k + 1, u))
                sp.dma_start(out_tok[:, k * step:(k + 1) * step, :],
                             x_sb[:, k * step:(k + 1) * step, :]).then_inc(x_out, 16)
            sp.wait_ge(x_out, 16 * PAIRS)

        @block.gpsimd
        def _(pool):
            nc.gpsimd.memset(half_neg[:, :], -0.5).then_inc(consts_set, 1)
            nc.gpsimd.memset(eps_cols[:, :], LN_EPS).then_inc(consts_set, 1)
            nc.gpsimd.memset(ones_col[:, :], 1.0).then_inc(consts_set, 1)
            nc.gpsimd.memset(dstep[:, :], 0.0).then_inc(consts_set, 1)
            pool.wait_ge(consts_set, 4)

            def ln_rstd(k, u):
                pool.wait_ge(mv_done, upto(k + 1, u))
                nc.gpsimd.tensor_tensor(var_eps[u][:, :], mv[u][:, :, 1], eps_cols[:, :], ALU.add).then_inc(var_done, 1)
                pool.wait_ge(var_done, upto(k + 1, u))
                nc.gpsimd.tensor_tensor(rstd[u][:, :], var_eps[u][:, :], half_neg[:, :], ALU.pow).then_inc(rstd_done, 1)

            def attention_half(u, iu, v, ib, jf):
                if ib is not None:
                    pool.wait_ge(rest_x_in, 16 * (PAIRS - 2))
                    pool.wait_ge(second_x_in, 16)
                    pool.wait_ge(first_x_in, 16 * STREAMS)
                    pool.wait_ge(xb_done, upto(ib, v))
                    pool.wait_ge(x_done, upto(ib, v))
                    nc.gpsimd.tensor_tensor(tile4(xb[v]), tile4(x_all[:, group_cols(ib, v)]),
                                            bo_row[:, :].unsqueeze(1).broadcast_to([P, GROUP_TILES, P]),
                                            ALU.add).then_inc(xb_done, 1)
                if iu is not None:
                    ln_rstd(iu + 1, u)
                if jf is not None:
                    pool.wait_ge(kmax_done, upto(jf + 1, v))
                    nc.gpsimd.tensor_tensor(kinv[v], kss[v], half_neg[:, :], ALU.pow).then_inc(kinv_done, 1)
                    pool.wait_ge(consts_set, 4)
                    pool.wait_ge(LTraw_done, upto(jf + 1, v))
                    for b in range(BATCHES):
                        square = LT[v][:, b * TRI:(b + 1) * TRI].rearrange("p (s c) -> p s c", c=P)[:, 0:3:2, :]
                        last = nc.gpsimd.affine_select(out=square, in_=square, compare_op=ALU.not_equal, fill=1.0, base=0,
                                                       pattern=[[0, 2], [-1, P]], channel_multiplier=1)
                    last.then_inc(LT_done, 1)

            for u in U:
                ln_rstd(0, u)
            pool.wait_ge(attn_in, 16 * ATTN_DMAS)
            attention_half(None, None, 0, None, 0)
            attention_half(0, 0, 1, None, 0)
            with pool.Fori(0, PAIRS - 1) as i:
                attention_half(1, i, 0, i, i + 1)
                attention_half(0, i + 1, 1, i, i + 1)
            attention_half(1, PAIRS - 1, 0, PAIRS - 1, None)
            attention_half(None, None, 1, PAIRS - 1, None)
            def ffn(run):
                def ffn_half(u, i, prev):
                    n = FF_BLOCKS * (i + PAIRS * run)
                    ln_rstd((2 * run + 1) * PAIRS + i + 1, u)
                    for j in range(FF_BLOCKS):
                        pool.wait_ge(hh_done[u], nth(n + j + 1))
                        nc.gpsimd.tensor_tensor(hl[u][:, j, :], hidT[u][:, j, :], hh[u][:, j, :],
                                                ALU.subtract).then_inc(hl_done[u], 1)

                ffn_half(0, 0, None)
                with pool.Fori(0, PAIRS - 1) as i:
                    ffn_half(1, i, i)
                    ffn_half(0, i + 1, i)
                ffn_half(1, PAIRS - 1, PAIRS - 1)

            ffn(0)

            def space_half(u, iu, v, jf):
                if u is not None:
                    for h in range(HEADS):
                        pool.wait_ge(hgam_done[u], nth(HEADS * iu + h + 1))
                        pool.wait_ge(cb_done[u], nth(BATCHES * (iu + 1)))
                        pool.wait_ge(hy_mm[u], nth(HEADS * iu + (h - 1 if h >= 2 else 0)))
                        nc.gpsimd.tensor_tensor(score[h % 2][u], cb[u], hgam[h % 2][u], ALU.mult).then_inc(score_done[u], 1)
                    for r in range(INNER_BLOCKS):
                        pool.wait_ge(ydt_done[u], nth(INNER_BLOCKS * iu + r + 1))
                        pool.wait_ge(sz_done[u], nth(INNER_BLOCKS * (iu + 1)))
                        nc.gpsimd.tensor_tensor(yT[r][u], yT[r][u], siluz[r][u], ALU.mult).then_inc(yT_done[u], 1)
                if v is not None:
                    ln_rstd(2 * PAIRS + jf + 1, v)
                if u is not None:
                    pool.wait_ge(ms_done, upto(iu + 1, u))
                    nc.gpsimd.tensor_tensor(rms[u], ms[u], half_neg[:, :], ALU.pow).then_inc(rms_done, 1)

            space_half(None, None, 0, 0)
            space_half(0, 0, 1, 0)
            with pool.Fori(0, PAIRS - 1) as i:
                space_half(1, i, 0, i + 1)
                space_half(0, i + 1, 1, i + 1)
            space_half(1, PAIRS - 1, None, None)
            ffn(1)

        @block.scalar
        def _(act):
            def feature_major(k, u, src):
                act.wait_ge(tr_done, upto(k + 1, u))
                nc.scalar.activation(xnT[u][:, :], bank[u][src][:, :], ACT.Copy).then_inc(xnT_done, 1)

            def T_out(u, i, level):
                act.wait_ge(T_mm[u], nth((LEVELS - 2) * i + level))
                nc.scalar.activation(halves(Tm[u], level, 0), packed(bank[u][2][:, 0:GROUP // 2], level),
                                     ACT.Copy).then_inc(T_done[u], 1)

            def R_out(u, i, level):
                act.wait_ge(R_mm[u], nth(LEVELS * i + level + 1))
                if level == 0:
                    nc.scalar.activation(Rm[u], bank[u][0][:, :], ACT.Copy).then_inc(R_done[u], 1)
                elif level < LEVELS - 1:
                    nc.scalar.activation(halves(Rm[u], level, 1), halves(bank[u][0][:, :], level, 1),
                                         ACT.Copy).then_inc(R_done[u], 1)
                else:
                    nc.scalar.activation(halves(Rm[u], level, 1), packed(bank[u][0][:, 0:GROUP // 2], level),
                                         ACT.Copy).then_inc(R_done[u], 1)

            def attention_half(u, iu, v, ib, jf):
                inverse, end, begin = iu is not None, ib is not None, jf is not None
                if end:
                    act.wait_ge(w0_mm, upto(ib + 1, v))
                    nc.scalar.activation(w0tok[v], bank[v][3][:, 0:BATCHES * P], ACT.Copy).then_inc(w0_done, 1)
                if inverse:
                    R_out(u, iu, 0)
                if end:
                    act.wait_ge(WT_mm, upto(ib + 1, v))
                    nc.scalar.activation(WT[v], bank[v][1][:, :], ACT.Copy).then_inc(WT_done, 1)
                if inverse:
                    T_out(u, iu, 1)
                if end:
                    feature_major(ib + 1, v, 2)
                if inverse:
                    R_out(u, iu, 1)
                    T_out(u, iu, 2)
                if begin:
                    act.wait_ge(ablog_done, upto(jf + 1, v))
                    act.wait_ge(PT_done, upto(jf, v))
                    nc.scalar.activation(ab[v], ablog[v], ACT.Sigmoid).then_inc(ab_done, 1)
                if inverse:
                    R_out(u, iu, 2)
                if begin:
                    act.wait_ge(kb_done, upto(jf + 1, v))
                    nc.scalar.activation(ksq[v], kb[v], ACT.Square).then_inc(ksq_done, 1)
                if inverse:
                    T_out(u, iu, 3)
                if begin:
                    act.wait_ge(q_mm, upto(jf + 1, v))
                    act.wait_ge(PT_mm, upto(jf, v))
                    nc.scalar.activation(qT[v], bank[v][3][:, :], ACT.Identity, bias=bq_col[:, :]).then_inc(q_done, 1)
                if inverse:
                    R_out(u, iu, 3)
                if begin:
                    act.wait_ge(kT_mm, upto(jf + 1, v))
                    nc.scalar.activation(kT[v], bank[v][1][:, :], ACT.Copy).then_inc(kT_done, 1)
                if inverse:
                    T_out(u, iu, 4)
                    R_out(u, iu, 4)
                if begin:
                    act.wait_ge(g_mm, upto(jf + 1, v))
                    act.wait_ge(og_done, upto(jf, v))
                    nc.scalar.activation(gT[v], bank[v][1][:, :], ACT.Sigmoid, bias=bg_col[:, :]).then_inc(g_done, 1)
                if inverse:
                    T_out(u, iu, 5)
                    R_out(u, iu, 5)
                    R_out(u, iu, 6)

            act.wait_ge(tables_in, 16)
            nc.scalar.activation(ff[0][:, :, :].rearrange("p k (t c) -> p (k t) c", c=P),
                                 ident.unsqueeze(1).broadcast_to([P, 2 * FF_BLOCKS * GROUP_TILES, P]),
                                 ACT.Copy).then_inc(W_set[0], 1)
            for u in U:
                feature_major(0, u, 3)
            act.wait_ge(attn_in, 16 * ATTN_DMAS)
            attention_half(None, None, 0, None, 0)
            attention_half(0, 0, 1, None, 0)
            act.wait_ge(later_in, 16 * LATER_DMAS)
            nc.scalar.activation(ff_raw[:, :, :], ff_int[:, :, :], ACT.Copy).then_inc(ff_float, 1)
            with act.Fori(0, PAIRS - 1) as i:
                attention_half(1, i, 0, i, i + 1)
                attention_half(0, i + 1, 1, i, i + 1)
            attention_half(1, PAIRS - 1, 0, PAIRS - 1, None)
            for n, dst in enumerate((gateT[:, :], upT[:, :], downT[:, :, :].rearrange("p k d -> p (k d)"))):
                act.wait_ge(ffT_mm, n + 1)
                nc.scalar.activation(dst, bank[0][1 + n][:, 0:HIDDEN], ACT.Copy).then_inc(ffT_done, 1)
            for n, dst in enumerate((gate16[:, :], up16[:, :], down16[:, :, :].rearrange("p k d -> p (k d)"))):
                nc.scalar.activation(dst, bank[0][1 + n][:, 0:HIDDEN], ACT.Copy).then_inc(ffT_done, 1)
            attention_half(None, None, 1, PAIRS - 1, None)

            def ffn(run):
                def high_x(k, i, u):
                    act.wait_ge(xnT_done, upto(k + 1, u))
                    nc.scalar.activation(xh[u][:, :], xnT[u][:, :], ACT.Copy).then_inc(xh_done[u], 1)

                def next_x(u, i):
                    k = (2 * run + 1) * PAIRS + i + 1
                    act.wait_ge(up_mm[u], nth(FF_BLOCKS * (i + 1 + PAIRS * run)))
                    feature_major(k, u, 0)
                    if u == 0 or not (isinstance(i, int) and i == PAIRS - 1):
                        high_x(k, i + 1, u)

                def ffn_half(u, i, prev):
                    n = FF_BLOCKS * (i + PAIRS * run)

                    def gate(j):
                        act.wait_ge(gate_mm[u], nth(n + j + 1))
                        act.wait_ge(hid_done[u], nth(n))
                        nc.scalar.activation(silu_g[u][:, j, :], bank[u][(1, 3, 1)[j]][:, :], ACT.Silu,
                                             scale=DEQUANT).then_inc(silu_done[u], 1)

                    def high_part(j):
                        act.wait_ge(hid_done[u], nth(n + j + 1))
                        act.wait_ge(down_mm, upto(i + PAIRS * run, u))
                        nc.scalar.activation(hh[u][:, j, :], hidT[u][:, j, :], ACT.Copy).then_inc(hh_done[u], 1)

                    gate(0)
                    gate(1)
                    if prev is not None:
                        next_x(1 - u, prev)
                    high_part(0)
                    gate(2)
                    high_part(1)
                    high_part(2)

                for u in U:
                    high_x((2 * run + 1) * PAIRS, 0, u)
                ffn_half(0, 0, None)
                with act.Fori(0, PAIRS - 1) as i:
                    ffn_half(1, i, i)
                    ffn_half(0, i + 1, i)
                ffn_half(1, PAIRS - 1, PAIRS - 1)
                next_x(1, PAIRS - 1)

            nc.scalar.activation(aexp_row[:, :], alog_row[:, :], ACT.Exp).then_inc(aexp_done, 1)
            ffn(0)

            def space_half(u, iu, v, jf):
                end, begin = u is not None, v is not None

                def first_tap(r):
                    act.wait_ge(conv_mm[v], nth(CONV_BLOCKS * jf + r + 1))
                    act.wait_ge(ydt_done[v], nth(INNER_BLOCKS * jf))
                    nc.scalar.activation(xbc[r][v], bank[v][(0, 3, 1, 0)[r]][:, :], ACT.Identity,
                                         scale=convw_sb[:, r, TAPS - 1:TAPS],
                                         bias=convb_sb[:, r:r + 1]).then_inc(conv_init[v], 1)

                def silu_x(r):
                    act.wait_ge(tap_done[v], nth(taps_upto(jf, r, TAPS - 1)))
                    nc.scalar.activation(xbc[r][v], xbc[r][v], ACT.Silu).then_inc(xbc_done[v], 1)

                def silu_z(r):
                    act.wait_ge(z_mm[v], nth(INNER_BLOCKS * jf + r + 1))
                    act.wait_ge(yT_done[v], nth(INNER_BLOCKS * jf))
                    nc.scalar.activation(siluz[r][v], bank[v][(3, 1)[r]][:, :], ACT.Silu).then_inc(sz_done[v], 1)

                def square_y(r):
                    act.wait_ge(yT_done[u], nth(INNER_BLOCKS * iu + r + 1))
                    act.wait_ge(out_mm, upto(iu, u))
                    nc.scalar.activation(ysq[r][u], yT[r][u], ACT.Square).then_inc(ysq_done[u], 1)

                if begin and v == 0:
                    act.wait_ge(dt_step, dt_steps(jf, 2))
                    nc.scalar.activation(e_dt[:, :], nabs_dt[:, :], ACT.Exp).then_inc(e_done, 1)
                if begin:
                    first_tap(0)
                    first_tap(1)
                    first_tap(2)
                if begin and v == 0:
                    act.wait_ge(back_mm, nth(jf + 1))
                    act.wait_ge(habc_mm[0], nth(HEADS * jf))
                    act.wait_ge(decay1_done, nth(jf))
                    nc.scalar.activation(decay[:, :], bank[0][2][:, 0:ROWS], ACT.Exp).then_inc(decay_done, 1)
                elif begin:
                    act.wait_ge(decay_done, nth(jf + 1))
                    act.wait_ge(habc_mm[v], nth(HEADS * jf))
                    nc.scalar.activation(decay1[:, :], decay[:, DT:2 * DT], ACT.Copy).then_inc(decay1_done, 1)
                if begin:
                    silu_x(0)
                if end:
                    square_y(0)
                if begin:
                    silu_x(1)
                    first_tap(3)
                    silu_z(0)
                if end:
                    square_y(1)
                if begin:
                    silu_x(2)
                    silu_x(3)
                    silu_z(1)
                    feature_major(2 * PAIRS + jf + 1, v, 0)
                    for b in range(BATCHES):
                        act.wait_ge(cb_mm[v], nth(BATCHES * jf + b + 1))
                        act.wait_ge(score_done[v], nth(HEADS * jf))
                        nc.scalar.activation(cb[v][:, b * TRI:(b + 1) * TRI], bank[v][1 + b][:, 0:TRI],
                                             ACT.Copy).then_inc(cb_done[v], 1)

            space_half(None, None, 0, 0)
            space_half(0, 0, 1, 0)
            with act.Fori(0, PAIRS - 1) as i:
                space_half(1, i, 0, i + 1)
                space_half(0, i + 1, 1, i + 1)
            space_half(1, PAIRS - 1, None, None)
            ffn(1)

        @block.vector
        def _(dve):
            def stats_of(k, u, pair, behind=1):
                if not isinstance(k, int) or k >= PAIRS:
                    dve.wait_ge(x_done, upto(k - behind, u))
                for t in range(GROUP_TILES):
                    last = nc.vector.bn_stats(stats[u][:, t, :], x_all[:, ds(pair * PAIR_COLS + u * GROUP + t * P, P)])
                last.then_inc(stats_done, 1)
                dve.wait_ge(stats_done, upto(k + 1, u))
                nc.vector.memset(carrier[u][:, :], 0.0)
                for t in range(GROUP_TILES):
                    last = nc.vector.bn_aggr(mv[u][:, t, :], stats[u][:, t, :])
                last.then_inc(mv_done, 1)

            def normalise(k, u, pair):
                dve.wait_ge(rstd_done, upto(k + 1, u))
                dve.wait_ge(tr_done, upto(k, u))
                for t in range(GROUP_TILES):
                    last = nc.vector.tensor_scalar(xn[u][:, cols(t)],
                                                   x_all[:, ds(pair * PAIR_COLS + u * GROUP + t * P, P)],
                                                   mv[u][:, t, 0:1], rstd[u][:, t:t + 1], ALU.subtract, ALU.mult)
                last.then_inc(xn_done, 1)

            dve.wait_ge(first_x_in, 16 * STREAMS)
            for u in U:
                stats_of(0, u, 0)
            for u in U:
                normalise(0, u, 0)
            dve.wait_ge(tables_in, 16)
            nc.vector.tensor_copy(ff[1][:, :, :].rearrange("p k (t c) -> p (k t) c", c=P),
                                  ident.unsqueeze(1).broadcast_to([P, 2 * FF_BLOCKS * GROUP_TILES, P])).then_inc(W_set[1], 1)
            dve.wait_ge(consts_set, 4)
            dve.wait_ge(attn_in, 16 * ATTN_DMAS)

            def per_tile(ap):
                return ap.unsqueeze(1).broadcast_to([P, GROUP_TILES, ap.shape[-1]])

            def masked(u, i, level):
                dve.wait_ge(Z_mm[u], nth(LEVELS * i + level + 1))
                dve.wait_ge(R_mm[u], nth(LEVELS * i))
                if level == 0:
                    nc.vector.tensor_tensor(tile4(Tm[u]), tile4(bank[u][1][:, :]), per_tile(masks[0]),
                                            ALU.mult).then_inc(W_done[u], 1)
                else:
                    n = 2 ** level
                    nc.vector.tensor_tensor(
                        halves(Wlev[level][u], level, 0).rearrange("p (t q) n -> p t q n", t=GROUP_TILES),
                        bank[u][1][:, 0:GROUP // 2].rearrange("p (t q n) -> p t q n", t=GROUP_TILES, n=n),
                        halves(masks[level], level, 0).unsqueeze(1).broadcast_to([P, GROUP_TILES, P // (2 * n), n]),
                        ALU.mult).then_inc(W_done[u], 1)

            def gated(dst, u, banks):
                for b in range(BATCHES):
                    for c in range(2):
                        last = nc.vector.scalar_tensor_tensor(
                            dst[u][:, strip(b, c)], bank[u][banks[b]][:, c * SEQ:c * SEQ + SEQ - c * P],
                            tile4(ab[u])[:, 2 * b + c, 1:2], gam[u][:, strip(b, c)], ALU.mult, ALU.mult)
                return last

            def attention_half(u, iu, v, ib, jf):
                inverse, end, begin = iu is not None, ib is not None, jf is not None
                if inverse:
                    masked(u, iu, 0)
                if end:
                    dve.wait_ge(corr_mm, upto(ib + 1, v))
                    second = tile4(vtok[v])[:, 1:GROUP_TILES:2, :]
                    nc.vector.tensor_tensor(second, second,
                                            bank[v][2][:, 0:BATCHES * P].rearrange("p (b c) -> p b c", c=P),
                                            ALU.subtract).then_inc(v1_done, 1)
                if inverse:
                    masked(u, iu, 1)
                    nxt = (iu + 1) % PAIRS
                    stats_of(iu + 1, u, nxt)
                    masked(u, iu, 2)
                if end:
                    dve.wait_ge(PT_mm, upto(ib + 1, v))
                    dve.wait_ge(OT_mm, upto(ib, v))
                    gated(PT, v, (0, 3)).then_inc(PT_done, 1)
                if begin:
                    dve.wait_ge(ab_mm, upto(jf + 1, v))
                    nc.vector.tensor_tensor(tile4(ablog[v]), tile4(bank[v][2][:, 0:2 * GROUP_TILES]),
                                            per_tile(bab_row[:, :]), ALU.add).then_inc(ablog_done, 1)
                    dve.wait_ge(k_mm, upto(jf + 1, v))
                    nc.vector.tensor_tensor(tile4(kb[v]), tile4(bank[v][0][:, :]), per_tile(bk_row[:, :]),
                                            ALU.add).then_inc(kb_done, 1)
                if inverse:
                    masked(u, iu, 3)
                if begin:
                    dve.wait_ge(v_mm, upto(jf + 1, v))
                    dve.wait_ge(WT_mm, upto(jf, v))
                    nc.vector.tensor_tensor(tile4(vtok[v]), tile4(bank[v][1][:, :]), per_tile(bv_row[:, :]),
                                            ALU.add).then_inc(v_done, 1)
                    dve.wait_ge(ksq_done, upto(jf + 1, v))
                    nc.vector.tensor_reduce(kss[v], tile4(ksq[v]), AX.X, ALU.add).then_inc(kss_done, 1)
                    dve.wait_ge(kss_done, upto(jf + 1, v))
                    nc.vector.tensor_scalar(kss[v], kss[v], 1e-24, None, ALU.max).then_inc(kmax_done, 1)
                if end:
                    dve.wait_ge(OT_mm, upto(ib + 1, v))
                    dve.wait_ge(y_mm, upto(ib, v))
                    nc.vector.tensor_tensor(og[v], bank[v][2][:, :], gT[v], ALU.mult).then_inc(og_done, 1)
                if begin:
                    dve.wait_ge(kinv_done, upto(jf + 1, v))
                    dve.wait_ge(OT_mm, upto(jf, v))
                    nc.vector.tensor_tensor(tile4(kn[v]), tile4(kb[v]),
                                            kinv[v].unsqueeze(2).broadcast_to([P, GROUP_TILES, P]),
                                            ALU.mult).then_inc(kn_done, 1)
                if inverse:
                    masked(u, iu, 4)
                if begin:
                    dve.wait_ge(abc_mm, upto(jf + 1, v))
                    for b in range(BATCHES):
                        for c in range(2):
                            last = nc.vector.tensor_tensor_scan(
                                gam[v][:, strip(b, c)], bank[v][0][:, b * SEQ + c * P:(b + 1) * SEQ],
                                eye_zero[:, 0:SEQ - c * P], 0.0, ALU.mult, ALU.add)
                    last.then_inc(gam_done, 1)
                if inverse:
                    normalise(iu + 1, u, nxt)
                    masked(u, iu, 5)
                if begin:
                    dve.wait_ge(gam_done, upto(jf + 1, v))
                    dve.wait_ge(G_mm, upto(jf + 1, v))
                    dve.wait_ge(corr_mm, upto(jf, v))
                    gated(LT, v, (2, 3)).then_inc(LTraw_done, 1)
                if inverse:
                    masked(u, iu, 6)
                if end:
                    dve.wait_ge(y_mm, upto(ib + 1, v))
                    dve.wait_ge(xb_done, upto(ib + 1, v))
                    nc.vector.tensor_tensor(x_all[:, group_cols(ib, v)], bank[v][0][:, :], xb[v],
                                            ALU.add).then_inc(x_done, 1)

            attention_half(None, None, 0, None, 0)
            dve.wait_ge(W_set[0], 1)
            dve.wait_ge(second_x_in, 16)
            attention_half(0, 0, 1, None, 0)
            dve.wait_ge(W_set[1], 1)
            dve.wait_ge(rest_x_in, 16 * (PAIRS - 2))
            with dve.Fori(0, PAIRS - 1) as i:
                attention_half(1, i, 0, i, i + 1)
                attention_half(0, i + 1, 1, i, i + 1)
            all_weights = ff_raw[:, :, :].rearrange("p k h -> p (k h)")
            dve.wait_ge(ff_float, 1)
            nc.vector.tensor_reduce(wmax[:, :], all_weights, AX.X, ALU.max).then_inc(widest_step, 1)
            nc.vector.tensor_reduce(wmin[:, :], all_weights, AX.X, ALU.min).then_inc(widest_step, 1)
            dve.wait_ge(widest_step, 2)
            nc.vector.scalar_tensor_tensor(widest[:, :], wmin[:, :], -1.0, wmax[:, :], ALU.mult, ALU.max).then_inc(widest_step, 1)
            attention_half(1, PAIRS - 1, 0, PAIRS - 1, None)
            dve.wait_ge(widest_mm, 1)
            nc.vector.tensor_reduce(widest_all[:, :], bank[0][0][:, 0:P], AX.X, ALU.max).then_inc(widest_step, 1)
            dve.wait_ge(widest_step, 4)
            nc.vector.tensor_scalar(narrow[:, :], widest_all[:, :], NARROW, None, ALU.is_le).then_inc(narrow_set, 1)
            attention_half(None, None, 1, PAIRS - 1, None)

            def ffn(run):
                phase = 2 * run + 1

                def low_x(i, u):
                    dve.wait_ge(xh_done[u], x_parts(run, i, u))
                    nc.vector.tensor_tensor(xl[u][:, :], xnT[u][:, :], xh[u][:, :], ALU.subtract).then_inc(xl_done[u], 1)

                def add_residual(u, i):
                    dve.wait_ge(down_mm, upto(i + PAIRS * run + 1, u))
                    nc.vector.scalar_tensor_tensor(x_all[:, group_cols(i, u)], bank[u][3][:, :], DEQUANT,
                                                   x_all[:, group_cols(i, u)], ALU.mult, ALU.add).then_inc(x_done, 1)

                def ffn_half(u, i, prev):
                    nxt = (i + 1) % PAIRS
                    k = phase * PAIRS + i + 1
                    n = FF_BLOCKS * (i + PAIRS * run)

                    def hidden(j):
                        dve.wait_ge(silu_done[u], nth(n + j + 1))
                        dve.wait_ge(up_mm[u], nth(n + j + 1))
                        dve.wait_ge(down_mm, upto(i + PAIRS * run, u))
                        nc.vector.scalar_tensor_tensor(hidT[u][:, j, :], bank[u][(2, 0, 2)[j]][:, :], DEQUANT,
                                                       silu_g[u][:, j, :], ALU.mult, ALU.mult).then_inc(hid_done[u], 1)

                    hidden(0)
                    hidden(1)
                    normalise(k, u, nxt)
                    if u == 0:
                        low_x(i, 1)
                    else:
                        low_x(i + 1, 0)
                    hidden(2)
                    if prev is not None:
                        add_residual(1 - u, prev)
                    if u == 0:
                        stats_of(k, 1, nxt, PAIRS - 1)
                    elif not (isinstance(i, int) and i == PAIRS - 1):
                        stats_of(k + 1, 0, (i + 2) % PAIRS, PAIRS - 1)

                stats_of(phase * PAIRS + 1, 0, 1, PAIRS - 1)
                low_x(0, 0)
                ffn_half(0, 0, None)
                with dve.Fori(0, PAIRS - 1) as i:
                    ffn_half(1, i, i)
                    ffn_half(0, i + 1, i)
                ffn_half(1, PAIRS - 1, PAIRS - 1)
                add_residual(1, PAIRS - 1)

            ffn(0)

            dve.wait_ge(later_in, 16 * LATER_DMAS)
            for k in range(INNER_BLOCKS):
                nc.vector.tensor_scalar(wout_sb[:, k, :], wout_raw[:, k, :], normw_col[:, k:k + 1], None,
                                        ALU.mult).then_inc(prep_done, 1)
            dve.wait_ge(aexp_done, 1)
            nc.vector.tensor_scalar(aneg_row[:, :], aexp_row[:, :], -1.0, None, ALU.mult).then_inc(prep_done, 1)

            def add_residual(w, it):
                dve.wait_ge(out_mm, upto(it + 1, w))
                dve.wait_ge(rms_done, upto(it + 1, w))
                for t in range(GROUP_TILES):
                    xs = x_all[:, ds(it * PAIR_COLS + w * GROUP + t * P, P)]
                    last = nc.vector.scalar_tensor_tensor(xs, bank[w][1][:, cols(t)], rms[w][:, t:t + 1], xs,
                                                          ALU.mult, ALU.add)
                last.then_inc(x_done, 1)

            def space_half(u, iu, v, jf, ended):
                end, begin, pair_dt = u is not None, v is not None, v == 0
                taken = [0]

                def step(ins):
                    taken[0] += 1
                    ins.then_inc(dt_step, 1)

                def prior():
                    dve.wait_ge(dt_step, dt_steps(jf, taken[0]))

                def taps(s, *blocks):
                    for q in blocks:
                        if s == 1:
                            dve.wait_ge(conv_init[v], nth(CONV_BLOCKS * jf + q + 1))
                        else:
                            dve.wait_ge(tap_done[v], nth(taps_upto(jf, q, s - 1)))
                        src = bank[v][(0, 3, 1, 0)[q]][:, :].rearrange("p (b t) -> p b t", t=SEQ)[:, :, 0:SEQ - s]
                        acc = xbc[q][v].rearrange("p (b t) -> p b t", t=SEQ)[:, :, s:SEQ]
                        nc.vector.scalar_tensor_tensor(acc, src, convw_sb[:, q, TAPS - 1 - s:TAPS - s], acc,
                                                       ALU.mult, ALU.add).then_inc(tap_done[v], 1)

                def head_decay(h):
                    dve.wait_ge(habc_mm[u], nth(HEADS * iu + h + 1))
                    dve.wait_ge(score_done[u], nth(HEADS * iu + (h - 1 if h >= 2 else 0)))
                    for b in range(BATCHES):
                        for c in range(2):
                            last = nc.vector.tensor_tensor_scan(
                                hgam[h % 2][u][:, strip(b, c)], bank[u][(3, 0)[h % 2]][:, b * SEQ + c * P:(b + 1) * SEQ],
                                eye_zero[:, 0:SEQ - c * P], 0.0, ALU.mult, ALU.add)
                    last.then_inc(hgam_done[u], 1)

                def skip(r):
                    dve.wait_ge(hy_mm[u], nth(HEADS * iu + 2 * r + 2))
                    dve.wait_ge(out_mm, upto(iu, u))
                    dve.wait_ge(ysq_done[u], nth(INNER_BLOCKS * iu))
                    dve.wait_ge(xbc_done[u], nth(CONV_BLOCKS * (iu + 1)))
                    nc.vector.scalar_tensor_tensor(yT[r][u], xbc[r][u], skip_col[:, r:r + 1], bank[u][1 + r][:, :],
                                                   ALU.mult, ALU.add).then_inc(ydt_done[u], 1)

                def times_dt(r):
                    dve.wait_ge(xtok_mm[v], nth(INNER_BLOCKS * jf + r + 1))
                    dve.wait_ge(hy_mm[v], nth(HEADS * jf))
                    dve.wait_ge(dt_step, dt_steps(jf, DT_STEPS))
                    by_head = "p (t h c) -> p t h c"
                    dt = dt_dt[:, v * DT:(v + 1) * DT].rearrange("p (t h) -> p t h", h=HEADS)[:, :, 2 * r:2 * r + 2]
                    nc.vector.tensor_tensor(
                        xt[v].rearrange(by_head, t=GROUP_TILES, h=HEADS)[:, :, 2 * r:2 * r + 2, :],
                        bank[v][(2, 3)[r]][:, :].rearrange(by_head, t=GROUP_TILES, h=2),
                        dt.unsqueeze(3).broadcast_to([P, GROUP_TILES, 2, HEAD_DIM]), ALU.mult).then_inc(xt_done[v], 1)

                if end:
                    head_decay(0)
                if ended is not None:
                    add_residual(*ended)
                if pair_dt:
                    dve.wait_ge(dt_mm, nth(jf + 1))
                    step(nc.vector.tensor_tensor(
                        z_dt[:, :].rearrange("p (t h) -> p t h", h=HEADS),
                        bank[0][2][:, 0:STREAMS * DT].rearrange("p (t h) -> p t h", h=HEADS),
                        dtb_row[:, :].unsqueeze(1).broadcast_to([P, STREAMS * GROUP_TILES, HEADS]), ALU.add))
                    prior()
                    dve.wait_ge(e_done, nth(jf))
                    step(nc.vector.scalar_tensor_tensor(nabs_dt[:, :], z_dt[:, :], -1.0, z_dt[:, :], ALU.mult, ALU.min))
                if end:
                    head_decay(1)
                if pair_dt:
                    dve.wait_ge(e_done, nth(jf + 1))
                    step(nc.vector.tensor_scalar(den_dt[:, :], e_dt[:, :], 2.0, None, ALU.add))
                    prior()
                    step(nc.vector.reciprocal(rec_dt[:, :], den_dt[:, :]))
                    prior()
                    step(nc.vector.tensor_tensor(w_dt[:, :], e_dt[:, :], rec_dt[:, :], ALU.mult))
                    prior()
                    step(nc.vector.tensor_tensor(w2_dt[:, :], w_dt[:, :], w_dt[:, :], ALU.mult))
                    prior()
                    step(nc.vector.tensor_scalar(acc_dt[:, :], w2_dt[:, :], 1.0 / 15, None, ALU.mult))
                if begin:
                    taps(1, 0)
                if end:
                    head_decay(2)
                if pair_dt:
                    for c in SERIES:
                        prior()
                        step(nc.vector.scalar_tensor_tensor(acc_dt[:, :], acc_dt[:, :], c, w2_dt[:, :], ALU.add, ALU.mult))
                    prior()
                    step(nc.vector.scalar_tensor_tensor(acc_dt[:, :], acc_dt[:, :], 1.0, w_dt[:, :], ALU.add, ALU.mult))
                    step(nc.vector.tensor_scalar(relu_dt[:, :], z_dt[:, :], 0.0, None, ALU.max))
                    prior()
                    step(nc.vector.scalar_tensor_tensor(dt_dt[:, :], acc_dt[:, :], 2.0, relu_dt[:, :], ALU.mult, ALU.add))
                    prior()
                    step(nc.vector.tensor_tensor(
                        dA_dt[:, :].rearrange("p (t h) -> p t h", h=HEADS), dt_dt[:, :].rearrange("p (t h) -> p t h", h=HEADS),
                        aneg_row[:, :].unsqueeze(1).broadcast_to([P, STREAMS * GROUP_TILES, HEADS]), ALU.mult))
                    assert taken[0] == DT_STEPS, taken[0]
                if begin:
                    taps(1, 1)
                if end:
                    head_decay(3)
                if pair_dt:
                    dve.wait_ge(dAT_mm, nth(jf + 1))
                    step(nc.vector.tensor_tensor_scan(csum[:, :], keep[0:ROWS, :], bank[0][2][0:ROWS, 0:P], 0.0,
                                                      ALU.mult, ALU.add))
                    prior()
                    dve.wait_ge(back_mm, nth(jf))
                    of_chunk = csum[:, :].rearrange("r (c t) -> r c t", t=CHUNK)
                    step_of_chunk = dstep[0:ROWS, :].rearrange("r (c t) -> r c t", t=CHUNK)
                    step(nc.vector.tensor_tensor(step_of_chunk[:, :, 1:CHUNK], of_chunk[:, :, 1:CHUNK],
                                                 of_chunk[:, :, 0:CHUNK - 1], ALU.subtract))
                    step(nc.vector.tensor_copy(step_of_chunk[:, :, 0:1], of_chunk[:, :, 0:1]))
                    assert taken[0] == DT_STEPS + CS_STEPS, taken[0]
                if begin:
                    taps(2, 0, 1)
                if end:
                    skip(0)
                if begin:
                    taps(3, 0, 1)
                if end:
                    skip(1)
                if begin:
                    nxt = (jf + 1) % PAIRS
                    stats_of(2 * PAIRS + jf + 1, v, nxt)
                    taps(1, 2, 3)
                    taps(2, 2, 3)
                    times_dt(0)
                    times_dt(1)
                    normalise(2 * PAIRS + jf + 1, v, nxt)
                    taps(3, 2)
                if end:
                    dve.wait_ge(ms_mm, upto(iu + 1, u))
                    dve.wait_ge(rms_done, upto(iu, u))
                    nc.vector.tensor_scalar(ms[u], bank[u][2][:, 0:GROUP_TILES], 1.0 / INNER, RMS_EPS,
                                            ALU.mult, ALU.add).then_inc(ms_done, 1)
                if begin:
                    taps(3, 3)

            space_half(None, None, 0, 0, None)
            space_half(0, 0, 1, 0, None)
            with dve.Fori(0, PAIRS - 1) as i:
                space_half(1, i, 0, i + 1, (0, i))
                space_half(0, i + 1, 1, i + 1, (1, i))
            space_half(1, PAIRS - 1, None, None, (0, PAIRS - 1))
            add_residual(1, PAIRS - 1)
            ffn(1)

        @block.tensor
        def _(pe):
            mm = nc.tensor.matmul

            def transposes(k, u, dst):
                pe.wait_ge(xn_done, upto(k + 1, u))
                for t in range(GROUP_TILES):
                    last = nc.tensor.transpose(bank[u][dst][:, cols(t)], xn[u][:, cols(t)], ident)
                last.then_inc(tr_done, 1)

            for s in paced:
                pe.sem_inc(s, STREAMS)
            for s in (*per_pair, *(s for pair in per_stream for s in pair)):
                pe.sem_inc(s, 1)
            pe.wait_ge(tables_in, 16)
            for u in U:
                transposes(0, u, 3)
            pe.wait_ge(attn_in, 16 * ATTN_DMAS)

            def Z_of(u, i, level):
                if level == 0:
                    pe.wait_ge(LT_done, upto(i + 1, u))
                    pe.wait_ge(g_done, upto(i + 1, u))
                elif level == 1:
                    pe.wait_ge(W_done[u], nth(LEVELS * i + 1))
                else:
                    pe.wait_ge(T_done[u], nth((LEVELS - 2) * i + level - 1))
                for t in range(GROUP_TILES):
                    if level == 0:
                        last = nc.tensor.transpose(bank[u][1][:, cols(t)], LT[u][:, diag(t)], ident)
                    else:
                        last = mm(packed(bank[u][1][:, half_cols(t)], level), LT[u][:, diag(t)],
                                  halves(Tm[u][:, cols(t)], level, 0), start=True, stop=True)
                last.then_inc(Z_mm[u], 1)

            def T_of(u, i, level):
                pe.wait_ge(W_done[u], nth(LEVELS * i + level + 1))
                pe.wait_ge(R_done[u], nth(LEVELS * i + level))
                for t in range(GROUP_TILES):
                    last = mm(packed(bank[u][2][:, half_cols(t)], level), Rm[u][:, cols(t)],
                              halves(Wlev[level][u][:, cols(t)], level, 0), start=True, stop=True)
                last.then_inc(T_mm[u], 1)

            def R_of(u, i, level):
                if level == 0:
                    pe.wait_ge(W_done[u], nth(LEVELS * i + 1))
                    pe.wait_ge(x_done, upto(i, u))
                elif level < LEVELS - 1:
                    pe.wait_ge(T_done[u], nth((LEVELS - 2) * i + level))
                else:
                    pe.wait_ge(W_done[u], nth(LEVELS * (i + 1)))
                    pe.wait_ge(R_done[u], nth(LEVELS * i + level))
                for t in range(GROUP_TILES):
                    if level < LEVELS - 1:
                        last = nc.tensor.transpose(bank[u][0][:, cols(t)], Tm[u][:, cols(t)], ident)
                    else:
                        last = mm(packed(bank[u][0][:, half_cols(t)], level), Wlev[level][u][:, cols(t)],
                                  halves(Rm[u][:, cols(t)], level, 1), start=True, stop=True)
                last.then_inc(R_mm[u], 1)

            def attention_half(u, iu, v, ib, jf):
                inverse, end, begin = iu is not None, ib is not None, jf is not None
                if inverse:
                    Z_of(u, iu, 0)
                if end:
                    pe.wait_ge(R_done[v], nth(LEVELS * (ib + 1)))
                    for b in range(BATCHES):
                        last = mm(bank[v][3][:, cols(b)], Rm[v][:, cols(2 * b)], vtok[v][:, cols(2 * b)], start=True, stop=True)
                    last.then_inc(w0_mm, 1)
                if inverse:
                    R_of(u, iu, 0)
                if end:
                    pe.wait_ge(w0_done, upto(ib + 1, v))
                    for b in range(BATCHES):
                        last = mm(bank[v][2][:, cols(b)], LT[v][:, b * TRI + P:b * TRI + 2 * P], w0tok[v][:, cols(b)],
                                  start=True, stop=True)
                    last.then_inc(corr_mm, 1)
                if inverse:
                    Z_of(u, iu, 1)
                if end:
                    pe.wait_ge(v1_done, upto(ib + 1, v))
                    for t in range(GROUP_TILES):
                        last = mm(bank[v][1][:, cols(t)], vtok[v][:, cols(t)], Rm[v][:, cols(t)], start=True, stop=True)
                    last.then_inc(WT_mm, 1)
                if inverse:
                    T_of(u, iu, 1)
                if end:
                    transposes(ib + 1, v, 2)
                if inverse:
                    Z_of(u, iu, 2)
                    R_of(u, iu, 1)
                if end:
                    pe.wait_ge(WT_done, upto(ib + 1, v))
                    for b in range(BATCHES):
                        for c in range(2):
                            last = mm(bank[v][(0, 3)[b]][:, c * SEQ:c * SEQ + SEQ - c * P], WT[v][:, cols(2 * b + c)],
                                      qT[v][:, b * SEQ + c * P:(b + 1) * SEQ], start=True, stop=True)
                    last.then_inc(PT_mm, 1)
                if inverse:
                    T_of(u, iu, 2)
                if begin:
                    pe.wait_ge(xnT_done, upto(jf + 1, v))
                    for t in range(GROUP_TILES):
                        last = mm(bank[v][2][:, 2 * t:2 * t + 2], xnT[v][:, cols(t)], wab_sb[:, :], start=True, stop=True)
                    last.then_inc(ab_mm, 1)
                    pe.wait_ge(PT_done, upto(jf, v))
                    for t in range(GROUP_TILES):
                        last = mm(bank[v][0][:, cols(t)], xnT[v][:, cols(t)], wk_sb[:, :], start=True, stop=True)
                    last.then_inc(k_mm, 1)
                if inverse:
                    Z_of(u, iu, 3)
                    R_of(u, iu, 2)
                if begin:
                    for t in range(GROUP_TILES):
                        last = mm(bank[v][1][:, cols(t)], xnT[v][:, cols(t)], wv_sb[:, :], start=True, stop=True)
                    last.then_inc(v_mm, 1)
                if end:
                    pe.wait_ge(PT_done, upto(ib + 1, v))
                    if begin:
                        pe.wait_ge(ablog_done, upto(jf + 1, v))
                    else:
                        pe.wait_ge(xnT_done, upto(ib + 2, v))
                    for b in range(BATCHES):
                        mm(bank[v][2][:, b * SEQ:(b + 1) * SEQ], kn[v][:, cols(2 * b)], PT[v][:, strip(b, 0)],
                           start=True, stop=False)
                        last = mm(bank[v][2][:, b * SEQ + P:(b + 1) * SEQ], kn[v][:, cols(2 * b + 1)], PT[v][:, strip(b, 1)],
                                  start=False, stop=True)
                    last.then_inc(OT_mm, 1)
                if inverse:
                    T_of(u, iu, 3)
                if begin:
                    mm(bank[v][3][:, :], wq_sb[:, :], xnT[v][:, :], start=True, stop=True).then_inc(q_mm, 1)
                    pe.wait_ge(ab_done, upto(jf + 1, v))
                    pe.wait_ge(kb_done, upto(jf + 1, v))
                    for t in range(GROUP_TILES):
                        last = nc.tensor.transpose(bank[v][0][:, cols(t)],
                                                   ab[v][:, 2 * t:2 * t + 1].broadcast_to([P, P]), ident)
                    last.then_inc(abc_mm, 1)
                if inverse:
                    Z_of(u, iu, 4)
                    R_of(u, iu, 3)
                if begin:
                    pe.wait_ge(kn_done, upto(jf + 1, v))
                    pe.wait_ge(v_done, upto(jf + 1, v))
                    for t in range(GROUP_TILES):
                        last = nc.tensor.transpose(bank[v][1][:, cols(t)], kn[v][:, cols(t)], ident)
                    last.then_inc(kT_mm, 1)
                if inverse:
                    T_of(u, iu, 4)
                if begin:
                    pe.wait_ge(kT_done, upto(jf + 1, v))
                    pe.wait_ge(q_done, upto(jf + 1, v))
                    pe.wait_ge(og_done, upto(jf, v))
                    for b in range(BATCHES):
                        for c in range(2):
                            last = mm(bank[v][2 + b][:, c * SEQ:c * SEQ + SEQ - c * P], kT[v][:, cols(2 * b + c)],
                                      kT[v][:, b * SEQ + c * P:(b + 1) * SEQ], start=True, stop=True)
                    last.then_inc(G_mm, 1)
                if inverse:
                    Z_of(u, iu, 5)
                    R_of(u, iu, 4)
                if begin:
                    mm(bank[v][1][:, :], wg_sb[:, :], xnT[v][:, :], start=True, stop=True).then_inc(g_mm, 1)
                if inverse:
                    T_of(u, iu, 5)
                if inverse:
                    Z_of(u, iu, 6)
                    R_of(u, iu, 5)
                if end:
                    pe.wait_ge(og_done, upto(ib + 1, v))
                    if begin:
                        pe.wait_ge(gam_done, upto(jf + 1, v))
                    for t in range(GROUP_TILES):
                        last = mm(bank[v][0][:, cols(t)], og[v][:, cols(t)], wo_sb[:, :], start=True, stop=True)
                    last.then_inc(y_mm, 1)
                if inverse:
                    R_of(u, iu, 6)

            attention_half(None, None, 0, None, 0)
            pe.wait_ge(W_set[0], 1)
            attention_half(0, 0, 1, None, 0)
            pe.wait_ge(W_set[1], 1)
            with pe.Fori(0, PAIRS - 1) as i:
                attention_half(1, i, 0, i, i + 1)
                attention_half(0, i + 1, 1, i, i + 1)
            attention_half(1, PAIRS - 1, 0, PAIRS - 1, None)
            pe.wait_ge(ff_float, 1)
            for n in range(3):
                for k in range(FF_BLOCKS):
                    last = nc.tensor.transpose(bank[0][1 + n][:, cols(k)], ff_raw[:, n, cols(k)], ident)
                last.then_inc(ffT_mm, 1)
            pe.wait_ge(widest_step, 3)
            pe.wait_ge(x_done, upto(PAIRS, 0))
            nc.tensor.transpose(bank[0][0][:, 0:P], widest[:, 0:1].broadcast_to([P, P]), ident).then_inc(widest_mm, 1)
            attention_half(None, None, 1, PAIRS - 1, None)

            def ffn_of(run, exact16):
                phase = 2 * run + 1

                def gate_up(u, i):
                    it = phase * PAIRS + i
                    n = FF_BLOCKS * (i + PAIRS * run)

                    def project(to, wide, narrow16, j):
                        if exact16:
                            mm(to, narrow16[:, cols(j)], xh[u][:, :], start=True, stop=False)
                            return mm(to, narrow16[:, cols(j)], xl[u][:, :], start=False, stop=True)
                        return mm(to, wide[:, cols(j)], xnT[u][:, :], start=True, stop=True)

                    pe.wait_ge(xl_done[u], x_parts(run, i, u))
                    for j in range(FF_BLOCKS):
                        if j == 0:
                            pe.wait_ge(silu_done[u], nth(n))
                            pe.wait_ge(hid_done[u], nth(n))
                        elif j == 1:
                            pe.wait_ge(x_done, upto(it, u))
                        else:
                            pe.wait_ge(silu_done[u], nth(n + 1))
                            pe.wait_ge(hid_done[u], nth(n + 1))
                        project(bank[u][(1, 3, 1)[j]][:, :], gateT, gate16, j).then_inc(gate_mm[u], 1)
                        project(bank[u][(2, 0, 2)[j]][:, :], upT, up16, j).then_inc(up_mm[u], 1)

                def down(u, i):
                    pe.wait_ge(hl_done[u], nth(FF_BLOCKS * (i + PAIRS * run + 1)))
                    for t in range(GROUP_TILES):
                        to = bank[u][3][:, cols(t)]
                        for j in range(FF_BLOCKS):
                            if exact16:
                                mm(to, hh[u][:, j, cols(t)], down16[:, j, :], start=(j == 0), stop=False)
                                last = mm(to, hl[u][:, j, cols(t)], down16[:, j, :], start=False, stop=(j == FF_BLOCKS - 1))
                            else:
                                last = mm(to, hidT[u][:, j, cols(t)], downT[:, j, :], start=(j == 0), stop=(j == FF_BLOCKS - 1))
                    last.then_inc(down_mm, 1)

                def ffn_half(u, i, prev):
                    gate_up(u, i)
                    if prev is not None:
                        down(1 - u, prev)
                    pe.wait_ge(hid_done[u], nth(FF_BLOCKS * (i + PAIRS * run) + 2))
                    transposes(phase * PAIRS + i + 1, u, 0)

                ffn_half(0, 0, None)
                with pe.Fori(0, PAIRS - 1) as i:
                    ffn_half(1, i, i)
                    ffn_half(0, i + 1, i)
                ffn_half(1, PAIRS - 1, PAIRS - 1)
                down(1, PAIRS - 1)

            def ffn(run):
                for u in U:
                    pe.wait_ge(x_done, upto((2 * run + 1) * PAIRS, u))
                fits = pe.value_load(narrow[0:1, 0:1], min_val=0, max_val=1)
                with pe.If(fits > 0):
                    ffn_of(run, True)
                with pe.Else():
                    ffn_of(run, False)

            pe.wait_ge(narrow_set, 1)
            pe.wait_ge(ffT_done, 6)
            pe.wait_ge(consts_set, 4)
            pe.wait_ge(later_in, 16 * LATER_DMAS)
            ffn(0)

            for u in U:
                pe.wait_ge(x_done, upto(2 * PAIRS, u))
            pe.wait_ge(prep_done, INNER_BLOCKS + 1)

            def space_half(u, iu, v, jf):
                end, begin, pair_dt = u is not None, v is not None, v == 0

                def conv(r):
                    mm(bank[v][(0, 3, 1, 0)[r]][:, :], win_sb[:, INNER + r * P:INNER + (r + 1) * P], xnT[v][:, :],
                       start=True, stop=True).then_inc(conv_mm[v], 1)

                def gate(r):
                    pe.wait_ge(tap_done[v], nth(taps_upto(jf, 1 + r, TAPS - 1)))
                    mm(bank[v][(3, 1)[r]][:, :], win_sb[:, cols(r)], xnT[v][:, :], start=True, stop=True).then_inc(z_mm[v], 1)

                def token_major(r):
                    pe.wait_ge(xbc_done[v], nth(CONV_BLOCKS * jf + r + 1))
                    if r == 1:
                        pe.wait_ge(sz_done[v], nth(INNER_BLOCKS * jf + 1))
                    elif v == 0:
                        pe.wait_ge(decay_done, nth(jf + 1))
                    else:
                        pe.wait_ge(ms_done, upto(jf, v))
                    for t in range(GROUP_TILES):
                        last = nc.tensor.transpose(bank[v][(2, 3)[r]][:, cols(t)], xbc[r][v][:, cols(t)], ident)
                    last.then_inc(xtok_mm[v], 1)

                def spread_decay(w, it, h):
                    if w == 0:
                        pe.wait_ge(decay_done, nth(it + 1))
                    else:
                        pe.wait_ge(decay1_done, nth(it + 1))
                    if h == 0:
                        pe.wait_ge(xt_done[w], nth(INNER_BLOCKS * (it + 1)))
                    elif h == 1:
                        pe.wait_ge(xnT_done, upto(2 * PAIRS + it + 2, w))
                    else:
                        pe.wait_ge(hgam_done[w], nth(HEADS * it + h - 1))
                    of_stream = (decay, decay1)[w]
                    for t in range(GROUP_TILES):
                        at = t * HEADS + h
                        last = nc.tensor.transpose(bank[w][(3, 0)[h % 2]][:, cols(t)],
                                                   of_stream[:, at:at + 1].broadcast_to([P, P]), ident)
                    last.then_inc(habc_mm[w], 1)

                def head_output(h):
                    pe.wait_ge(score_done[u], nth(HEADS * iu + h + 1))
                    pe.wait_ge(xt_done[u], nth(INNER_BLOCKS * (iu + 1)))
                    pe.wait_ge(cb_done[u], nth(BATCHES * (iu + 1)))
                    half = (h % 2) * HEAD_DIM
                    xh = xt[u].rearrange("p (t c) -> p t c", t=GROUP_TILES)[:, :, h * HEAD_DIM:(h + 1) * HEAD_DIM]
                    for b in range(BATCHES):
                        yh = bank[u][1 + h // 2][half:half + HEAD_DIM, :]
                        mm(yh[:, b * SEQ:(b + 1) * SEQ], xh[:, 2 * b, :], score[h % 2][u][:, strip(b, 0)],
                           start=True, stop=False)
                        last = mm(yh[:, b * SEQ + P:(b + 1) * SEQ], xh[:, 2 * b + 1, :],
                                  score[h % 2][u][:, strip(b, 1)], start=False, stop=True)
                    last.then_inc(hy_mm[u], 1)

                if pair_dt:
                    pe.wait_ge(ms_done, upto(jf, 0))
                    for w in U:
                        pe.wait_ge(xnT_done, upto(2 * PAIRS + jf + 1, w))
                        for t in range(GROUP_TILES):
                            at = w * DT + t * HEADS
                            last = mm(bank[0][2][:, at:at + HEADS], xnT[w][:, cols(t)], win_sb[:, PROJ - HEADS:PROJ],
                                      start=True, stop=True)
                    last.then_inc(dt_mm, 1)
                if end:
                    spread_decay(u, iu, 1)
                if begin:
                    pe.wait_ge(xnT_done, upto(2 * PAIRS + jf + 1, v))
                    pe.wait_ge(hgam_done[v], nth(HEADS * jf))
                    conv(0)
                    conv(1)
                if end:
                    spread_decay(u, iu, 2)
                    head_output(0)
                if begin:
                    pe.wait_ge(x_done, upto(2 * PAIRS + jf, v))
                    conv(2)
                if end:
                    spread_decay(u, iu, 3)
                    head_output(1)
                    head_output(2)
                if pair_dt:
                    pe.wait_ge(dt_step, dt_steps(jf, DT_STEPS))
                    nc.tensor.transpose(bank[0][2][0:ROWS, 0:P], dA_dt[:, :], ident).then_inc(dAT_mm, 1)
                    pe.wait_ge(dt_step, dt_steps(jf, DT_STEPS + CS_STEPS))
                    nc.tensor.transpose(bank[0][2][:, 0:P], dstep[:, :], ident).then_inc(back_mm, 1)
                if end:
                    head_output(3)
                if begin:
                    pe.wait_ge(tap_done[v], nth(taps_upto(jf, 0, TAPS - 1)))
                    conv(3)
                    gate(0)
                    token_major(0)
                    token_major(1)
                if end:
                    pe.wait_ge(ysq_done[u], nth(INNER_BLOCKS * (iu + 1)))
                    for t in range(GROUP_TILES):
                        for r in range(INNER_BLOCKS):
                            last = mm(bank[u][2][:, t:t + 1], ysq[r][u][:, cols(t)], ones_col[:, :],
                                      start=(r == 0), stop=(r == INNER_BLOCKS - 1))
                    last.then_inc(ms_mm, 1)
                    for t in range(GROUP_TILES):
                        for r in range(INNER_BLOCKS):
                            last = mm(bank[u][1][:, cols(t)], yT[r][u][:, cols(t)], wout_sb[:, r, :],
                                      start=(r == 0), stop=(r == INNER_BLOCKS - 1))
                    last.then_inc(out_mm, 1)
                if begin:
                    gate(1)
                    spread_decay(v, jf, 0)
                    pe.wait_ge(tap_done[v], nth(taps_upto(jf, 3, TAPS - 1)))
                    transposes(2 * PAIRS + jf + 1, v, 0)
                    for b in range(BATCHES):
                        pe.wait_ge(xbc_done[v], nth(CONV_BLOCKS * (jf + 1)))
                        if b == 0:
                            pe.wait_ge(sz_done[v], nth(INNER_BLOCKS * (jf + 1)))
                        else:
                            pe.wait_ge(xt_done[v], nth(INNER_BLOCKS * jf + 1))
                        for c in range(2):
                            last = mm(bank[v][1 + b][:, c * SEQ:c * SEQ + SEQ - c * P], xbc[2][v][:, cols(2 * b + c)],
                                      xbc[3][v][:, b * SEQ + c * P:(b + 1) * SEQ], start=True, stop=True)
                        last.then_inc(cb_mm[v], 1)

            space_half(None, None, 0, 0)
            space_half(0, 0, 1, 0)
            with pe.Fori(0, PAIRS - 1) as i:
                space_half(1, i, 0, i + 1)
                space_half(0, i + 1, 1, i + 1)
            space_half(1, PAIRS - 1, None, None)
            ffn(1)


_INS = ['L0_attn_a_x', 'L0_attn_a_Wq', 'L0_attn_a_bq', 'L0_attn_a_Wk', 'L0_attn_a_bk', 'L0_attn_a_Wv', 'L0_attn_a_bv',
        'L0_attn_a_Wa', 'L0_attn_a_ba', 'L0_attn_a_Wb', 'L0_attn_a_bb', 'L0_attn_a_Wg', 'L0_attn_a_bg', 'L0_attn_a_Wo',
        'L0_attn_a_bo', 'L0_attn_b_W_in', 'L0_attn_b_conv_w', 'L0_attn_b_conv_b', 'L0_attn_b_dt_bias', 'L0_attn_b_A_log',
        'L0_attn_b_D', 'L0_attn_b_norm_w', 'L0_attn_b_W_out', 'L0_ffn_w_gate', 'L0_ffn_w_up', 'L0_ffn_w_down']


def kernel(**inputs):
    import numpy as _np
    import concourse.bacc as _bacc
    from concourse import mybir as _mybir
    from concourse.bass_utils import run_bass_kernel_spmd as _run

    nc = _bacc.Bacc("TRN2", target_bir_lowering=False, num_devices=1)
    arrays, args = {}, []
    for name in _INS:
        a = _np.ascontiguousarray(inputs[name])
        arrays[f"in_{name}"] = a
        args.append(nc.dram_tensor(f"in_{name}", a.shape, _mybir.dt.from_np(a.dtype), kind="ExternalInput").ap())
    table = constants()
    arrays["in_tables"] = table
    args.append(nc.dram_tensor("in_tables", table.shape, _mybir.dt.float32, kind="ExternalInput").ap())
    out = nc.dram_tensor("out", (BATCH, SEQ, DIM), _mybir.dt.float32, kind="ExternalOutput").ap()
    build(nc, *args, out)
    r = _run(nc, [arrays], core_ids=[0])
    return r.results[0]["out"]
```
